# Optimizing a Trainium2 kernel written in Bass

```python
import numpy as np
import jax
import jax.numpy as jnp

def _softmax(x, axis=-1):
    return jax.nn.softmax(x, axis=axis)

def _gelu(x):
    return jax.nn.gelu(x, approximate=True)

def _silu(x):
    return jax.nn.silu(x)

def _sigmoid(x):
    return jax.nn.sigmoid(x)

def _layernorm(x, axis=-1, eps=1e-05):
    m = jnp.mean(x, axis=axis, keepdims=True)
    v = jnp.var(x, axis=axis, keepdims=True)
    return (x - m) / jnp.sqrt(v + eps)

def _scatter_add(tgt, idx, src, axis=0):
    return tgt.at[idx].add(src)

def _segment_sum(src, seg, n):
    return jax.ops.segment_sum(src, seg, n)
kernel_name = 'mk_xattn_ffn_d4_seqx_r4_31608e'

def setup_inputs(seed: int=0):
    np.random.seed(seed)
    _w = jnp.asarray

    def _rec_inputs():
        import jax
        import jax.numpy as jnp
        _rk = jax.random.key(seed)
        x = 0.5 + 0.2887 * jax.random.normal(jax.random.fold_in(_rk, 1), (4, 512, 512), jnp.float32)
        _lenS = 512 - jax.random.randint(jax.random.fold_in(_rk, 7), (4,), 0, max(1, 512 // 4) + 1, jnp.int32)
        _lenS2 = 512 - jax.random.randint(jax.random.fold_in(_rk, 8), (4,), 0, max(1, 512 // 4) + 1, jnp.int32)
        _ctx_512P = jax.random.normal(jax.random.fold_in(_rk, 11), (4, 16, 128), jnp.float32)
        _ctx_512c = jax.random.dirichlet(jax.random.fold_in(_rk, 511), 0.3 * jnp.ones((16,), jnp.float32), (4, 512))
        _ctx_512t = jnp.einsum('bsk,bkd->bsd', _ctx_512c, _ctx_512P)
        _ctx_512t = _ctx_512t * jax.lax.rsqrt(jnp.mean(jnp.square(_ctx_512t)) + 1e-12) * 0.953939
        ctx_512 = 7.22013e-05 + 1.00017 * (_ctx_512t + 0.3 * jax.random.normal(jax.random.fold_in(_rk, 611), (4, 512, 128), jnp.float32))
        _validS = jnp.arange(512)[None, :] < _lenS[:, None]
        _validS2 = jnp.arange(512)[None, :] < _lenS2[:, None]
        _causal = jnp.tril(jnp.ones((512, 512), dtype=bool))
        mask_SxS2_bk1 = jnp.broadcast_to(_validS2[0:1, :], (512, 512))
        mask_BxS2_bf0 = jnp.logical_not(jnp.ones((4, 512), dtype=bool))
        return (x, ctx_512, mask_SxS2_bk1, mask_BxS2_bf0)
    x, ctx_512, mask_SxS2_bk1, mask_BxS2_bf0 = _rec_inputs()

    def _L0_xattn_setup():
        import jax, jax.numpy as jnp
        import numpy as np
        P_ASEM = 0.6
        key = jax.random.key(seed)
        k1, k2, k3 = jax.random.split(key, 3)
        B, N, D = (8, 512, 128)
        x = jax.random.normal(k1, (B, N, D), dtype=jnp.float32)
        adj = jax.random.uniform(k2, (B, N, N), dtype=jnp.float32)
        bound = 1.0 / np.sqrt(2 * D)
        W = jax.random.uniform(k3, (1, 2 * D), dtype=jnp.float32, minval=-bound, maxval=bound)
        b = jnp.zeros((1,), dtype=jnp.float32)
        return {'x': x, 'adj': adj, 'W': W, 'b': b}
    _L0_xattn_all = _L0_xattn_setup()
    _L0_xattn_in = {k: v for k, v in _L0_xattn_all.items() if k in ('W', 'b')}
    del _L0_xattn_all

    def _L0_ffn_setup():
        import jax, jax.numpy as jnp
        import numpy as np
        HID = 512
        N_EXP = 32
        F_EXP = 192
        TOP_K = 6
        F_SH = 384
        B, S = (1, 256)
        key = jax.random.key(seed)
        ks = jax.random.split(key, 8)
        s = 0.02
        return {'hidden_states': jax.random.normal(ks[0], (B, S, HID), dtype=jnp.float32), 'gate_w': jax.random.normal(ks[1], (HID, N_EXP), dtype=jnp.float32) * s, 'wg': jax.random.normal(ks[2], (N_EXP, HID, F_EXP), dtype=jnp.float32) * s, 'wu': jax.random.normal(ks[3], (N_EXP, HID, F_EXP), dtype=jnp.float32) * s, 'wd': jax.random.normal(ks[4], (N_EXP, F_EXP, HID), dtype=jnp.float32) * s, 'sg': jax.random.normal(ks[5], (HID, F_SH), dtype=jnp.float32) * s, 'su': jax.random.normal(ks[6], (HID, F_SH), dtype=jnp.float32) * s, 'sd': jax.random.normal(ks[7], (F_SH, HID), dtype=jnp.float32) * s}
    _L0_ffn_all = _L0_ffn_setup()
    _L0_ffn_in = {k: v for k, v in _L0_ffn_all.items() if k in ('gate_w', 'wg', 'wu', 'wd', 'sg', 'su', 'sd')}
    del _L0_ffn_all

    def _L1_xattn_setup():
        import jax, jax.numpy as jnp
        import numpy as np
        B, N, D = (16, 512, 128)
        H = 4
        TOP_K_RATIO = 0.3
        key = jax.random.key(seed)
        k1, k2, k3, k4 = jax.random.split(key, 4)
        h = jax.random.normal(k1, (B, N, D), dtype=jnp.float32)
        adj_raw = jax.random.uniform(k2, (B, N, N), dtype=jnp.float32)
        lim = 1.0 / np.sqrt(D)
        Wq = jax.random.uniform(k3, (D, D), minval=-lim, maxval=lim, dtype=jnp.float32)
        Wk = jax.random.uniform(k4, (D, D), minval=-lim, maxval=lim, dtype=jnp.float32)
        gamma_raw = jnp.float32(-0.85)
        return {'h': h, 'adj_raw': adj_raw, 'Wq': Wq, 'Wk': Wk, 'gamma_raw': gamma_raw}
    _L1_xattn_all = _L1_xattn_setup()
    _L1_xattn_in = {k: v for k, v in _L1_xattn_all.items() if k in ('Wq', 'Wk', 'gamma_raw')}
    del _L1_xattn_all

    def _L1_ffn_setup():
        import math
        import jax, jax.numpy as jnp
        import numpy as np
        DIM = 512
        RANK = 8
        B, T = (4, 1024)

        def _orthogonal(key, n):
            a = jax.random.normal(key, (n, n), dtype=jnp.float32)
            q, r = jnp.linalg.qr(a)
            q = q * jnp.sign(jnp.diagonal(r))[None, :]
            return q
        key = jax.random.key(seed)
        kx, kf = jax.random.split(key)
        x = jax.random.normal(kx, (B, T, DIM), dtype=jnp.float32)
        fkeys = jax.random.split(kf, RANK)
        factors = jnp.stack([_orthogonal(fkeys[r], DIM) * (r + 1) ** (-0.5) for r in range(RANK)])
        bias = jnp.zeros((DIM,), dtype=jnp.float32)
        return {'x': x, 'factors': factors, 'bias': bias}
    _L1_ffn_all = _L1_ffn_setup()
    _L1_ffn_in = {k: v for k, v in _L1_ffn_all.items() if k in ('factors', 'bias')}
    del _L1_ffn_all

    def _L2_xattn_setup():
        import jax, jax.numpy as jnp
        import numpy as np
        B, S, H = (8, 512, 128)
        key = jax.random.key(seed)
        kq, kk, kqc, kwq, kwk = jax.random.split(key, 5)
        q = jax.random.normal(kq, (B, S, H), dtype=jnp.float32)
        k = jax.random.normal(kk, (B, S, H), dtype=jnp.float32)
        qc_score = jax.random.uniform(kqc, (B, S, S), dtype=jnp.float32)
        attn_mask = jnp.triu(jnp.ones((S, S), dtype=bool), k=1)
        key_padding_mask = jnp.zeros((B, S), dtype=bool)
        scale = 1.0 / np.sqrt(H)
        Wq = jax.random.normal(kwq, (H, H), dtype=jnp.float32) * scale
        Wk = jax.random.normal(kwk, (H, H), dtype=jnp.float32) * scale
        bq = jnp.zeros((H,), dtype=jnp.float32)
        bk = jnp.zeros((H,), dtype=jnp.float32)
        return {'q': q, 'k': k, 'attn_mask': attn_mask, 'key_padding_mask': key_padding_mask, 'qc_score': qc_score, 'Wq': Wq, 'bq': bq, 'Wk': Wk, 'bk': bk}
    _L2_xattn_all = _L2_xattn_setup()
    _L2_xattn_in = {k: v for k, v in _L2_xattn_all.items() if k in ('Wq', 'bq', 'Wk', 'bk')}
    del _L2_xattn_all

    def _L2_ffn_setup():
        import jax, jax.numpy as jnp
        import numpy as np
        EPS = 1e-06
        K_STEPS = 4
        USE_GATING = True

        def layer_norm(x, gamma, beta):
            mu = jnp.mean(x, axis=-1, keepdims=True)
            var = jnp.mean(jnp.square(x - mu), axis=-1, keepdims=True)
            return (x - mu) * jax.lax.rsqrt(var + EPS) * gamma + beta
        key = jax.random.key(seed)
        B, L, D, H = (4, 1024, 512, 2048)
        ks = jax.random.split(key, 16)
        s = 0.02
        return {'x': jax.random.normal(ks[0], (B, L, D), dtype=jnp.float32), 'in_gamma': jnp.ones((D,), jnp.float32), 'in_beta': jnp.zeros((D,), jnp.float32), 'agg_w': jax.random.normal(ks[1], (D, D), jnp.float32) * s, 'agg_b': jnp.zeros((D,), jnp.float32), 'pn_gamma': jnp.ones((D,), jnp.float32), 'pn_beta': jnp.zeros((D,), jnp.float32), 'd1_w': jax.random.normal(ks[2], (D, H), jnp.float32) * s, 'd1_b': jnp.zeros((H,), jnp.float32), 'd2_w': jax.random.normal(ks[3], (H, D), jnp.float32) * s, 'd2_b': jnp.zeros((D,), jnp.float32), 'bc_w': jax.random.normal(ks[4], (D, D), jnp.float32) * s, 'bc_b': jnp.zeros((D,), jnp.float32), 'gate_w': jax.random.normal(ks[5], (D, D), jnp.float32) * s, 'gate_b': jnp.zeros((D,), jnp.float32), 'out_gamma': jnp.ones((D,), jnp.float32), 'out_beta': jnp.zeros((D,), jnp.float32)}
    _L2_ffn_all = _L2_ffn_setup()
    _L2_ffn_in = {k: v for k, v in _L2_ffn_all.items() if k in ('in_gamma', 'in_beta', 'agg_w', 'agg_b', 'pn_gamma', 'pn_beta', 'd1_w', 'd1_b', 'd2_w', 'd2_b', 'bc_w', 'bc_b', 'gate_w', 'gate_b', 'out_gamma', 'out_beta')}
    del _L2_ffn_all

    def _L3_xattn_setup():
        import jax, jax.numpy as jnp
        import numpy as np
        B, S, E = (2, 512, 512)
        QH, KVH = (32, 8)
        D = E // QH
        G = QH // KVH
        DROPOUT = 1.0
        key = jax.random.key(seed)
        k1, k2, k3 = jax.random.split(key, 3)
        q = jax.random.normal(k1, (B, S, E), dtype=jnp.float32)
        k = jax.random.normal(k2, (B, S, E // G), dtype=jnp.float32)
        v = jax.random.normal(k3, (B, S, E // G), dtype=jnp.float32)
        return {'q': q, 'k': k, 'v': v}
    _L3_xattn_all = _L3_xattn_setup()
    _L3_xattn_in = {k: v for k, v in _L3_xattn_all.items() if k in ()}
    del _L3_xattn_all

    def _L3_ffn_setup():
        import jax, jax.numpy as jnp
        import numpy as np
        EPS = 1e-05

        def _act_quant(x, bits=8):
            qb = float(2 ** (bits - 1) - 1)
            scale = qb / jnp.clip(jnp.max(jnp.abs(x), axis=-1, keepdims=True), EPS, None)
            x_dq = jnp.clip(jnp.round(x * scale), -qb, qb) / scale
            return x + jax.lax.stop_gradient(x_dq - x)

        def _weight_quant(w):
            s = jnp.clip(jnp.mean(jnp.abs(w)), EPS, None)
            w_dq = jnp.clip(jnp.round(w / s), -1.0, 1.0) * s
            return w + jax.lax.stop_gradient(w_dq - w)

        def _bitlinear(x, w, bits=8):
            return jnp.einsum('bsi,oi->bso', _act_quant(x, bits), _weight_quant(w))
        key = jax.random.key(seed)
        k1, k2, k3 = jax.random.split(key, 3)
        B, S, H = (4, 1024, 512)
        I = int(H * 2.0)
        return {'hidden_states': jax.random.normal(k1, (B, S, H), dtype=jnp.float32), 'w_up': jax.random.normal(k2, (I, H), dtype=jnp.float32) * (1.0 / np.sqrt(H)), 'w_down': jax.random.normal(k3, (H, I), dtype=jnp.float32) * (1.0 / np.sqrt(I))}
    _L3_ffn_all = _L3_ffn_setup()
    _L3_ffn_in = {k: v for k, v in _L3_ffn_all.items() if k in ('w_up', 'w_down')}
    del _L3_ffn_all
    return {'x': x, 'ctx_512': ctx_512, 'mask_SxS2_bk1': mask_SxS2_bk1, 'mask_BxS2_bf0': mask_BxS2_bf0, 'L0_xattn_W': _L0_xattn_in['W'], 'L0_xattn_b': _L0_xattn_in['b'], 'L0_ffn_gate_w': _L0_ffn_in['gate_w'], 'L0_ffn_wg': _L0_ffn_in['wg'], 'L0_ffn_wu': _L0_ffn_in['wu'], 'L0_ffn_wd': _L0_ffn_in['wd'], 'L0_ffn_sg': _L0_ffn_in['sg'], 'L0_ffn_su': _L0_ffn_in['su'], 'L0_ffn_sd': _L0_ffn_in['sd'], 'L1_xattn_Wq': _L1_xattn_in['Wq'], 'L1_xattn_Wk': _L1_xattn_in['Wk'], 'L1_xattn_gamma_raw': _L1_xattn_in['gamma_raw'], 'L1_ffn_factors': _L1_ffn_in['factors'], 'L1_ffn_bias': _L1_ffn_in['bias'], 'L2_xattn_Wq': _L2_xattn_in['Wq'], 'L2_xattn_bq': _L2_xattn_in['bq'], 'L2_xattn_Wk': _L2_xattn_in['Wk'], 'L2_xattn_bk': _L2_xattn_in['bk'], 'L2_ffn_in_gamma': _L2_ffn_in['in_gamma'], 'L2_ffn_in_beta': _L2_ffn_in['in_beta'], 'L2_ffn_agg_w': _L2_ffn_in['agg_w'], 'L2_ffn_agg_b': _L2_ffn_in['agg_b'], 'L2_ffn_pn_gamma': _L2_ffn_in['pn_gamma'], 'L2_ffn_pn_beta': _L2_ffn_in['pn_beta'], 'L2_ffn_d1_w': _L2_ffn_in['d1_w'], 'L2_ffn_d1_b': _L2_ffn_in['d1_b'], 'L2_ffn_d2_w': _L2_ffn_in['d2_w'], 'L2_ffn_d2_b': _L2_ffn_in['d2_b'], 'L2_ffn_bc_w': _L2_ffn_in['bc_w'], 'L2_ffn_bc_b': _L2_ffn_in['bc_b'], 'L2_ffn_gate_w': _L2_ffn_in['gate_w'], 'L2_ffn_gate_b': _L2_ffn_in['gate_b'], 'L2_ffn_out_gamma': _L2_ffn_in['out_gamma'], 'L2_ffn_out_beta': _L2_ffn_in['out_beta'], 'L3_ffn_w_up': _L3_ffn_in['w_up'], 'L3_ffn_w_down': _L3_ffn_in['w_down']}

def reference(x, ctx_512, mask_SxS2_bk1, mask_BxS2_bf0, L0_xattn_W, L0_xattn_b, L0_ffn_gate_w, L0_ffn_wg, L0_ffn_wu, L0_ffn_wd, L0_ffn_sg, L0_ffn_su, L0_ffn_sd, L1_xattn_Wq, L1_xattn_Wk, L1_xattn_gamma_raw, L1_ffn_factors, L1_ffn_bias, L2_xattn_Wq, L2_xattn_bq, L2_xattn_Wk, L2_xattn_bk, L2_ffn_in_gamma, L2_ffn_in_beta, L2_ffn_agg_w, L2_ffn_agg_b, L2_ffn_pn_gamma, L2_ffn_pn_beta, L2_ffn_d1_w, L2_ffn_d1_b, L2_ffn_d2_w, L2_ffn_d2_b, L2_ffn_bc_w, L2_ffn_bc_b, L2_ffn_gate_w, L2_ffn_gate_b, L2_ffn_out_gamma, L2_ffn_out_beta, L3_ffn_w_up, L3_ffn_w_down):
    import jax
    import jax.numpy as jnp

    def _L0_xattn_ref(x, adj, W, b):
        import jax, jax.numpy as jnp
        import numpy as np
        P_ASEM = 0.6
        D = x.shape[-1]
        Wi = W[:, :D]
        Wj = W[:, D:]
        si = jnp.einsum('bnd,d->bn', x, Wi[0])
        sj = jnp.einsum('bnd,d->bn', x, Wj[0])
        xij = jax.nn.sigmoid(si[:, :, None] + sj[:, None, :] + b[0])
        return P_ASEM * xij + (1.0 - P_ASEM) * adj

    def _L0_ffn_ref(hidden_states, gate_w, wg, wu, wd, sg, su, sd):
        import jax, jax.numpy as jnp
        import numpy as np
        HID = 512
        N_EXP = 32
        F_EXP = 192
        TOP_K = 6
        F_SH = 384
        B, S = (1, 256)
        orig_shape = hidden_states.shape
        x = hidden_states.reshape(-1, HID)
        scores = jax.nn.sigmoid(x @ gate_w)
        topk_w, topk_i = jax.lax.top_k(scores, TOP_K)
        topk_w = topk_w / (jnp.sum(topk_w, axis=-1, keepdims=True) + 1e-20)
        combine = jnp.sum(jax.nn.one_hot(topk_i, N_EXP, dtype=topk_w.dtype) * topk_w[..., None], axis=1)
        g = jnp.einsum('td,edf->tef', x, wg)
        u = jnp.einsum('td,edf->tef', x, wu)
        act = jax.nn.silu(g) * u
        routed = jnp.einsum('tef,efd,te->td', act, wd, combine)
        routed = routed.reshape(orig_shape)
        shared = jax.nn.silu(hidden_states @ sg) * (hidden_states @ su) @ sd
        return routed + shared

    def _L1_xattn_ref(h, adj_raw, Wq, Wk, gamma_raw):
        import jax, jax.numpy as jnp
        import numpy as np
        B, N, D = (16, 512, 128)
        H = 4
        TOP_K_RATIO = 0.3
        b, n, dm = h.shape
        d = dm // H
        Q = (h @ Wq.T).reshape(b, n, H, d).transpose(0, 2, 1, 3)
        K = (h @ Wk.T).reshape(b, n, H, d).transpose(0, 2, 1, 3)
        sim = jnp.einsum('bhnd,bhmd->bnm', Q, K) / (jnp.sqrt(jnp.float32(d)) * H)
        k = max(1, int(n * TOP_K_RATIO))
        topk_vals = jax.lax.top_k(sim, k)[0]
        threshold = topk_vals[:, :, -1:]
        sparse_mask = (sim >= threshold).astype(sim.dtype)
        A_learned = jax.nn.sigmoid(sim) * sparse_mask
        A_learned = (A_learned + jnp.swapaxes(A_learned, -1, -2)) * 0.5
        gamma = jax.nn.sigmoid(gamma_raw)
        return (1.0 - gamma) * adj_raw + gamma * A_learned

    def _L1_ffn_ref(x, factors, bias):
        import math
        import jax, jax.numpy as jnp
        import numpy as np
        DIM = 512
        RANK = 8
        B, T = (4, 1024)

        def _orthogonal(key, n):
            a = jax.random.normal(key, (n, n), dtype=jnp.float32)
            q, r = jnp.linalg.qr(a)
            q = q * jnp.sign(jnp.diagonal(r))[None, :]
            return q
        rank = factors.shape[0]
        mixed = jnp.einsum('btd,rde->bte', x, factors)
        mixed = mixed / math.sqrt(rank) + bias
        return mixed

    def _L2_xattn_ref(q, k, attn_mask, key_padding_mask, qc_score, Wq, bq, Wk, bk):
        import jax, jax.numpy as jnp
        import numpy as np
        B, S, H = (8, 512, 128)
        qp = jnp.einsum('bsh,oh->bso', q, Wq) + bq
        kp = jnp.einsum('bth,oh->bto', k, Wk) + bk
        scaling = jnp.asarray(float(H) ** (-0.5), dtype=qp.dtype)
        scores = jnp.einsum('bsh,bth->bst', qp, kp) * scaling
        scores = scores * qc_score
        mask = attn_mask[None, :, :] | key_padding_mask[:, None, :]
        scores = jnp.where(mask, -jnp.inf, scores)
        return jax.nn.softmax(scores, axis=-1)

    def _L2_ffn_ref(x, in_gamma, in_beta, agg_w, agg_b, pn_gamma, pn_beta, d1_w, d1_b, d2_w, d2_b, bc_w, bc_b, gate_w, gate_b, out_gamma, out_beta):
        import jax, jax.numpy as jnp
        import numpy as np
        EPS = 1e-06
        K_STEPS = 4
        USE_GATING = True

        def layer_norm(x, gamma, beta):
            mu = jnp.mean(x, axis=-1, keepdims=True)
            var = jnp.mean(jnp.square(x - mu), axis=-1, keepdims=True)
            return (x - mu) * jax.lax.rsqrt(var + EPS) * gamma + beta
        x_norm = layer_norm(x, in_gamma, in_beta)
        thought = x_norm[:, -1, :] @ agg_w + agg_b
        for _ in range(K_STEPS):
            t = layer_norm(thought, pn_gamma, pn_beta)
            t = jax.nn.gelu(t @ d1_w + d1_b, approximate=False)
            thought = thought + (t @ d2_w + d2_b)
        broadcast = (thought @ bc_w + bc_b)[:, None, :]
        if USE_GATING:
            gate = jax.nn.sigmoid(x @ gate_w + gate_b)
            out = x + gate * broadcast
        else:
            out = x + broadcast
        return layer_norm(out, out_gamma, out_beta)

    def _L3_xattn_ref(q, k, v):
        import jax, jax.numpy as jnp
        import numpy as np
        B, S, E = (2, 512, 512)
        QH, KVH = (32, 8)
        D = E // QH
        G = QH // KVH
        DROPOUT = 1.0
        b, s, _ = q.shape
        qh = q.reshape(b, s, KVH, G, D).transpose(0, 2, 3, 1, 4)
        kh = k.reshape(b, s, KVH, D).transpose(0, 2, 1, 3)
        vh = v.reshape(b, s, KVH, D).transpose(0, 2, 1, 3)
        scale = 1.0 / jnp.sqrt(jnp.float32(D))
        scores = jnp.einsum('bkgsd,bktd->bkgst', qh, kh) * scale
        attn = jax.nn.softmax(scores, axis=-1) / DROPOUT
        out = jnp.einsum('bkgst,bktd->bkgsd', attn, vh)
        return out.transpose(0, 3, 1, 2, 4).reshape(b, s, E)

    def _L3_ffn_ref(hidden_states, w_up, w_down):
        import jax, jax.numpy as jnp
        import numpy as np
        EPS = 1e-05

        def _act_quant(x, bits=8):
            qb = float(2 ** (bits - 1) - 1)
            scale = qb / jnp.clip(jnp.max(jnp.abs(x), axis=-1, keepdims=True), EPS, None)
            x_dq = jnp.clip(jnp.round(x * scale), -qb, qb) / scale
            return x + jax.lax.stop_gradient(x_dq - x)

        def _weight_quant(w):
            s = jnp.clip(jnp.mean(jnp.abs(w)), EPS, None)
            w_dq = jnp.clip(jnp.round(w / s), -1.0, 1.0) * s
            return w + jax.lax.stop_gradient(w_dq - w)

        def _bitlinear(x, w, bits=8):
            return jnp.einsum('bsi,oi->bso', _act_quant(x, bits), _weight_quant(w))
        bits = 8
        h = _bitlinear(hidden_states, w_up, bits)
        h = jnp.square(jax.nn.relu(h))
        out = _bitlinear(h, w_down, bits)
        return out
    x = x + _L0_xattn_ref(ctx_512, _layernorm(x, axis=-1), L0_xattn_W, L0_xattn_b)
    x = x + _L0_ffn_ref(_layernorm(x, axis=-1), L0_ffn_gate_w, L0_ffn_wg, L0_ffn_wu, L0_ffn_wd, L0_ffn_sg, L0_ffn_su, L0_ffn_sd)
    x = x + _L1_xattn_ref(ctx_512, _layernorm(x, axis=-1), L1_xattn_Wq, L1_xattn_Wk, L1_xattn_gamma_raw)
    x = x + _L1_ffn_ref(_layernorm(x, axis=-1), L1_ffn_factors, L1_ffn_bias)
    x = x + _L2_xattn_ref(ctx_512, ctx_512, mask_SxS2_bk1, mask_BxS2_bf0, _layernorm(x, axis=-1), L2_xattn_Wq, L2_xattn_bq, L2_xattn_Wk, L2_xattn_bk)
    x = x + _L2_ffn_ref(_layernorm(x, axis=-1), L2_ffn_in_gamma, L2_ffn_in_beta, L2_ffn_agg_w, L2_ffn_agg_b, L2_ffn_pn_gamma, L2_ffn_pn_beta, L2_ffn_d1_w, L2_ffn_d1_b, L2_ffn_d2_w, L2_ffn_d2_b, L2_ffn_bc_w, L2_ffn_bc_b, L2_ffn_gate_w, L2_ffn_gate_b, L2_ffn_out_gamma, L2_ffn_out_beta)
    x = x + _L3_xattn_ref(_layernorm(x, axis=-1), ctx_512, ctx_512)
    x = x + _L3_ffn_ref(_layernorm(x, axis=-1), L3_ffn_w_up, L3_ffn_w_down)
    return x

_drawn_inputs = setup_inputs


def setup_inputs(seed=0):
    import zlib

    import numpy as np

    out = dict(_drawn_inputs(seed))
    spreads = {'L1_ffn_bias': (0.0, 0.1),
     'L2_xattn_bq': (0.0, 0.8),
     'L2_xattn_bk': (0.0, 0.8),
     'L2_ffn_in_gamma': (1.0, 0.6),
     'L2_ffn_in_beta': (0.0, 0.734),
     'L2_ffn_agg_b': (0.0, 0.451),
     'L2_ffn_pn_gamma': (1.0, 0.6),
     'L2_ffn_pn_beta': (0.0, 0.696),
     'L2_ffn_d1_b': (0.0, 0.387),
     'L2_ffn_d2_b': (0.0, 0.1),
     'L2_ffn_bc_b': (0.0, 0.407),
     'L2_ffn_gate_b': (0.0, 0.8),
     'L2_ffn_out_gamma': (1.0, 0.2),
     'L2_ffn_out_beta': (0.0, 0.1)}
    factors = {'L0_ffn_gate_w': 3.878,
     'L0_ffn_wg': 3.612,
     'L0_ffn_wu': 3.553,
     'L0_ffn_wd': 3.551,
     'L2_xattn_Wq': 6.468,
     'L2_xattn_Wk': 6.367,
     'L2_ffn_gate_w': 2.93}
    for name, (base, spread) in spreads.items():
        noise = np.random.default_rng([zlib.crc32(name.encode()), seed]).standard_normal(out[name].shape)
        drawn = base * np.exp(spread * noise) if base else spread * noise
        out[name] = jnp.asarray(drawn.astype(out[name].dtype))
    for name, factor in factors.items():
        out[name] = (out[name] * factor).astype(out[name].dtype)
    return out
```

```python
from contextlib import ExitStack

import concourse.bass as bass
from concourse import mybir
from concourse.alu_op_type import AluOpType as ALU

F32 = mybir.dt.float32
F16 = mybir.dt.float16
BF16 = mybir.dt.bfloat16
U8 = mybir.dt.uint8
I32 = mybir.dt.int32
ACT = mybir.ActivationFunctionType
AX = mybir.AxisListType

P = 128
B, S, D = 4, 512, 512
C = 128
TPB = S // P
NT = B * TPB
KC = D // P
E, F, TOPK = 32, 192, 6
FSH = 384
NE = E + FSH // F
W_SCALE = 64.0
K_SEL = int(S * 0.3)
NEG = -3.0e38
MASKED = -1.0e38
P_ASEM = 0.6
HID = 2048
K_STEPS = 4
QH, KVH, DH = 32, 8, 16
IUP = 1024
G_SCALE = 16.0
MAGIC = 1.5 * 2.0 ** 23


def tile_of(tensor, t):
    if isinstance(t, int):
        return tensor[:, t, :]
    return tensor[:, bass.ds(t, 1), :].rearrange("p a d -> p (a d)")


def hold(eng, semaphore, value):
    eng.wait_ge(semaphore, value)
    eng.sem_inc(Norm.held, 1)


class Norm:

    held = None

    def __init__(self, name, sb, sem, eps):
        self.eps = eps
        self.stats = sb(name + "_stats", [P, TPB, 6], F32)
        self.meanvar = sb(name + "_meanvar", [P, TPB, 2], F32)
        self.vareps = sb(name + "_vareps", [P, TPB], F32)
        self.rstd = sb(name + "_rstd", [P, TPB], F32)
        self.shift = sb(name + "_shift", [P, TPB], F32)
        self.stats_done = sem(name + "_stats_done")
        self.meanvar_done = sem(name + "_meanvar_done")
        self.vareps_done = sem(name + "_vareps_done")
        self.rstd_done = sem(name + "_rstd_done")
        self.shift_done = sem(name + "_shift_done")

    def on_vector(self, dve, source, b, before):
        if before is not None:
            hold(dve, before[0], before[1])
        for t in range(TPB):
            dve.bn_stats(self.stats[:, t, :], source(t)).then_inc(self.stats_done, 1)
        hold(dve, self.stats_done, TPB * b + TPB)
        for t in range(TPB):
            dve.bn_aggr(self.meanvar[:, t, :], self.stats[:, t, :]).then_inc(self.meanvar_done, 1)
        dve.wait_ge(self.meanvar_done, TPB * b + TPB)
        dve.tensor_scalar(self.vareps[:], self.meanvar[:, :, 1], self.eps, None, ALU.add)\
            .then_inc(self.vareps_done, 1)
        dve.wait_ge(self.rstd_done, b + 1)
        dve.scalar_tensor_tensor(out=self.shift[:], in0=self.meanvar[:, :, 0], scalar=-1.0, in1=self.rstd[:],
                                 op0=ALU.mult, op1=ALU.mult).then_inc(self.shift_done, 1)
        dve.wait_ge(self.shift_done, b + 1)

    def on_gpsimd(self, pool, half, b):
        pool.wait_ge(self.vareps_done, b + 1)
        pool.tensor_tensor(self.rstd[:], self.vareps[:], half[:, 0:TPB], ALU.pow).then_inc(self.rstd_done, 1)


def split_matmul(pe, out, lhs_hi, lhs_lo, rhs_hi, rhs_lo, first, last):
    pe.matmul(out, lhs_hi, rhs_hi, start=first, stop=False)
    pe.matmul(out, lhs_hi, rhs_lo, start=False, stop=False)
    return pe.matmul(out, lhs_lo, rhs_hi, start=False, stop=last)


def program(nc, x, ctx_512, mask_SxS2_bk1, mask_BxS2_bf0, L0_xattn_W, L0_xattn_b, L0_ffn_gate_w, L0_ffn_wg,
            L0_ffn_wu, L0_ffn_wd, L0_ffn_sg, L0_ffn_su, L0_ffn_sd, L1_xattn_Wq, L1_xattn_Wk,
            L1_xattn_gamma_raw, L1_ffn_factors, L1_ffn_bias, L2_xattn_Wq, L2_xattn_bq, L2_xattn_Wk,
            L2_xattn_bk, L2_ffn_in_gamma, L2_ffn_in_beta, L2_ffn_agg_w, L2_ffn_agg_b, L2_ffn_pn_gamma,
            L2_ffn_pn_beta, L2_ffn_d1_w, L2_ffn_d1_b, L2_ffn_d2_w, L2_ffn_d2_b, L2_ffn_bc_w, L2_ffn_bc_b,
            L2_ffn_gate_w, L2_ffn_gate_b, L2_ffn_out_gamma, L2_ffn_out_beta, L3_ffn_w_up, L3_ffn_w_down,
            out):
    x_d = x.rearrange("b (t p) d -> p (b t) d", p=P)
    out_d = out.rearrange("b (t p) d -> p (b t) d", p=P)
    ctx_d = ctx_512.rearrange("b (t p) d -> p (b t) d", p=P)

    with ExitStack() as whole:
        def sb(name, shape, dt=F32):
            return whole.enter_context(nc.sbuf_tensor(name, shape, dt))

        signals = []

        def sem(name):
            signals.append(nc.alloc_semaphore(name))
            return signals[-1]

        def psum_banks(scope, name, n, dt=F32):
            width = 512 if dt == F32 else 1024
            return [scope.enter_context(nc.psum_tensor(f"{name}{i}", [P, width], dt)) for i in range(n)]

        Norm.held = nc.alloc_semaphore("held")

        xres = sb("xres", [P, NT, D])
        ctxs = sb("ctxs", [P, NT, C])
        ident = sb("ident", [P, P])
        ident_h = sb("ident_h", [P, P], F16)
        ident_b = sb("ident_b", [P, P], BF16)
        ones = sb("ones", [P, P])
        minus_half = sb("minus_half", [P, NT])
        gam = sb("gam", [P, 4])
        gate2_hi = sb("gate2_hi", [P, KC, D], F16)
        gate2_lo = sb("gate2_lo", [P, KC, D], F16)
        gate2_bias = sb("gate2_bias", [2, D], F16)
        ones_h = sb("ones_h", [2, P], F16)
        up_t = sb("up_t", [P, KC, IUP], BF16)
        dn_t = sb("dn_t", [P, IUP // P, D], BF16)
        tern = sb("tern", [P, 4])

        middle = whole.enter_context(ExitStack())
        def sbd(name, shape, dt=F32):
            return middle.enter_context(nc.sbuf_tensor(name, shape, dt))
        learned = sbd("learned", [P, NT, S])
        proj_hi = [None, None] + [sbd(f"proj_hi{i}", [P, B * S], F16) for i in (2, 3)]
        proj_lo = [None, None] + [sbd(f"proj_lo{i}", [P, B * S], F16) for i in (2, 3)]

        early = whole.enter_context(ExitStack())
        def sbe(name, shape, dt=F32):
            return early.enter_context(nc.sbuf_tensor(name, shape, dt))

        proj_hi[0], proj_lo[0] = [m[:].rearrange("p c e -> p (c e)") for m in (gate2_hi, gate2_lo)]
        halves_of_up = up_t[:].rearrange("p c e -> p (c e)").bitcast(F16)
        proj_hi[1], proj_lo[1] = halves_of_up[:, 0:B * S], halves_of_up[:, B * S:2 * B * S]
        hT_hi = sbe("hT_hi", [P, KC, B * S], F16)
        hT_lo = sbe("hT_lo", [P, KC, B * S], F16)
        scores = dn_t[:].rearrange("p k e -> p (k e)").bitcast(F32)[:, 0:NT * E].rearrange("p (t e) -> p t e", e=E)
        combine = sbe("combine", [P, NT, NE])

        first = whole.enter_context(ExitStack())
        def sbe(name, shape, dt=F32):
            return first.enter_context(nc.sbuf_tensor(name, shape, dt))

        ctxT = sbe("ctxT", [P, B * S])
        proj_f = [sbe(f"proj_f{i}", [P, S]) for i in range(2)]
        w0 = sbe("w0", [P, 2])
        b0 = sbe("b0", [P, 1])
        wj_rep = sbe("wj_rep", [P, P])
        row_term = sbe("row_term", [P, NT])
        proj_w = sbe("proj_w", [P, 4, C])
        proj_wT = sbe("proj_wT", [P, 4, C])
        proj_b = sbe("proj_b", [P, 2])
        gate_f = sbe("gate_f", [P, KC, E])
        gate_hi = sbe("gate_hi", [P, KC, E], F16)
        gate_lo = sbe("gate_lo", [P, KC, E], F16)

        x_in = sem("x_in")
        small_in = sem("small_in")
        ctx_in = sem("ctx_in")
        gamma_in = sem("gamma_in")
        consts_zeroed = sem("consts_zeroed")
        consts_done = sem("consts_done")
        ctx_transposed = sem("ctx_transposed")
        ctxT_done = sem("ctxT_done")
        projT_ready = sem("projT_ready")
        projT_done = sem("projT_done")
        proj_ready = sem("proj_ready")
        proj_done = sem("proj_done")
        wj_done = sem("wj_done")
        row_ready = sem("row_ready")
        row_done = sem("row_done")
        gate_hi_done = sem("gate_hi_done")
        gate_lo_done = sem("gate_lo_done")
        gamma_sig = sem("gamma_sig")
        gamma_done = sem("gamma_done")
        proj_hi_done = sem("proj_hi_done")
        proj_lo_done = sem("proj_lo_done")

        with ExitStack() as scope, nc.Block() as block:
            pT = psum_banks(scope, "setupT", 4)
            pW = psum_banks(scope, "setupW", 1)[0]
            pP = psum_banks(scope, "setupP", 2)
            pR = psum_banks(scope, "setupR", 1)[0]

            @block.sync
            def _(sp):
                sp.dma_start(ctxs[:], ctx_d).then_inc(ctx_in, 16)
                for i, w in enumerate((L1_xattn_Wq, L1_xattn_Wk, L2_xattn_Wq, L2_xattn_Wk)):
                    sp.dma_start(proj_w[:, i, :], w[:]).then_inc(small_in, 16)
                for i in range(2):
                    sp.dma_start(w0[:, i:i + 1], L0_xattn_W[0, i * C:(i + 1) * C].rearrange("(p a) -> p a", a=1))\
                        .then_inc(small_in, 16)
                sp.dma_start(b0[:], L0_xattn_b.rearrange("(a c) -> a c", a=1).to_broadcast([P, 1]))\
                    .then_inc(small_in, 16)
                sp.dma_start(proj_b[:, 0:1], L2_xattn_bq.rearrange("(p a) -> p a", a=1)).then_inc(small_in, 16)
                sp.dma_start(proj_b[:, 1:2], L2_xattn_bk.rearrange("(p a) -> p a", a=1)).then_inc(small_in, 16)
                sp.dma_start(gate_f[:], L0_ffn_gate_w.rearrange("(p c) e -> p c e", c=KC)).then_inc(small_in, 16)
                sp.dma_start(gam[:, 0:1], L1_xattn_gamma_raw.rearrange("(a c) -> a c", a=1).to_broadcast([P, 1])).then_inc(gamma_in, 16)
                for b in range(B):
                    sp.dma_start(xres[:, TPB * b:TPB * (b + 1), :], x_d[:, TPB * b:TPB * (b + 1), :])\
                        .then_inc(x_in, 16)

            @block.gpsimd
            def _(pool):
                for m in (ident, ident_h, ident_b):
                    pool.memset(m[:], 0.0).then_inc(consts_zeroed, 1)
                pool.memset(ones[:], 1.0).then_inc(consts_done, 1)
                pool.memset(minus_half[:], -0.5).then_inc(consts_done, 1)
                pool.wait_ge(consts_zeroed, 3)
                for m in (ident, ident_h, ident_b):
                    pool.affine_select(out=m[:], in_=m[:], compare_op=ALU.not_equal, fill=1.0, base=0,
                                       pattern=[[-1, P]], channel_multiplier=1).then_inc(consts_done, 1)

            @block.tensor
            def _(pe):
                pe.wait_ge(consts_done, 5)
                pe.wait_ge(small_in, 160)
                for i in range(4):
                    m = pe.transpose(pW[:, i * C:(i + 1) * C], proj_w[:, i, :], ident[:])
                m.then_inc(projT_ready, 1)
                pe.wait_ge(ctx_in, 16)
                for b in range(B):
                    for t in range(TPB):
                        m = pe.transpose(pT[b][:, t * P:(t + 1) * P], ctxs[:, TPB * b + t, :], ident[:])
                    m.then_inc(ctx_transposed, 1)
                pe.wait_ge(ctxT_done, B)
                for t in range(NT):
                    m = pe.matmul(pR[:, t:t + 1], ctxT[:, t * P:(t + 1) * P], w0[:, 0:1], start=True, stop=True)
                m.then_inc(row_ready, 1)
                pe.wait_ge(projT_done, 1)
                n = 0
                for i in range(4):
                    for b in range(B):
                        if n >= 2:
                            pe.wait_ge(proj_done, n - 1)
                        pe.matmul(pP[n % 2][:], proj_wT[:, i, :], ctxT[:, b * S:(b + 1) * S],
                                  start=True, stop=True).then_inc(proj_ready, 1)
                        n += 1

            @block.scalar
            def _(act):
                act.wait_ge(gamma_in, 16)
                act.activation(gam[:, 1:2], gam[:, 0:1], ACT.Sigmoid).then_inc(gamma_sig, 1)
                act.wait_ge(small_in, 160)
                act.activation(gate_hi[:], gate_f[:], ACT.Copy).then_inc(gate_hi_done, 1)
                for b in range(B):
                    act.wait_ge(ctx_transposed, b + 1)
                    act.activation(ctxT[:, b * S:(b + 1) * S], pT[b][:], ACT.Copy).then_inc(ctxT_done, 1)
                n = 0
                for i in range(4):
                    for b in range(B):
                        act.wait_ge(proj_ready, n + 1)
                        if n >= 2:
                            act.wait_ge(proj_lo_done, n - 1)
                        act.activation(proj_f[n % 2][:], pP[n % 2][:], ACT.Identity,
                                       bias=0.0 if i < 2 else proj_b[:, i - 2:i - 1]).then_inc(proj_done, 1)
                        act.wait_ge(proj_done, n + 1)
                        act.activation(proj_hi[i][:, b * S:(b + 1) * S], proj_f[n % 2][:], ACT.Copy)\
                            .then_inc(proj_hi_done, 1)
                        n += 1

            @block.vector
            def _(dve):
                dve.wait_ge(small_in, 160)
                dve.wait_ge(consts_done, 5)
                dve.tensor_scalar(wj_rep[:], ones[:], w0[:, 1:2], None, ALU.mult).then_inc(wj_done, 1)
                dve.wait_ge(projT_ready, 1)
                dve.tensor_copy(proj_wT[:].rearrange("p a c -> p (a c)"), pW[:]).then_inc(projT_done, 1)
                dve.wait_ge(gate_hi_done, 1)
                dve.tensor_tensor(gate_lo[:], gate_f[:], gate_hi[:], ALU.subtract).then_inc(gate_lo_done, 1)
                dve.wait_ge(gamma_sig, 1)
                dve.tensor_scalar(gam[:, 2:3], gam[:, 1:2], 0.5, None, ALU.mult).then_inc(gamma_done, 1)
                dve.tensor_scalar(gam[:, 3:4], gam[:, 1:2], -1.0, 1.0, ALU.mult, ALU.add).then_inc(gamma_done, 1)
                dve.wait_ge(row_ready, 1)
                dve.tensor_scalar(row_term[:], pR[:, 0:NT], b0[:, 0:1], None, ALU.add).then_inc(row_done, 1)
                n = 0
                for i in range(4):
                    for b in range(B):
                        dve.wait_ge(proj_hi_done, n + 1)
                        dve.tensor_tensor(proj_lo[i][:, b * S:(b + 1) * S], proj_f[n % 2][:],
                                          proj_hi[i][:, b * S:(b + 1) * S], ALU.subtract).then_inc(proj_lo_done, 1)
                        n += 1


        col_ready = sem("col_ready")
        sig_done = sem("sig_done")
        l0_scale_done = sem("l0_scale_done")
        l0_norm_done = sem("l0_norm_done")
        x1_done = sem("x1_done")
        h_done = sem("h_done")
        hT_ready = sem("hT_ready")
        hT_hi_done = sem("hT_hi_done")
        hT_lo_done = sem("hT_lo_done")
        logits_ready = sem("logits_ready")
        scores_done = sem("scores_done")

        with ExitStack() as scope:
            def sbl(name, shape, dt=F32):
                return scope.enter_context(nc.sbuf_tensor(name, shape, dt))
            l0_in = Norm("l0_in", sbl, sem, 1e-5)
            l0_out = Norm("l0_out", sbl, sem, 1e-5)
            sig = sbl("sig", [P, TPB, S])
            xn = sbl("xn", [P, TPB, D])
            h = xn
            l0_mul = sbl("l0_mul", [P, TPB])
            l0_add = sbl("l0_add", [P, TPB])
            pC = psum_banks(scope, "l0col", 1)[0]
            pH = psum_banks(scope, "l0hT", KC)
            pL = psum_banks(scope, "l0log", 1)[0]
            with nc.Fori(0, B) as b, nc.Block() as block:
                @block.tensor
                def _(pe):
                    pe.matmul(pC[:], wj_rep[:], ctxT[:, bass.ds(b * S, S)], start=True, stop=True)\
                        .then_inc(col_ready, 1)
                    pe.wait_ge(h_done, TPB * b + TPB)
                    for c in range(KC):
                        for t in range(TPB):
                            m = pe.transpose(pH[c][:, t * P:(t + 1) * P], h[:, t, c::KC], ident[:])
                        m.then_inc(hT_ready, 1)
                    pe.wait_ge(hT_lo_done, KC * b + KC)
                    for t in range(TPB):
                        for c in range(KC):
                            hi = hT_hi[:, c, bass.ds(b * S + t * P, P)]
                            lo = hT_lo[:, c, bass.ds(b * S + t * P, P)]
                            m = split_matmul(pe, pL[:, t * E:(t + 1) * E], hi, lo, gate_hi[:, c, :],
                                             gate_lo[:, c, :], c == 0, c == KC - 1)
                    m.then_inc(logits_ready, 1)

                @block.scalar
                def _(act):
                    act.wait_ge(col_ready, b + 1)
                    for t in range(TPB):
                        act.activation(sig[:, t, :], pC[:], ACT.Sigmoid, bias=row_term[:, bass.ds(b * TPB + t, 1)])\
                            .then_inc(sig_done, 1)
                    for c in range(KC):
                        act.wait_ge(hT_ready, KC * b + c + 1)
                        act.activation(hT_hi[:, c, bass.ds(b * S, S)], pH[c][:], ACT.Copy).then_inc(hT_hi_done, 1)
                    act.wait_ge(logits_ready, b + 1)
                    act.activation(scores[:, bass.ds(b * TPB, TPB), :].rearrange("p t e -> p (t e)"),
                                   pL[:, 0:TPB * E], ACT.Sigmoid).then_inc(scores_done, 1)

                @block.gpsimd
                def _(pool):
                    l0_in.on_gpsimd(pool, minus_half, b)
                    l0_out.on_gpsimd(pool, minus_half, b)

                @block.vector
                def _(dve):
                    l0_in.on_vector(dve, lambda t: tile_of(xres, b * TPB + t), b, (x_in, 16 * B))
                    dve.tensor_scalar(l0_mul[:], l0_in.rstd[:], 1.0 - P_ASEM, 1.0, ALU.mult, ALU.add)\
                        .then_inc(l0_scale_done, 1)
                    dve.tensor_scalar(l0_add[:], l0_in.shift[:], 1.0 - P_ASEM, None, ALU.mult)\
                        .then_inc(l0_scale_done, 1)
                    dve.wait_ge(l0_scale_done, 2 * b + 2)
                    for t in range(TPB):
                        dve.tensor_scalar(xn[:, t, :], tile_of(xres, b * TPB + t), l0_mul[:, t:t + 1],
                                          l0_add[:, t:t + 1], ALU.mult, ALU.add).then_inc(l0_norm_done, 1)
                    dve.wait_ge(l0_norm_done, TPB * b + TPB)
                    for t in range(TPB):
                        dve.wait_ge(sig_done, TPB * b + t + 1)
                        dve.scalar_tensor_tensor(out=tile_of(xres, b * TPB + t), in0=sig[:, t, :], scalar=P_ASEM,
                                                 in1=xn[:, t, :], op0=ALU.mult, op1=ALU.add).then_inc(x1_done, 1)
                    l0_out.on_vector(dve, lambda t: tile_of(xres, b * TPB + t), b, (x1_done, TPB * b + TPB))
                    for t in range(TPB):
                        dve.tensor_scalar(h[:, t, :], tile_of(xres, b * TPB + t), l0_out.rstd[:, t:t + 1],
                                          l0_out.shift[:, t:t + 1], ALU.mult, ALU.add).then_inc(h_done, 1)
                    for c in range(KC):
                        dve.wait_ge(hT_hi_done, KC * b + c + 1)
                        dve.tensor_tensor(hT_lo[:, c, bass.ds(b * S, S)], pH[c][:], hT_hi[:, c, bass.ds(b * S, S)],
                                          ALU.subtract).then_inc(hT_lo_done, 1)

        first.close()

        route = sem("route")
        with ExitStack() as scope, nc.Block() as block:
            def sbl(name, shape, dt=F32):
                return scope.enter_context(nc.sbuf_tensor(name, shape, dt))
            top8 = sbl("top8", [P, NT, 8])
            above = sbl("above", [P, NT, E])
            equal = sbl("equal", [P, NT, E])
            rank = sbl("rank", [P, NT, E])
            zero = sbl("zero_row", [P, E])
            room = sbl("room", [P, NT])
            weight = sbl("weight", [P, NT])

            @block.vector
            def _(dve):
                steps = [0]

                def done(*instructions):
                    for ins in instructions:
                        ins.then_inc(route, 1)
                        steps[0] += 1
                    dve.wait_ge(route, steps[0])

                done(*[dve.max(top8[:, t, :], scores[:, t, :]) for t in range(NT)],
                     dve.memset(zero[:], 0.0))
                least = top8[:, :, TOPK - 1:TOPK].to_broadcast([P, NT, E])
                done(dve.tensor_tensor(above[:], scores[:], least, ALU.is_gt),
                     dve.tensor_tensor(equal[:], scores[:], least, ALU.is_equal))
                done(dve.tensor_reduce(room[:], above[:], AX.X, ALU.add),
                     *[dve.tensor_tensor_scan(rank[:, t, :], equal[:, t, :], zero[:], 0.0, ALU.add, ALU.add)
                       for t in range(NT)])
                done(dve.tensor_scalar(room[:], room[:], -1.0, float(TOPK), ALU.mult, ALU.add))
                done(dve.tensor_tensor(rank[:], rank[:], room[:].unsqueeze(2).to_broadcast([P, NT, E]), ALU.is_le))
                done(dve.tensor_tensor(equal[:], equal[:], rank[:], ALU.mult))
                done(dve.tensor_tensor(above[:], above[:], equal[:], ALU.add))
                done(dve.tensor_tensor(above[:], above[:], scores[:], ALU.mult))
                done(dve.tensor_reduce(weight[:], above[:], AX.X, ALU.add))
                done(dve.tensor_scalar(weight[:], weight[:], 1e-20, W_SCALE, ALU.add, ALU.mult))
                done(dve.reciprocal(weight[:], weight[:]))
                done(dve.tensor_tensor(combine[:, :, 0:E], above[:],
                                       weight[:].unsqueeze(2).to_broadcast([P, NT, E]), ALU.mult),
                     dve.memset(combine[:, :, E:NE], 1.0 / W_SCALE))

        w_in = [sem("w_in_even"), sem("w_in_odd")]
        w_hi_done = sem("w_hi_done")
        w_lo_done = sem("w_lo_done")
        up_ready = sem("up_ready")
        silu_done = sem("silu_done")
        act_done = sem("act_done")
        act_hi_done = sem("act_hi_done")
        act_lo_done = sem("act_lo_done")
        down_ready = sem("down_ready")
        added = sem("added")
        sim_ready = sem("sim_ready")
        sim_copied = sem("sim_copied")
        sel_step = sem("sel_step")
        sim_sig_done = sem("sim_sig_done")
        learned_done = sem("learned_done")
        kept_done = sem("kept_done")

        PAIRS = NE // 2
        GB = B
        NBLK = 2 * GB
        ROUNDS = (K_SEL - 1) // 8
        SEL_STEPS = 2 * ROUNDS + 1

        with ExitStack() as scope:
            def sbl(name, shape, dt=F32):
                return scope.enter_context(nc.sbuf_tensor(name, shape, dt))
            wup_f = [sbl(f"wup_f{i}", [P, KC, 2, F]) for i in range(2)]
            wdn_f = [sbl(f"wdn_f{i}", [P, 2, D]) for i in range(2)]
            wup_hi = [sbl(f"wup_hi{i}", [P, KC, 3 * P], F16) for i in range(2)]
            wup_lo = [sbl(f"wup_lo{i}", [P, KC, 3 * P], F16) for i in range(2)]
            wdn_hi = [sbl(f"wdn_hi{i}", [P, 2, D], F16) for i in range(2)]
            wdn_lo = [sbl(f"wdn_lo{i}", [P, 2, D], F16) for i in range(2)]
            silu_a = sbl("silu_a", [P, S])
            silu_c = sbl("silu_c", [P // 2, S])
            prod_a = sbl("prod_a", [P, S])
            prod_c = sbl("prod_c", [P // 2, S])
            acta_hi = sbl("acta_hi", [P, S], F16)
            acta_lo = sbl("acta_lo", [P, S], F16)
            actc = sbl("actc", [P, S], F16)
            sim = sbl("sim", [P, S])
            sim_work = sbl("sim_work", [P, S])
            sim_top = sbl("sim_top", [P, 8])
            sim_sig = sbl("sim_sig", [P, S])
            pU = psum_banks(scope, "moeU", 3)
            pY = psum_banks(scope, "moeY", 4)
            pS = psum_banks(scope, "moeS", 1)[0]

            def load(sp, par, wg, wu, wd):
                sp.dma_start(wup_f[par][:, :, 0, :], wg.rearrange("(p c) f -> p c f", c=KC)).then_inc(w_in[par], 16)
                sp.dma_start(wup_f[par][:, :, 1, :], wu.rearrange("(p c) f -> p c f", c=KC)).then_inc(w_in[par], 16)
                sp.dma_start(wdn_f[par][:, 0, :], wd[0:P, :]).then_inc(w_in[par], 16)
                for half in range(2):
                    sp.dma_start(wdn_f[par][64 * half:64 * half + 64, 1, :], wd[P:F, :]).then_inc(w_in[par], 16)

            def expert(w, n):
                return w[n] if isinstance(n, int) else w[bass.ds(n, 1)].rearrange("a r f -> (a r) f")

            def split_hi(act, par, pair):
                act.wait_ge(w_in[par], 80 * pair + 80)
                f, h16 = wup_f[par], wup_hi[par]
                act.activation(h16[:, :, 0:P], f[:, :, 0, 0:P], ACT.Copy, scale=W_SCALE).then_inc(w_hi_done, 1)
                act.activation(h16[:, :, P:2 * P], f[:, :, 1, 0:P], ACT.Copy, scale=W_SCALE).then_inc(w_hi_done, 1)
                act.activation(h16[:, :, 2 * P:3 * P].rearrange("p c (g f) -> p c g f", g=2), f[:, :, :, P:F],
                               ACT.Copy, scale=W_SCALE).then_inc(w_hi_done, 1)
                act.activation(wdn_hi[par][:], wdn_f[par][:], ACT.Copy, scale=W_SCALE).then_inc(w_hi_done, 1)

            def split_lo(dve, par, n):
                dve.wait_ge(w_hi_done, 4 * n + 4)
                f, h16, l16 = wup_f[par], wup_hi[par], wup_lo[par]
                for o, i0, i1 in ((l16[:, :, 0:P], f[:, :, 0, 0:P], h16[:, :, 0:P]),
                                  (l16[:, :, P:2 * P], f[:, :, 1, 0:P], h16[:, :, P:2 * P]),
                                  (l16[:, :, 2 * P:2 * P + 64], f[:, :, 0, P:F], h16[:, :, 2 * P:2 * P + 64]),
                                  (l16[:, :, 2 * P + 64:3 * P], f[:, :, 1, P:F], h16[:, :, 2 * P + 64:3 * P]),
                                  (wdn_lo[par][:], wdn_f[par][:], wdn_hi[par][:])):
                    dve.scalar_tensor_tensor(out=o, in0=i0, scalar=W_SCALE, in1=i1, op0=ALU.mult,
                                             op1=ALU.subtract).then_inc(w_lo_done, 1)

            def pe_pair(pe, pair, with_sim):
                def up(k):
                    par, g, m = k // GB, k % GB, NBLK * pair + k
                    if g == 0:
                        pe.wait_ge(w_lo_done, 5 * (2 * pair + par) + 5)
                    if k >= 1:
                        pe.wait_ge(act_done, 2 * m)
                    for col, bank in ((0, 0), (2, 2), (1, 1)):
                        cols = slice(col * P, (col + 1) * P)
                        for c in range(KC):
                            mm = split_matmul(pe, pU[bank][:], wup_hi[par][:, c, cols], wup_lo[par][:, c, cols],
                                              hT_hi[:, c, g * S:(g + 1) * S], hT_lo[:, c, g * S:(g + 1) * S],
                                              c == 0, c == KC - 1)
                        mm.then_inc(up_ready, 1)

                def down(k):
                    par, m = k // GB, NBLK * pair + k
                    pe.wait_ge(act_lo_done, 2 * m + 2)
                    for t in range(TPB):
                        pe.wait_ge(added, TPB * m + t + 1)
                        tok = slice(t * P, (t + 1) * P)
                        pe.matmul(pY[t][:], acta_hi[:, tok], wdn_hi[par][:, 0, :], start=True, stop=False)
                        pe.matmul(pY[t][:], acta_hi[:, tok], wdn_lo[par][:, 0, :], start=False, stop=False)
                        pe.matmul(pY[t][:], acta_lo[:, tok], wdn_hi[par][:, 0, :], start=False, stop=False)
                        pe.matmul(pY[t][:], actc[:, tok], wdn_hi[par][:, 1, :], start=False, stop=False)
                        pe.matmul(pY[t][:], actc[0:64, tok], wdn_lo[par][0:64, 1, :], start=False, stop=True)\
                            .then_inc(down_ready, 1)

                for k in range(NBLK):
                    up(k)
                    if k >= 1:
                        down(k - 1)
                    if k == 0 and with_sim:
                        pe.wait_ge(act_done, 2 * NBLK * pair + 2)
                        rows = bass.ds(pair * P, P)
                        cols = bass.ds((pair // TPB) * S, S)
                        split_matmul(pe, pS[:], proj_hi[0][:, rows], proj_lo[0][:, rows], proj_hi[1][:, cols],
                                     proj_lo[1][:, cols], True, True).then_inc(sim_ready, 1)
                down(NBLK - 1)

            def act_pair(act, pair, with_sim, with_next):
                for k in range(NBLK):
                    m = NBLK * pair + k
                    act.wait_ge(up_ready, 3 * m + 1)
                    act.activation(silu_a[:], pU[0][:], ACT.Silu, scale=1.0 / W_SCALE).then_inc(silu_done, 1)
                    act.wait_ge(up_ready, 3 * m + 2)
                    act.activation(silu_c[:], pU[2][0:64, :], ACT.Silu, scale=1.0 / W_SCALE).then_inc(silu_done, 1)
                    if k >= 1:
                        act.wait_ge(down_ready, TPB * m)
                    act.wait_ge(act_done, 2 * m + 1)
                    act.activation(acta_hi[:], prod_a[:], ACT.Copy).then_inc(act_hi_done, 1)
                    act.wait_ge(act_done, 2 * m + 2)
                    act.activation(actc[0:64, :], prod_c[:], ACT.Copy).then_inc(act_hi_done, 1)
                    if k == 0:
                        split_hi(act, 1, pair)
                    if k == GB and with_next:
                        split_hi(act, 0, pair + 1)
                    if k == 2 and with_sim:
                        act.wait_ge(sim_copied, pair + 1)
                        act.activation(sim_sig[:], sim[:], ACT.Sigmoid).then_inc(sim_sig_done, 1)

            def dve_pair(dve, pair, with_sim, with_next):
                def add(k):
                    par, g, m = k // GB, k % GB, NBLK * pair + k
                    for t in range(TPB):
                        tile = TPB * g + t
                        dve.wait_ge(down_ready, TPB * m + t + 1)
                        n = 2 * pair + par
                        w = combine[:, tile, n:n + 1] if isinstance(n, int) else combine[:, tile, bass.ds(n, 1)]
                        dve.scalar_tensor_tensor(out=xres[:, tile, :], in0=pY[t][:], scalar=w,
                                                 in1=xres[:, tile, :], op0=ALU.mult, op1=ALU.add).then_inc(added, 1)

                def rounds(first, last):
                    for r in range(first, last):
                        step = SEL_STEPS * pair + 2 * r
                        src = sim if r == 0 else sim_work
                        if r >= 1:
                            hold(dve, sel_step, step)
                        dve.max(sim_top[:], src[:]).then_inc(sel_step, 1)
                        if r < ROUNDS:
                            hold(dve, sel_step, step + 1)
                            dve.match_replace(sim_work[:], sim_top[:], src[:], NEG).then_inc(sel_step, 1)

                for k in range(NBLK):
                    m = NBLK * pair + k
                    dve.wait_ge(silu_done, 2 * m + 1)
                    dve.wait_ge(up_ready, 3 * m + 3)
                    if k >= 1:
                        dve.wait_ge(act_lo_done, 2 * m)
                    dve.scalar_tensor_tensor(out=prod_a[:], in0=pU[1][:], scalar=1.0 / W_SCALE, in1=silu_a[:],
                                             op0=ALU.mult, op1=ALU.mult).then_inc(act_done, 1)
                    dve.wait_ge(silu_done, 2 * m + 2)
                    dve.scalar_tensor_tensor(out=prod_c[:], in0=pU[2][64:128, :], scalar=1.0 / W_SCALE,
                                             in1=silu_c[:], op0=ALU.mult, op1=ALU.mult).then_inc(act_done, 1)
                    dve.wait_ge(act_hi_done, 2 * m + 1)
                    dve.tensor_tensor(acta_lo[:], prod_a[:], acta_hi[:], ALU.subtract).then_inc(act_lo_done, 1)
                    dve.wait_ge(act_hi_done, 2 * m + 2)
                    dve.tensor_tensor(actc[64:128, :], prod_c[:], actc[0:64, :], ALU.subtract)\
                        .then_inc(act_lo_done, 1)
                    if k == 0:
                        split_lo(dve, 1, 2 * pair + 1)
                    if k == GB and with_next:
                        split_lo(dve, 0, 2 * pair + 2)
                    if k >= 1:
                        add(k - 1)
                    if with_sim:
                        if k == 1:
                            dve.wait_ge(sim_ready, pair + 1)
                            dve.tensor_scalar(sim[:], pS[:], 1.0 / (4.0 * 32.0 ** 0.5), None, ALU.mult)\
                                .then_inc(sim_copied, 1)
                            hold(dve, sim_copied, pair + 1)
                        if k >= 2:
                            per = -(-(ROUNDS + 1) // (NBLK - 2))
                            rounds(per * (k - 2), min(per * (k - 1), ROUNDS + 1))
                        if k == NBLK - 1:
                            dve.wait_ge(sel_step, SEL_STEPS * pair + SEL_STEPS)
                            dve.wait_ge(sim_sig_done, pair + 1)
                            at = (K_SEL - 1) % 8
                            dve.scalar_tensor_tensor(out=sim_work[:], in0=sim[:], scalar=sim_top[:, at:at + 1],
                                                     in1=sim_sig[:], op0=ALU.is_ge, op1=ALU.mult)\
                                .then_inc(kept_done, 1)
                            dve.wait_ge(kept_done, pair + 1)
                            dve.tensor_scalar(tile_of(learned, pair), sim_work[:], gam[:, 2:3], None, ALU.mult)\
                                .then_inc(learned_done, 1)
                add(NBLK - 1)

            with nc.Block() as block:
                @block.sync
                def _(sp):
                    for par in range(2):
                        load(sp, par, L0_ffn_wg[par], L0_ffn_wu[par], L0_ffn_wd[par])
                    with sp.Fori(1, E // 2) as pair:
                        for par in range(2):
                            n = 2 * pair + par
                            sp.wait_ge(w_lo_done, 5 * n - 5)
                            load(sp, par, expert(L0_ffn_wg, n), expert(L0_ffn_wu, n), expert(L0_ffn_wd, n))
                    for par in range(2):
                        cols = slice(par * F, (par + 1) * F)
                        sp.wait_ge(w_lo_done, 5 * (E + par) - 5)
                        load(sp, par, L0_ffn_sg[:, cols], L0_ffn_su[:, cols], L0_ffn_sd[cols, :])

                @block.tensor
                def _(pe):
                    with pe.Fori(0, E // 2) as pair:
                        pe_pair(pe, pair, True)
                    pe_pair(pe, E // 2, False)

                @block.scalar
                def _(act):
                    split_hi(act, 0, 0)
                    with act.Fori(0, E // 2) as pair:
                        act_pair(act, pair, True, True)
                    act_pair(act, E // 2, False, False)

                @block.vector
                def _(dve):
                    dve.sem_inc(added, TPB)
                    split_lo(dve, 0, 0)
                    with dve.Fori(0, E // 2) as pair:
                        dve_pair(dve, pair, True, True)
                    dve_pair(dve, E // 2, False, False)
        early.close()
        nc.clear_and_free_semaphores(signals)
        nc.all_engine_barrier()
        mid = whole.enter_context(ExitStack())
        def sbm(name, shape, dt=F32):
            return mid.enter_context(nc.sbuf_tensor(name, shape, dt))
        mix_hi = sbm("mix_hi", [P, KC, D], F16)
        mix_lo = sbm("mix_lo", [P, KC, D], F16)
        mix_bias = sbm("mix_bias", [2, D], F16)
        mask_rows = sbm("mask_rows", [P, TPB, S])
        mask_keys = sbm("mask_keys", [P, B, S])

        weights_in = sem("weights_in")
        ones_set = sem("ones_set")
        prep = sem("prep")
        prep_hi = sem("prep_hi")
        halves_done = sem("halves_done")
        prep_tern = sem("prep_tern")
        tern_in = sem("tern_in")
        abs_done = sem("abs_done")
        total_ready = sem("total_ready")
        rounded = sem("rounded")
        turned = sem("turned")
        turn_copied = sem("turn_copied")
        bias_moved = sem("bias_moved")

        with ExitStack() as scope, nc.Block() as block:
            def sbl(name, shape, dt=F32):
                return scope.enter_context(nc.sbuf_tensor(name, shape, dt))
            factor = sbl("factor", [P, 8, KC, D // 4])
            mix_f = sbl("mix_f", [P, KC, D])
            mask_words = sbl("mask_words", [P, TPB, S // 4], I32)
            keys_words = sbl("keys_words", [P, B, S // 4], I32)
            gate2_f = sbl("gate2_f", [P, KC, D])
            row_scratch = sbl("row_scratch", [1, 2, D])
            bias_halves = sbl("bias_halves", [1, 2, 2, D], F16)

            @block.sync
            def _(sp):
                sp.dma_start(gate2_f[:], L2_ffn_gate_w.rearrange("(p c) e -> p c e", c=KC)).then_inc(weights_in, 16)
                sp.dma_start(mask_words[:], mask_SxS2_bk1.rearrange("(t p) s -> p t s", p=P)).then_inc(weights_in, 16)
                for b in range(B):
                    sp.dma_start(keys_words[:, b, :], mask_BxS2_bf0[b:b + 1, :].to_broadcast([P, S // 4]))\
                        .then_inc(weights_in, 16)
                for i, bias in enumerate((L1_ffn_bias, L2_ffn_gate_b)):
                    sp.dma_start(row_scratch[0:1, i, :], bias.rearrange("(a d) -> a d", a=1)).then_inc(weights_in, 16)
                for q in range(4):
                    if q >= 1:
                        sp.wait_ge(prep, 7 * q)
                    for r in range(8):
                        quarter = L1_ffn_factors[r].rearrange("(p c) e -> p c e", c=KC)[:, :, q * P:(q + 1) * P]
                        sp.dma_start(factor[:, r, :, :], quarter).then_inc(weights_in, 16)
                sp.wait_ge(halves_done, 1)
                for i, dst in enumerate((mix_bias, gate2_bias)):
                    for half in range(2):
                        sp.dma_start(dst[half:half + 1, :], bias_halves[0:1, i, half, :]).then_inc(bias_moved, 16)
                sp.wait_ge(bias_moved, 64)

            @block.scalar
            def _(act):
                act.wait_ge(prep, 28)
                act.activation(mix_hi[:], mix_f[:], ACT.Copy, scale=G_SCALE / 8.0 ** 0.5).then_inc(prep_hi, 1)
                act.activation(gate2_hi[:], gate2_f[:], ACT.Copy, scale=G_SCALE).then_inc(prep_hi, 1)

            @block.vector
            def _(dve):
                steps = [0]

                def done(*instructions):
                    for ins in instructions:
                        ins.then_inc(prep, 1)
                        steps[0] += 1
                    dve.wait_ge(prep, steps[0])

                for q in range(4):
                    dve.wait_ge(weights_in, 16 * (8 + 8 * (q + 1)))
                    part = mix_f[:, :, q * P:(q + 1) * P]
                    done(dve.tensor_tensor(part, factor[:, 0, :, :], factor[:, 1, :, :], ALU.add))
                    for r in range(2, 8):
                        done(dve.tensor_tensor(part, part, factor[:, r, :, :], ALU.add))
                dve.memset(ones_h[:], 1.0).then_inc(ones_set, 1)
                dve.wait_ge(prep_hi, 2)
                done(dve.scalar_tensor_tensor(out=mix_lo[:], in0=mix_f[:], scalar=G_SCALE / 8.0 ** 0.5,
                                              in1=mix_hi[:], op0=ALU.mult, op1=ALU.subtract),
                     dve.scalar_tensor_tensor(out=gate2_lo[:], in0=gate2_f[:], scalar=G_SCALE, in1=gate2_hi[:],
                                              op0=ALU.mult, op1=ALU.subtract))
                for i in range(2):
                    row = row_scratch[0:1, i, :]
                    done(dve.tensor_scalar(bias_halves[0:1, i, 0, :], row, G_SCALE, None, ALU.mult))
                    done(dve.scalar_tensor_tensor(out=bias_halves[0:1, i, 1, :], in0=row, scalar=G_SCALE,
                                                  in1=bias_halves[0:1, i, 0, :], op0=ALU.mult, op1=ALU.subtract))
                dve.sem_inc(halves_done, 1)
                done(dve.tensor_scalar(mask_rows[:], mask_words[:].bitcast(U8), MASKED, None, ALU.mult),
                     dve.tensor_scalar(mask_keys[:], keys_words[:].bitcast(U8), MASKED, None, ALU.mult))

        with ExitStack() as scope, nc.Block() as block:
            def sbl(name, shape, dt=F32):
                return scope.enter_context(nc.sbuf_tensor(name, shape, dt))
            tern_f = [sbl(f"tern_f{i}", [P, 8, D]) for i in range(2)]
            tern_b = sbl("tern_b", [P, 8, D], BF16)
            abs_sum = sbl("abs_sum", [P, 2])
            pA = psum_banks(scope, "prepA", 1)[0]
            pB = psum_banks(scope, "prepB", 4, BF16)

            @block.sync
            def _(sp):
                sp.dma_start(tern_f[0][:], L3_ffn_w_up.rearrange("(o p) i -> p o i", p=P)).then_inc(tern_in, 16)
                sp.dma_start(tern_f[1][:].rearrange("p (o j) i -> p o (j i)", o=4),
                             L3_ffn_w_down.rearrange("(o p) i -> p o i", p=P)).then_inc(tern_in, 16)

            @block.vector
            def _(dve):
                steps = [0]

                def done(*instructions):
                    for ins in instructions:
                        ins.then_inc(prep_tern, 1)
                        steps[0] += 1
                    dve.wait_ge(prep_tern, steps[0])

                for i in range(2):
                    dve.wait_ge(tern_in, 32)
                    flat = tern_f[i][:].rearrange("p o i -> p (o i)")
                    dve.tensor_reduce(abs_sum[:, i:i + 1], flat, AX.X, ALU.add, apply_absolute_value=True)\
                        .then_inc(abs_done, 1)
                    dve.wait_ge(total_ready, i + 1)
                    mean = tern[:, 2 * i + 1:2 * i + 2]
                    done(dve.tensor_scalar(mean, pA[:, i:i + 1], 1.0 / (IUP * D), 1e-5, ALU.mult, ALU.max))
                    done(dve.reciprocal(tern[:, 2 * i:2 * i + 1], mean))
                    done(dve.tensor_scalar(flat, flat, tern[:, 2 * i:2 * i + 1], 1.0, ALU.mult, ALU.min))
                    done(dve.tensor_scalar(flat, flat, -1.0, MAGIC, ALU.max, ALU.add))
                    dve.tensor_scalar(tern_b[:].rearrange("p o i -> p (o i)"), flat, MAGIC, None, ALU.subtract)\
                        .then_inc(rounded, 1)
                    for k in range(8):
                        dve.wait_ge(turned, 8 * i + k + 1)
                        dst = (up_t[:, :, k * P:(k + 1) * P], dn_t[:, k, :].rearrange("p (c o) -> p c o", c=4))[i]
                        dve.tensor_copy(dst, pB[k % 4][:, 0:D].rearrange("p (c o) -> p c o", c=4))\
                            .then_inc(turn_copied, 1)

            @block.tensor
            def _(pe):
                for i in range(2):
                    pe.wait_ge(abs_done, i + 1)
                    pe.matmul(pA[:, i:i + 1], ones[:], abs_sum[:, i:i + 1], start=True, stop=True)\
                        .then_inc(total_ready, 1)
                    pe.wait_ge(rounded, i + 1)
                    for k in range(8):
                        if 8 * i + k >= 4:
                            pe.wait_ge(turn_copied, 8 * i + k - 3)
                        for c in range(4):
                            if i == 0:
                                src = tern_b[:, k, c::KC]
                            else:
                                src = tern_b[:].rearrange("p (o j) i -> p o (j i)", o=4)[:, c, k::8]
                            m = pe.transpose(pB[k % 4][:, c * P:(c + 1) * P], src, ident_b[:])
                        m.then_inc(turned, 1)

        def transposed_split(pe, source, banks, ready):
            for c in range(KC):
                for t in range(TPB):
                    m = pe.transpose(banks[c][:, t * P:(t + 1) * P], source[:, t, c::KC], ident[:])
                m.then_inc(ready, 1)

        def dense(pe, out, t, a_hi, a_lo, w_hi, w_lo, bias):
            tok = slice(t * P, (t + 1) * P)
            for c in range(KC):
                split_matmul(pe, out, a_hi[:, c, tok], a_lo[:, c, tok], w_hi[:, c, :], w_lo[:, c, :], c == 0, False)
            return pe.matmul(out, ones_h[:], bias[:], start=False, stop=True)

        learned_copied = sem("learned_copied")
        learned_turned = sem("learned_turned")
        l1_scale_done = sem("l1_scale_done")
        l1_half = sem("l1_half")
        x3_done = sem("x3_done")
        n3_done = sem("n3_done")
        n3T_ready = sem("n3T_ready")
        n3T_hi_done = sem("n3T_hi_done")
        n3T_lo_done = sem("n3T_lo_done")
        mixed_ready = sem("mixed_ready")
        x4_done = sem("x4_done")
        n4_done = sem("n4_done")
        scores2_ready = sem("scores2_ready")
        scores2_step = sem("scores2_step")
        max2_done = sem("max2_done")
        negmax2_done = sem("negmax2_done")
        exp2_done = sem("exp2_done")
        recip2_done = sem("recip2_done")
        x5_done = sem("x5_done")

        with ExitStack() as scope:
            def sbl(name, shape, dt=F32):
                return scope.enter_context(nc.sbuf_tensor(name, shape, dt))
            l1_in = Norm("l1_in", sbl, sem, 1e-5)
            l1_mid = Norm("l1_mid", sbl, sem, 1e-5)
            l2_in = Norm("l2_in", sbl, sem, 1e-5)
            xw = sbl("xw", [P, TPB, D])
            lw = sbl("lw", [P, TPB, S])
            nrm = sbl("nrm", [P, TPB, D])
            nT_hi = sbl("nT_hi", [P, KC, S], F16)
            nT_lo = sbl("nT_lo", [P, KC, S], F16)
            mul1 = sbl("mul1", [P, TPB])
            add1 = sbl("add1", [P, TPB])
            max2 = sbl("max2", [P, TPB])
            negmax2 = sbl("negmax2", [P, TPB])
            sum2 = sbl("sum2", [P, TPB])
            recip2 = sbl("recip2", [P, TPB])
            live2 = sbl("live2", [P, TPB])
            pT = psum_banks(scope, "tail1T", 4)
            pG = psum_banks(scope, "tail1G", 4)
            with nc.Fori(0, B) as b, nc.Block() as block:
                @block.tensor
                def _(pe):
                    pe.wait_ge(learned_copied, TPB * b + TPB)
                    for t in range(TPB):
                        for j in range(TPB):
                            m = pe.transpose(pG[t][:, j * P:(j + 1) * P], lw[:, j, t * P:(t + 1) * P], ident[:])
                        m.then_inc(learned_turned, 1)
                    pe.wait_ge(n3_done, TPB * b + TPB)
                    transposed_split(pe, nrm, pT, n3T_ready)
                    pe.wait_ge(n3T_lo_done, KC * b + KC)
                    for t in range(TPB):
                        dense(pe, pG[t][:], t, nT_hi, nT_lo, mix_hi, mix_lo, mix_bias).then_inc(mixed_ready, 1)
                    for t in range(TPB):
                        rows, cols = bass.ds(b * S + t * P, P), bass.ds(b * S, S)
                        split_matmul(pe, pT[t][:], proj_hi[2][:, rows], proj_lo[2][:, rows], proj_hi[3][:, cols],
                                     proj_lo[3][:, cols], True, True).then_inc(scores2_ready, 1)

                @block.gpsimd
                def _(pool):
                    for norm in (l1_in, l1_mid, l2_in):
                        norm.on_gpsimd(pool, minus_half, b)

                @block.scalar
                def _(act):
                    for t in range(TPB):
                        act.activation(lw[:, t, :], tile_of(learned, b * TPB + t), ACT.Copy).then_inc(learned_copied, 1)
                    for c in range(KC):
                        act.wait_ge(n3T_ready, KC * b + c + 1)
                        act.activation(nT_hi[:, c, :], pT[c][:], ACT.Copy).then_inc(n3T_hi_done, 1)
                    act.wait_ge(negmax2_done, b + 1)
                    for t in range(TPB):
                        act.activation(lw[:, t, :], lw[:, t, :], ACT.Exp, bias=negmax2[:, t:t + 1],
                                       accum_out=sum2[:, t:t + 1]).then_inc(exp2_done, 1)

                @block.vector
                def _(dve):
                    l1_in.on_vector(dve, lambda t: tile_of(xres, b * TPB + t), b, None)
                    dve.tensor_scalar(mul1[:], l1_in.rstd[:], gam[:, 3:4], 1.0, ALU.mult, ALU.add).then_inc(l1_scale_done, 1)
                    dve.tensor_scalar(add1[:], l1_in.shift[:], gam[:, 3:4], None, ALU.mult).then_inc(l1_scale_done, 1)
                    dve.wait_ge(l1_scale_done, 2 * b + 2)
                    for t in range(TPB):
                        dve.wait_ge(learned_copied, TPB * b + t + 1)
                        dve.scalar_tensor_tensor(out=xw[:, t, :], in0=tile_of(xres, b * TPB + t), scalar=mul1[:, t:t + 1],
                                                 in1=lw[:, t, :], op0=ALU.mult, op1=ALU.add).then_inc(l1_half, 1)
                    dve.wait_ge(l1_half, TPB * b + TPB)
                    for t in range(TPB):
                        dve.wait_ge(learned_turned, TPB * b + t + 1)
                        dve.scalar_tensor_tensor(out=xw[:, t, :], in0=xw[:, t, :], scalar=add1[:, t:t + 1],
                                                 in1=pG[t][:], op0=ALU.add, op1=ALU.add).then_inc(x3_done, 1)
                    l1_mid.on_vector(dve, lambda t: xw[:, t, :], b, (x3_done, TPB * b + TPB))
                    for t in range(TPB):
                        dve.tensor_scalar(nrm[:, t, :], xw[:, t, :], l1_mid.rstd[:, t:t + 1],
                                          l1_mid.shift[:, t:t + 1], ALU.mult, ALU.add).then_inc(n3_done, 1)
                    for c in range(KC):
                        dve.wait_ge(n3T_hi_done, KC * b + c + 1)
                        dve.tensor_tensor(nT_lo[:, c, :], pT[c][:], nT_hi[:, c, :], ALU.subtract).then_inc(n3T_lo_done, 1)
                    for t in range(TPB):
                        dve.wait_ge(mixed_ready, TPB * b + t + 1)
                        dve.scalar_tensor_tensor(out=xw[:, t, :], in0=pG[t][:], scalar=1.0 / G_SCALE,
                                                 in1=xw[:, t, :], op0=ALU.mult, op1=ALU.add).then_inc(x4_done, 1)
                    l2_in.on_vector(dve, lambda t: xw[:, t, :], b, (x4_done, TPB * b + TPB))
                    for t in range(TPB):
                        dve.tensor_scalar(nrm[:, t, :], xw[:, t, :], l2_in.rstd[:, t:t + 1],
                                          l2_in.shift[:, t:t + 1], ALU.mult, ALU.add).then_inc(n4_done, 1)
                    dve.wait_ge(n4_done, TPB * b + TPB)
                    for t in range(TPB):
                        dve.wait_ge(scores2_ready, TPB * b + t + 1)
                        dve.scalar_tensor_tensor(out=lw[:, t, :], in0=pT[t][:], scalar=C ** -0.5, in1=nrm[:, t, :],
                                                 op0=ALU.mult, op1=ALU.mult).then_inc(scores2_step, 1)
                    dve.wait_ge(scores2_step, 2 * TPB * b + TPB)
                    for t in range(TPB):
                        dve.tensor_tensor(lw[:, t, :], lw[:, t, :], tile_of(mask_keys, b), ALU.add).then_inc(scores2_step, 1)
                    hold(dve, scores2_step, 2 * TPB * b + 2 * TPB)
                    for t in range(TPB):
                        dve.tensor_tensor_reduce(lw[:, t, :], lw[:, t, :], mask_rows[:, t, :], 1.0, NEG, ALU.add,
                                                 ALU.max, max2[:, t:t + 1]).then_inc(max2_done, 1)
                    dve.wait_ge(max2_done, TPB * b + TPB)
                    dve.tensor_scalar(negmax2[:], max2[:], -1.0, None, ALU.mult).then_inc(negmax2_done, 1)
                    dve.tensor_scalar(live2[:], max2[:], 0.5 * MASKED, None, ALU.is_ge).then_inc(recip2_done, 1)
                    dve.wait_ge(recip2_done, 4 * b + 1)
                    dve.wait_ge(exp2_done, TPB * b + TPB)
                    dve.tensor_tensor(sum2[:], sum2[:], live2[:], ALU.mult).then_inc(recip2_done, 1)
                    dve.wait_ge(recip2_done, 4 * b + 2)
                    dve.reciprocal(recip2[:], sum2[:]).then_inc(recip2_done, 1)
                    dve.wait_ge(recip2_done, 4 * b + 3)
                    dve.tensor_tensor(recip2[:], recip2[:], live2[:], ALU.mult).then_inc(recip2_done, 1)
                    dve.wait_ge(recip2_done, 4 * b + 4)
                    for t in range(TPB):
                        dve.scalar_tensor_tensor(out=tile_of(xres, b * TPB + t), in0=lw[:, t, :],
                                                 scalar=recip2[:, t:t + 1], in1=xw[:, t, :], op0=ALU.mult,
                                                 op1=ALU.add).then_inc(x5_done, 1)
        mid.close()
        middle.close()
        bc_rows = sb("bc_rows", [P, B, D])
        out_gamma = sb("out_gamma", [P, D])
        out_beta = sb("out_beta", [P, D])
        values_hi = sb("values_hi", [P, NT, KVH, DH + 1], F16)
        values_lo = sb("values_lo", [P, NT, KVH, DH + 1], F16)

        th_in = sem("th_in")
        last_in = sem("last_in")
        values_done = sem("values_done")
        th = sem("th")
        th_rstd = sem("th_rstd")
        last_ready = sem("last_ready")
        last_turned = sem("last_turned")
        agg_ready = sem("agg_ready")
        thn = sem("thn")
        sum_ready = sem("sum_ready")
        th_rstd_step = sem("th_rstd_step")
        d1_ready = sem("d1_ready")
        gelu_in = sem("gelu_in")
        gelu_done = sem("gelu_done")
        d2_ready = sem("d2_ready")
        bc_ready = sem("bc_ready")
        bc_done = sem("bc_done")
        HC = HID // P
        with ExitStack() as scope, nc.Block() as block:
            def sbl(name, shape, dt=F32):
                return scope.enter_context(nc.sbuf_tensor(name, shape, dt))
            d1_w = sbl("d1_w", [P, KC, HID])
            d2_w = sbl("d2_w", [P, HC, D])
            agg_w = sbl("agg_w", [P, KC, D])
            bc_w = sbl("bc_w", [P, KC, D])
            bc_b = sbl("bc_b", [P, D])
            d1_b = sbl("d1_b", [P, HC])
            vecs = sbl("vecs", [P, 4, KC])
            last = sbl("last", [B, D])
            in_rows = sbl("in_rows", [B, 2, D])
            last_stats = sbl("last_stats", [B, 6])
            last_mv = sbl("last_mv", [B, 2])
            last_ve = sbl("last_ve", [B, 1])
            last_rstd = sbl("last_rstd", [B, 1])
            lastT = sbl("lastT", [P, KC, B])
            thought = sbl("thought", [P, KC, B])
            part = sbl("part", [P, B])
            mean = sbl("mean", [P, B])
            centred = sbl("centred", [P, KC, B])
            square = sbl("square", [P, KC, B])
            ve = sbl("ve", [P, B])
            rstd = sbl("rstd", [P, B])
            tn = sbl("tn", [P, KC, B])
            hid_f = sbl("hid_f", [P, HC, B])
            hid = sbl("hid", [P, HC, B])
            th_rep = sbl("th_rep", [P, KC, B, P])
            pL = psum_banks(scope, "thL", 1)[0]
            pA = psum_banks(scope, "thA", 1)[0]
            pS = psum_banks(scope, "thS", 1)[0]
            pH = psum_banks(scope, "thH", 1)[0]
            pD = psum_banks(scope, "thD", 1)[0]
            pB = psum_banks(scope, "thB", 2)

            @block.sync
            def _(sp):
                for b in range(B):
                    sp.dma_start(last[b:b + 1, :], xres[P - 1:P, TPB * b + TPB - 1, :]).then_inc(last_in, 16)
                for i, v in enumerate((L2_ffn_in_gamma, L2_ffn_in_beta)):
                    sp.dma_start(in_rows[:, i, :], v.rearrange("(a d) -> a d", a=1).to_broadcast([B, D])).then_inc(last_in, 16)
                sp.dma_start(agg_w[:], L2_ffn_agg_w.rearrange("(p c) e -> p c e", c=KC)).then_inc(last_in, 16)
                for i, v in enumerate((L2_ffn_agg_b, L2_ffn_pn_gamma, L2_ffn_pn_beta, L2_ffn_d2_b)):
                    sp.dma_start(vecs[:, i, :], v.rearrange("(p c) -> p c", c=KC)).then_inc(last_in, 16)
                sp.dma_start(d1_b[:], L2_ffn_d1_b.rearrange("(p m) -> p m", m=HC)).then_inc(last_in, 16)
                sp.dma_start(d1_w[:], L2_ffn_d1_w.rearrange("(p c) e -> p c e", c=KC)).then_inc(th_in, 16)
                sp.dma_start(d2_w[:], L2_ffn_d2_w.rearrange("(p m) e -> p m e", m=HC)).then_inc(th_in, 16)
                sp.dma_start(bc_w[:], L2_ffn_bc_w.rearrange("(p c) e -> p c e", c=KC)).then_inc(th_in, 16)
                for dst, v in ((bc_b, L2_ffn_bc_b), (out_gamma, L2_ffn_out_gamma), (out_beta, L2_ffn_out_beta)):
                    sp.dma_start(dst[:], v.rearrange("(a d) -> a d", a=1).to_broadcast([P, D])).then_inc(th_in, 16)
                sp.wait_ge(th_in, 96)

            @block.gpsimd
            def _(pool):
                heads = ctxs[:].rearrange("p t (g d) -> p t g d", d=DH)
                pool.memset(values_hi[:, :, :, DH:DH + 1], 1.0).then_inc(values_done, 1)
                pool.memset(values_lo[:, :, :, DH:DH + 1], 0.0).then_inc(values_done, 1)
                pool.tensor_copy(values_hi[:, :, :, 0:DH], heads).then_inc(values_done, 1)
                pool.wait_ge(values_done, 3)
                pool.tensor_tensor(values_lo[:, :, :, 0:DH], heads, values_hi[:, :, :, 0:DH], ALU.subtract)\
                    .then_inc(values_done, 1)
                for i in range(2):
                    pool.wait_ge(th, 4 * i + 3)
                    pool.tensor_tensor(last_rstd[:], last_ve[:], minus_half[0:B, 0:1], ALU.pow).then_inc(th_rstd, 1)
                with pool.Fori(0, K_STEPS) as k:
                    pool.wait_ge(thn, 11 * k + 6)
                    pool.tensor_tensor(rstd[:], ve[:], minus_half[:, 0:B], ALU.pow).then_inc(th_rstd_step, 1)

            @block.tensor
            def _(pe):
                pe.wait_ge(last_ready, 1)
                for c in range(KC):
                    m = pe.transpose(pL[:, c * B:(c + 1) * B], last[:, c::KC], ident[0:B, 0:B])
                m.then_inc(last_turned, 1)
                pe.wait_ge(th, 11)
                for o in range(KC):
                    for c in range(KC):
                        m = pe.matmul(pA[:, o * B:(o + 1) * B], agg_w[:, c, o::KC], lastT[:, c, :],
                                      start=c == 0, stop=c == KC - 1)
                m.then_inc(agg_ready, 1)
                pe.wait_ge(th_in, 96)
                with pe.Fori(0, K_STEPS) as k:
                    pe.wait_ge(thn, 11 * k + 1)
                    pe.matmul(pS[:, 0:B], ones[:], part[:], start=True, stop=True).then_inc(sum_ready, 1)
                    pe.wait_ge(thn, 11 * k + 5)
                    pe.matmul(pS[:, B:2 * B], ones[:], part[:], start=True, stop=True).then_inc(sum_ready, 1)
                    pe.wait_ge(thn, 11 * k + 9)
                    for m in range(HC):
                        for c in range(KC):
                            mm = pe.matmul(pH[:, m * B:(m + 1) * B], d1_w[:, c, m::HC], tn[:, c, :],
                                           start=c == 0, stop=c == KC - 1)
                    mm.then_inc(d1_ready, 1)
                    pe.wait_ge(gelu_done, k + 1)
                    for o in range(KC):
                        for m in range(HC):
                            mm = pe.matmul(pD[:, o * B:(o + 1) * B], d2_w[:, m, o::KC], hid[:, m, :],
                                           start=m == 0, stop=m == HC - 1)
                    mm.then_inc(d2_ready, 1)
                pe.wait_ge(bc_ready, 1)
                for b in range(B):
                    if b >= 2:
                        pe.wait_ge(bc_done, b - 1)
                    for c in range(KC):
                        mm = pe.matmul(pB[b % 2][:], th_rep[:, c, b, :], bc_w[:, c, :], start=c == 0, stop=c == KC - 1)
                    mm.then_inc(bc_ready, 1)

            @block.scalar
            def _(act):
                with act.Fori(0, K_STEPS) as k:
                    act.wait_ge(gelu_in, k + 1)
                    act.activation(hid[:], hid_f[:], ACT.Gelu).then_inc(gelu_done, 1)

            @block.vector
            def _(dve):
                steps = [0]

                def done(*instructions):
                    for ins in instructions:
                        ins.then_inc(th, 1)
                        steps[0] += 1
                    dve.wait_ge(th, steps[0])

                dve.wait_ge(last_in, 16 * 12)
                for i, eps in enumerate((1e-5, 1e-6)):
                    done(dve.bn_stats(last_stats[:], last[:]))
                    done(dve.bn_aggr(last_mv[:], last_stats[:]))
                    done(dve.tensor_scalar(last_ve[:], last_mv[:, 1:2], eps, None, ALU.add))
                    dve.wait_ge(th_rstd, i + 1)
                    done(dve.tensor_scalar(last[:], last[:], last_mv[:, 0:1], last_rstd[:, 0:1], ALU.subtract, ALU.mult))
                done(dve.tensor_tensor(last[:], last[:], in_rows[:, 0, :], ALU.mult))
                done(dve.tensor_tensor(last[:], last[:], in_rows[:, 1, :], ALU.add))
                dve.sem_inc(last_ready, 1)
                dve.wait_ge(last_turned, 1)
                done(dve.tensor_copy(lastT[:].rearrange("p c b -> p (c b)"), pL[:, 0:KC * B]))
                dve.wait_ge(agg_ready, 1)

                def vec(i):
                    return vecs[:, i, :].unsqueeze(2).to_broadcast([P, KC, B])

                def per_batch(v):
                    return v[:].unsqueeze(1).to_broadcast([P, KC, B])

                done(dve.tensor_tensor(thought[:], pA[:, 0:KC * B].rearrange("p (c b) -> p c b", b=B), vec(0), ALU.add))
                with dve.Fori(0, K_STEPS) as k:
                    n = [0]

                    def step(ins):
                        ins.then_inc(thn, 1)
                        n[0] += 1
                        hold(dve, thn, 11 * k + n[0])

                    step(dve.tensor_reduce(part[:], thought[:].rearrange("p c b -> p b c"), AX.X, ALU.add))
                    dve.wait_ge(sum_ready, 2 * k + 1)
                    step(dve.tensor_scalar(mean[:], pS[:, 0:B], 1.0 / D, None, ALU.mult))
                    step(dve.tensor_tensor(centred[:], thought[:], per_batch(mean), ALU.subtract))
                    step(dve.tensor_tensor(square[:], centred[:], centred[:], ALU.mult))
                    step(dve.tensor_reduce(part[:], square[:].rearrange("p c b -> p b c"), AX.X, ALU.add))
                    dve.wait_ge(sum_ready, 2 * k + 2)
                    step(dve.tensor_scalar(ve[:], pS[:, B:2 * B], 1.0 / D, 1e-6, ALU.mult, ALU.add))
                    dve.wait_ge(th_rstd_step, k + 1)
                    step(dve.tensor_tensor(tn[:], centred[:], per_batch(rstd), ALU.mult))
                    step(dve.tensor_tensor(tn[:], tn[:], vec(1), ALU.mult))
                    step(dve.tensor_tensor(tn[:], tn[:], vec(2), ALU.add))
                    dve.wait_ge(d1_ready, k + 1)
                    dve.tensor_tensor(hid_f[:], pH[:, 0:HC * B].rearrange("p (m b) -> p m b", b=B),
                                      d1_b[:].unsqueeze(2).to_broadcast([P, HC, B]), ALU.add).then_inc(gelu_in, 1)
                    dve.wait_ge(d2_ready, k + 1)
                    step(dve.tensor_tensor(thought[:], thought[:], pD[:, 0:KC * B].rearrange("p (c b) -> p c b", b=B),
                                           ALU.add))
                    step(dve.tensor_tensor(thought[:], thought[:], vec(3), ALU.add))
                dve.tensor_copy(th_rep[:], thought[:].unsqueeze(3).to_broadcast([P, KC, B, P])).then_inc(bc_ready, 1)
                for b in range(B):
                    dve.wait_ge(bc_ready, b + 2)
                    dve.tensor_tensor(bc_rows[:, b, :], pB[b % 2][:], bc_b[:], ALU.add).then_inc(bc_done, 1)

        PAIR = QH // 2
        SLOT = 64
        ROWS = 3 * DH
        x5_copied = sem("x5_copied")
        n5_done = sem("n5_done")
        n5T_ready = sem("n5T_ready")
        n5T_hi_done = sem("n5T_hi_done")
        n5T_lo_done = sem("n5T_lo_done")
        gate_ready = sem("gate_ready")
        gate_done = sem("gate_done")
        gated = sem("gated")
        x6_step = sem("x6_step")
        n6_done = sem("n6_done")
        q_hi_done = sem("q_hi_done")
        q_lo_done = sem("q_lo_done")
        q_pad_done = sem("q_pad_done")
        k_hi_done = sem("k_hi_done")
        k_lo_done = sem("k_lo_done")
        kT_ready = sem("kT_ready")
        kT_done = sem("kT_done")
        qT_ready = sem("qT_ready")
        qT_done = sem("qT_done")
        qT_odd_done = sem("qT_odd_done")
        s_ready = sem("s_ready")
        max_done = sem("max_done")
        negmax_done = sem("negmax_done")
        negmaxT_ready = sem("negmaxT_ready")
        negmaxT_done = sem("negmaxT_done")
        negmax_moved = sem("negmax_moved")
        sT_ready = sem("sT_ready")
        exp_done = sem("exp_done")
        probs_hi0_done = sem("probs_hi0_done")
        probs_hi1_done = sem("probs_hi1_done")
        probs_lo_done = sem("probs_lo_done")
        pv_ready = sem("pv_ready")
        recip_done = sem("recip_done")
        weighed_done = sem("weighed_done")
        x7_done = sem("x7_done")
        n7_done = sem("n7_done")
        amax_done = sem("amax_done")
        scale_step = sem("scale_step")
        quant_step = sem("quant_step")
        q7_done = sem("q7_done")
        q7T_ready = sem("q7T_ready")
        q7T_done = sem("q7T_done")
        hid_ready = sem("hid_ready")
        relu_done = sem("relu_done")
        hmax_done = sem("hmax_done")
        hscale_step = sem("hscale_step")
        hsq_done = sem("hsq_done")
        hquant_step = sem("hquant_step")
        hq_done = sem("hq_done")
        hqT_ready = sem("hqT_ready")
        hqT_done = sem("hqT_done")
        y_ready = sem("y_ready")
        x8_done = sem("x8_done")
        stored = sem("stored")
        k_ones_done = sem("k_ones_done")

        with ExitStack() as scope:
            def sbl(name, shape, dt=F32, scope=scope):
                return scope.enter_context(nc.sbuf_tensor(name, shape, dt))
            l2_ffn = Norm("l2_ffn", sbl, sem, 1e-5)
            l2_out = Norm("l2_out", sbl, sem, 1e-6)
            l3_in = Norm("l3_in", sbl, sem, 1e-5)
            l3_mid = Norm("l3_mid", sbl, sem, 1e-5)
            xw = sbl("xw2", [P, TPB, D])
            nrm = sbl("nrm2", [P, TPB, D])
            with nc.Fori(0, B) as b:
                attn = ExitStack()
                def sba(name, shape, dt=F32):
                    return attn.enter_context(nc.sbuf_tensor(name, shape, dt))
                q_rows = sba("q_rows", [P, TPB, QH, SLOT], F16)
                k_rows = sba("k_rows", [P, TPB, KVH, 2, SLOT], F16)
                qT = sba("qT", [P, PAIR, S], F16)
                kT = sba("kT", [P, KVH, S], F16)
                maxes = sba("maxes", [P, TPB, QH])
                negmax = sba("negmax", [P, TPB, QH], F16)
                negmaxT = sba("negmaxT", [QH, S], F16)

                with ExitStack() as inner, nc.Block() as block:
                    gate = inner.enter_context(nc.sbuf_tensor("gate", [P, TPB, D], F32))
                    n5T_hi = inner.enter_context(nc.sbuf_tensor("n5T_hi", [P, KC, S], F16))
                    n5T_lo = inner.enter_context(nc.sbuf_tensor("n5T_lo", [P, KC, S], F16))
                    pT = psum_banks(inner, "gateT", 4)
                    pG = psum_banks(inner, "gateG", 4)

                    @block.gpsimd
                    def _(pool):
                        l2_ffn.on_gpsimd(pool, minus_half, b)
                        l2_out.on_gpsimd(pool, minus_half, b)
                        l3_in.on_gpsimd(pool, minus_half, b)
                        pool.memset(q_rows[:, :, :, ROWS:SLOT], 0.0).then_inc(q_pad_done, 1)
                        pool.memset(k_rows[:, :, :, :, ROWS:SLOT], 0.0).then_inc(q_pad_done, 1)
                        for t in range(TPB):
                            src = ctxs[:, bass.ds(b * TPB + t, 1), :].rearrange("p a (g d) -> p (a g) d", d=DH)
                            for dup in range(2):
                                for i in range(2):
                                    pool.tensor_copy(k_rows[:, t, :, dup, i * DH:(i + 1) * DH], src).then_inc(k_hi_done, 1)
                        hold(pool, q_pad_done, 2 * b + 2)
                        pool.memset(k_rows[:, :, :, :, ROWS:ROWS + 1], 1.0).then_inc(k_ones_done, 1)
                        hold(pool, k_hi_done, 16 * b + 16)
                        for t in range(TPB):
                            src = ctxs[:, bass.ds(b * TPB + t, 1), :].rearrange("p a (g d) -> p (a g) d", d=DH)
                            for dup in range(2):
                                pool.tensor_tensor(k_rows[:, t, :, dup, 2 * DH:ROWS], src, k_rows[:, t, :, dup, 0:DH],
                                                   ALU.subtract).then_inc(k_lo_done, 1)

                    @block.tensor
                    def _(pe):
                        pe.wait_ge(n5_done, TPB * b + TPB)
                        transposed_split(pe, nrm, pT, n5T_ready)
                        pe.wait_ge(n5T_lo_done, KC * b + KC)
                        for t in range(TPB):
                            dense(pe, pG[t][:], t, n5T_hi, n5T_lo, gate2_hi, gate2_lo, gate2_bias)\
                                .then_inc(gate_ready, 1)
                        pe.wait_ge(k_lo_done, 8 * b + 8)
                        pe.wait_ge(k_ones_done, b + 1)
                        for g in range(KVH):
                            bank = pT[g // 2][:].bitcast(F16)
                            for t in range(TPB):
                                at = (g % 2) * S + t * P
                                m = pe.transpose(bank[:, at:at + P], k_rows[:, t, g, :, :].rearrange("p e r -> p (e r)"),
                                                 ident_h[:])
                            if g % 2:
                                m.then_inc(kT_ready, 1)

                    @block.scalar
                    def _(act):
                        for t in range(TPB):
                            act.activation(xw[:, t, :], tile_of(xres, b * TPB + t), ACT.Copy).then_inc(x5_copied, 1)
                        for c in range(KC):
                            act.wait_ge(n5T_ready, KC * b + c + 1)
                            act.activation(n5T_hi[:, c, :], pT[c][:], ACT.Copy).then_inc(n5T_hi_done, 1)
                        for t in range(TPB):
                            act.wait_ge(gate_ready, TPB * b + t + 1)
                            act.activation(gate[:, t, :], pG[t][:], ACT.Sigmoid, scale=1.0 / G_SCALE).then_inc(gate_done, 1)
                        for i in range(KVH // 2):
                            act.wait_ge(kT_ready, KVH // 2 * b + i + 1)
                            act.activation(kT[:, 2 * i:2 * i + 2, :].rearrange("p g s -> p (g s)"),
                                           pT[i][:].bitcast(F16), ACT.Copy).then_inc(kT_done, 1)
                        for t in range(TPB):
                            act.wait_ge(n6_done, TPB * b + t + 1)
                            src = nrm[:, t, :].rearrange("p (h d) -> p h d", d=DH)
                            act.activation(q_rows[:, t, :, 0:DH], src, ACT.Copy).then_inc(q_hi_done, 1)
                            act.activation(q_rows[:, t, :, 2 * DH:ROWS], src, ACT.Copy).then_inc(q_hi_done, 1)

                    @block.vector
                    def _(dve):
                        l2_ffn.on_vector(dve, lambda t: tile_of(xres, b * TPB + t), b, None)
                        for t in range(TPB):
                            dve.tensor_scalar(nrm[:, t, :], tile_of(xres, b * TPB + t), l2_ffn.rstd[:, t:t + 1],
                                              l2_ffn.shift[:, t:t + 1], ALU.mult, ALU.add).then_inc(n5_done, 1)
                        for c in range(KC):
                            dve.wait_ge(n5T_hi_done, KC * b + c + 1)
                            dve.tensor_tensor(n5T_lo[:, c, :], pT[c][:], n5T_hi[:, c, :], ALU.subtract)\
                                .then_inc(n5T_lo_done, 1)
                        for t in range(TPB):
                            dve.wait_ge(gate_done, TPB * b + t + 1)
                            dve.tensor_tensor(gate[:, t, :], gate[:, t, :], tile_of(bc_rows, b), ALU.mult).then_inc(gated, 1)
                        dve.wait_ge(gated, 2 * TPB * b + TPB)
                        dve.tensor_tensor(gate[:], gate[:], nrm[:], ALU.add).then_inc(x6_step, 1)
                        l2_out.on_vector(dve, lambda t: gate[:, t, :], b, (x6_step, 4 * b + 1))
                        for t in range(TPB):
                            dve.tensor_scalar(gate[:, t, :], gate[:, t, :], l2_out.rstd[:, t:t + 1],
                                              l2_out.shift[:, t:t + 1], ALU.mult, ALU.add).then_inc(gated, 1)
                        hold(dve, gated, 2 * TPB * b + 2 * TPB)
                        gamma = out_gamma[:].unsqueeze(1).to_broadcast([P, TPB, D])
                        beta = out_beta[:].unsqueeze(1).to_broadcast([P, TPB, D])
                        dve.tensor_tensor(gate[:], gate[:], gamma, ALU.mult).then_inc(x6_step, 1)
                        dve.wait_ge(x5_copied, TPB * b + TPB)
                        dve.tensor_tensor(xw[:], xw[:], beta, ALU.add).then_inc(x6_step, 1)
                        dve.wait_ge(x6_step, 4 * b + 3)
                        dve.tensor_tensor(xw[:], xw[:], gate[:], ALU.add).then_inc(x6_step, 1)
                        l3_in.on_vector(dve, lambda t: xw[:, t, :], b, (x6_step, 4 * b + 4))
                        for t in range(TPB):
                            dve.tensor_scalar(nrm[:, t, :], xw[:, t, :], l3_in.rstd[:, t:t + 1],
                                              l3_in.shift[:, t:t + 1], ALU.mult, ALU.add).then_inc(n6_done, 1)
                        for t in range(TPB):
                            dve.wait_ge(q_hi_done, 2 * TPB * b + 2 * t + 1)
                            dve.tensor_tensor(q_rows[:, t, :, DH:2 * DH], nrm[:, t, :].rearrange("p (h d) -> p h d", d=DH),
                                              q_rows[:, t, :, 0:DH], ALU.subtract).then_inc(q_lo_done, 1)

                with ExitStack() as inner:
                    with nc.Block() as block:
                        pQ = psum_banks(inner, "qT", 8, F16)

                        @block.tensor
                        def _(pe):
                            for j in range(PAIR):
                                for t in range(TPB):
                                    at = (j % 2) * S + t * P
                                    m = pe.transpose(pQ[j // 2][:, at:at + P],
                                                     q_rows[:, t, 2 * j:2 * j + 2, :].rearrange("p e r -> p (e r)"),
                                                     ident_h[:])
                                if j % 2:
                                    m.then_inc(qT_ready, 1)

                        def copy_out(eng, i):
                            return (qT[:, 2 * i:2 * i + 2, :].rearrange("p j s -> p (j s)"), pQ[i][:])

                        @block.scalar
                        def _(act):
                            for i in range(0, 8, 2):
                                act.wait_ge(qT_ready, 8 * b + i + 1)
                                act.activation(*copy_out(act, i), ACT.Copy).then_inc(qT_done, 1)

                        @block.vector
                        def _(dve):
                            for i in range(1, 8, 2):
                                dve.wait_ge(qT_ready, 8 * b + i + 1)
                                dve.tensor_copy(*copy_out(dve, i)).then_inc(qT_odd_done, 1)

                def rows_of(head, n):
                    return slice(SLOT * (head % 2), SLOT * (head % 2) + n)

                with ExitStack() as inner, nc.Block() as block:
                    pS = [inner.enter_context(nc.psum_tensor(f"pS{i}", [P, TPB, S], F32)) for i in range(2)]

                    @block.tensor
                    def _(pe):
                        for h in range(QH):
                            if h >= 2:
                                pe.wait_ge(max_done, QH * b + h - 1)
                            r = rows_of(h, ROWS)
                            for t in range(TPB):
                                m = pe.matmul(pS[h % 2][:, t, :], qT[r, h // 2, t * P:(t + 1) * P],
                                              kT[r, h // 4, :], start=True, stop=True)
                            m.then_inc(s_ready, 1)
                        pe.wait_ge(negmax_done, b + 1)
                        for t in range(TPB):
                            m = pe.transpose(pS[0][:, 0, :].bitcast(F16)[0:QH, t * P:(t + 1) * P], negmax[:, t, :],
                                             ident_h[:])
                        m.then_inc(negmaxT_ready, 1)

                    @block.vector
                    def _(dve):
                        for h in range(QH):
                            dve.wait_ge(s_ready, QH * b + h + 1)
                            at = (h % 2) * PAIR + h // 2
                            dve.tensor_reduce(maxes[:, :, at:at + 1], pS[h % 2][:], AX.X, ALU.max).then_inc(max_done, 1)
                        dve.wait_ge(max_done, QH * b + QH)
                        dve.tensor_scalar(negmax[:], maxes[:], -1.0, None, ALU.mult).then_inc(negmax_done, 1)
                        dve.wait_ge(negmaxT_ready, b + 1)
                        dve.tensor_copy(negmaxT[:], pS[0][:, 0, :].bitcast(F16)[0:QH, 0:S]).then_inc(negmaxT_done, 1)

                    @block.sync
                    def _(sp):
                        for parity in range(2):
                            sp.wait_ge(negmaxT_done, b + 1)
                            row = SLOT * parity + ROWS
                            sp.dma_start(qT[row:row + 1, :, :], negmaxT[parity * PAIR:(parity + 1) * PAIR, :])\
                                .then_inc(negmax_moved, 16)

                with ExitStack() as inner, nc.Block() as block:
                    probs, probs_hi, probs_lo = [
                        [inner.enter_context(nc.sbuf_tensor(f"{name}{i}", [P, TPB, S], dt)) for i in range(2)]
                        for name, dt in (("probs", F32), ("probs_hi", F16), ("probs_lo", F16))]
                    recip = inner.enter_context(nc.sbuf_tensor("recip", [P, 16], F32))
                    weighed = inner.enter_context(nc.sbuf_tensor("weighed", [P, 16, DH], F32))
                    pX = [inner.enter_context(nc.psum_tensor(f"pX{i}", [P, 2, S], F32)) for i in range(3)]
                    pO = psum_banks(inner, "pO", 2)
                    W = DH + 1

                    @block.tensor
                    def _(pe):
                        pe.wait_ge(negmax_moved, 32 * b + 32)

                        def scores(h):
                            for half in range(2):
                                n = 2 * h + half
                                if n >= 3:
                                    pe.wait_ge(exp_done, 2 * QH * b + n - 2)
                                r = rows_of(h, ROWS + 1)
                                for i in range(2):
                                    kt = 2 * half + i
                                    m = pe.matmul(pX[n % 3][:, i, :], kT[r, h // 4, kt * P:(kt + 1) * P],
                                                  qT[r, h // 2, :], start=True, stop=True)
                                m.then_inc(sT_ready, 1)

                        def weigh(h):
                            pe.wait_ge(probs_lo_done, 2 * QH * b + 2 * h + 2)
                            if h % 4 == 0 and h >= 8:
                                pe.wait_ge(weighed_done, KVH * b + h // 4 - 1)
                            for qt in range(TPB):
                                at = ((h % 4) * TPB + qt) * W
                                for kt in range(TPB):
                                    v_hi, v_lo = [v[:, bass.ds(b * TPB + kt, 1), h // 4, :].rearrange("p a w -> p (a w)")
                                                  for v in (values_hi, values_lo)]
                                    q = slice(qt * P, (qt + 1) * P)
                                    m = split_matmul(pe, pO[h // 4 % 2][:, at:at + W], probs_hi[h % 2][:, kt, q],
                                                     probs_lo[h % 2][:, kt, q], v_hi, v_lo, kt == 0, kt == TPB - 1)
                            m.then_inc(pv_ready, 1)

                        for h in range(QH):
                            scores(h)
                            if h >= 1:
                                weigh(h - 1)
                        weigh(QH - 1)

                    @block.scalar
                    def _(act):
                        def high(h):
                            if h >= 2:
                                act.wait_ge(pv_ready, QH * b + h - 1)
                            act.wait_ge(exp_done, 2 * QH * b + 2 * h + 1)
                            act.activation(probs_hi[h % 2][:, 0:2, :], probs[h % 2][:, 0:2, :], ACT.Copy)\
                                .then_inc(probs_hi0_done, 1)

                        for h in range(QH):
                            for half in range(2):
                                n = 2 * h + half
                                if h >= 2:
                                    act.wait_ge(probs_lo_done, 2 * QH * b + n - 3)
                                act.wait_ge(sT_ready, 2 * QH * b + n + 1)
                                act.activation(probs[h % 2][:, 2 * half:2 * half + 2, :], pX[n % 3][:], ACT.Exp,
                                               scale=DH ** -0.5).then_inc(exp_done, 1)
                            high(h)

                    @block.vector
                    def _(dve):
                        def normalise(g):
                            dve.wait_ge(pv_ready, QH * b + 4 * g + 4)
                            o = pO[g % 2][:, 0:16 * W].rearrange("p (q w) -> p q w", w=W)
                            dve.reciprocal(recip[:].unsqueeze(2), o[:, :, DH:W]).then_inc(recip_done, 1)
                            if g >= 1:
                                dve.wait_ge(x7_done, KVH * b + g)
                            dve.wait_ge(recip_done, KVH * b + g + 1)
                            dve.tensor_tensor(weighed[:], o[:, :, 0:DH], recip[:].unsqueeze(2).to_broadcast([P, 16, DH]),
                                              ALU.mult).then_inc(weighed_done, 1)
                            dve.wait_ge(weighed_done, KVH * b + g + 1)
                            x = xw[:, :, g * 4 * DH:(g + 1) * 4 * DH].rearrange("p t (h d) -> p t h d", d=DH)
                            dve.tensor_tensor(x, x, weighed[:].rearrange("p (h t) d -> p t h d", t=TPB), ALU.add)\
                                .then_inc(x7_done, 1)

                        for h in range(QH):
                            if h >= 2:
                                dve.wait_ge(pv_ready, QH * b + h - 1)
                            dve.wait_ge(exp_done, 2 * QH * b + 2 * h + 2)
                            full, hi, lo = probs[h % 2], probs_hi[h % 2], probs_lo[h % 2]
                            dve.tensor_copy(hi[:, 2:4, :], full[:, 2:4, :]).then_inc(probs_hi1_done, 1)
                            dve.wait_ge(probs_hi0_done, QH * b + h + 1)
                            dve.tensor_tensor(lo[:, 0:2, :], full[:, 0:2, :], hi[:, 0:2, :], ALU.subtract)\
                                .then_inc(probs_lo_done, 1)
                            dve.wait_ge(probs_hi1_done, QH * b + h + 1)
                            dve.tensor_tensor(lo[:, 2:4, :], full[:, 2:4, :], hi[:, 2:4, :], ALU.subtract)\
                                .then_inc(probs_lo_done, 1)
                            if h % 4 == 1 and h >= 5:
                                normalise(h // 4 - 1)
                        normalise(KVH - 1)
                attn.close()

                with ExitStack() as inner, nc.Block() as block:
                    def sbf(name, shape, dt=F32):
                        return inner.enter_context(nc.sbuf_tensor(name, shape, dt))
                    q7 = sbf("q7", [P, TPB, D], BF16)
                    q7T = sbf("q7T", [P, KC, S], BF16)
                    hid = sbf("hidden", [P, TPB, IUP])
                    hq = sbf("hq", [P, TPB, IUP], BF16)
                    hqT = sbf("hqT", [P, IUP // P, S], BF16)
                    amax, scale7, deq7, hmax, hscale, hdeq = [sbf(n, [P, TPB]) for n in
                                                              ("amax", "scale7", "deq7", "hmax", "hscale", "hdeq")]
                    pT = psum_banks(inner, "ffnT", 4)
                    pU = psum_banks(inner, "ffnU", 4)

                    @block.gpsimd
                    def _(pool):
                        l3_mid.on_gpsimd(pool, minus_half, b)

                    @block.tensor
                    def _(pe):
                        pe.wait_ge(q7_done, b + 1)
                        for c in range(KC):
                            for t in range(TPB):
                                m = pe.transpose(pT[c][:].bitcast(BF16)[:, t * P:(t + 1) * P], q7[:, t, c::KC], ident_b[:])
                            m.then_inc(q7T_ready, 1)
                        pe.wait_ge(q7T_done, KC * b + KC)
                        for t in range(TPB):
                            for half in range(2):
                                n = 2 * t + half
                                if n >= 4:
                                    pe.wait_ge(relu_done, 8 * b + n - 3)
                                for c in range(KC):
                                    m = pe.matmul(pU[n % 4][:], q7T[:, c, t * P:(t + 1) * P],
                                                  up_t[:, c, half * D:(half + 1) * D], start=c == 0, stop=c == KC - 1)
                                m.then_inc(hid_ready, 1)
                        pe.wait_ge(hq_done, TPB * b + TPB)
                        for k in range(8):
                            if k >= 4:
                                pe.wait_ge(hqT_done, 8 * b + k - 3)
                            for t in range(TPB):
                                m = pe.transpose(pT[k % 4][:].bitcast(BF16)[:, t * P:(t + 1) * P], hq[:, t, k::8], ident_b[:])
                            m.then_inc(hqT_ready, 1)
                        pe.wait_ge(hqT_done, 8 * b + 8)
                        for t in range(TPB):
                            for k in range(8):
                                m = pe.matmul(pU[t][:], hqT[:, k, t * P:(t + 1) * P], dn_t[:, k, :], start=k == 0, stop=k == 7)
                            m.then_inc(y_ready, 1)

                    @block.scalar
                    def _(act):
                        for c in range(KC):
                            act.wait_ge(q7T_ready, KC * b + c + 1)
                            act.activation(q7T[:, c, :], pT[c][:].bitcast(BF16)[:, 0:S], ACT.Copy).then_inc(q7T_done, 1)
                        for t in range(TPB):
                            for half in range(2):
                                n = 2 * t + half
                                act.wait_ge(hid_ready, 8 * b + n + 1)
                                act.activation(hid[:, t, half * D:(half + 1) * D], pU[n % 4][:], ACT.Relu,
                                               scale=deq7[:, t:t + 1]).then_inc(relu_done, 1)
                        for t in range(TPB):
                            act.wait_ge(hmax_done, TPB * b + t + 1)
                            act.activation(hid[:, t, :], hid[:, t, :], ACT.Square).then_inc(hsq_done, 1)
                        for k in range(8):
                            act.wait_ge(hqT_ready, 8 * b + k + 1)
                            act.activation(hqT[:, k, :], pT[k % 4][:].bitcast(BF16)[:, 0:S], ACT.Copy).then_inc(hqT_done, 1)

                    @block.vector
                    def _(dve):
                        l3_mid.on_vector(dve, lambda t: xw[:, t, :], b, None)
                        for t in range(TPB):
                            dve.tensor_scalar(nrm[:, t, :], xw[:, t, :], l3_mid.rstd[:, t:t + 1],
                                              l3_mid.shift[:, t:t + 1], ALU.mult, ALU.add).then_inc(n7_done, 1)
                        dve.wait_ge(n7_done, TPB * b + TPB)
                        dve.tensor_reduce(amax[:], nrm[:], AX.X, ALU.max, apply_absolute_value=True).then_inc(amax_done, 1)
                        dve.wait_ge(amax_done, b + 1)

                        def scales(top, scale, deq, mean, counter):
                            dve.tensor_scalar(top[:], top[:], 1e-5, None, ALU.max).then_inc(counter, 1)
                            dve.wait_ge(counter, 4 * b + 1)
                            dve.reciprocal(scale[:], top[:]).then_inc(counter, 1)
                            dve.wait_ge(counter, 4 * b + 2)
                            dve.tensor_scalar(scale[:], scale[:], 127.0, None, ALU.mult).then_inc(counter, 1)
                            dve.tensor_scalar(deq[:], top[:], 1.0 / 127.0, mean, ALU.mult, ALU.mult).then_inc(counter, 1)
                            dve.wait_ge(counter, 4 * b + 4)

                        scales(amax, scale7, deq7, tern[:, 1:2], scale_step)
                        for t in range(TPB):
                            dve.tensor_scalar(nrm[:, t, :], nrm[:, t, :], scale7[:, t:t + 1], 127.0, ALU.mult, ALU.min)\
                                .then_inc(quant_step, 1)
                        dve.wait_ge(quant_step, 5 * b + 4)
                        dve.tensor_scalar(nrm[:], nrm[:], -127.0, MAGIC, ALU.max, ALU.add).then_inc(quant_step, 1)
                        dve.wait_ge(quant_step, 5 * b + 5)
                        dve.tensor_scalar(q7[:], nrm[:], MAGIC, None, ALU.subtract).then_inc(q7_done, 1)
                        for t in range(TPB):
                            dve.wait_ge(relu_done, 8 * b + 2 * t + 2)
                            dve.tensor_reduce(hmax[:, t:t + 1], hid[:, t, :], AX.X, ALU.max).then_inc(hmax_done, 1)
                        dve.wait_ge(hmax_done, TPB * b + TPB)
                        dve.tensor_tensor(hmax[:], hmax[:], hmax[:], ALU.mult).then_inc(hquant_step, 1)
                        dve.wait_ge(hquant_step, 9 * b + 1)
                        scales(hmax, hscale, hdeq, tern[:, 3:4], hscale_step)
                        for t in range(TPB):
                            dve.wait_ge(hsq_done, TPB * b + t + 1)
                            dve.tensor_scalar(hid[:, t, :], hid[:, t, :], hscale[:, t:t + 1], 127.0, ALU.mult, ALU.min)\
                                .then_inc(hquant_step, 1)
                        for t in range(TPB):
                            dve.wait_ge(hquant_step, 9 * b + 2 + t)
                            dve.tensor_scalar(hid[:, t, :], hid[:, t, :], -127.0, MAGIC, ALU.max, ALU.add)\
                                .then_inc(hquant_step, 1)
                        for t in range(TPB):
                            dve.wait_ge(hquant_step, 9 * b + 6 + t)
                            dve.tensor_scalar(hq[:, t, :], hid[:, t, :], MAGIC, None, ALU.subtract).then_inc(hq_done, 1)
                        for t in range(TPB):
                            dve.wait_ge(y_ready, TPB * b + t + 1)
                            dve.scalar_tensor_tensor(out=nrm[:, t, :], in0=pU[t][:], scalar=hdeq[:, t:t + 1],
                                                     in1=xw[:, t, :], op0=ALU.mult, op1=ALU.add).then_inc(x8_done, 1)

                    @block.sync
                    def _(sp):
                        for t in range(TPB):
                            sp.wait_ge(x8_done, TPB * b + t + 1)
                            sp.dma_start(out_d[:, bass.ds(b * TPB + t, 1), :], nrm[:, t:t + 1, :]).then_inc(stored, 16)
                        sp.wait_ge(stored, 16 * TPB * b + 16 * TPB)
                        sp.sem_inc(Norm.held, 1)




_INS = ['x', 'ctx_512', 'mask_SxS2_bk1', 'mask_BxS2_bf0', 'L0_xattn_W', 'L0_xattn_b', 'L0_ffn_gate_w', 'L0_ffn_wg',
        'L0_ffn_wu', 'L0_ffn_wd', 'L0_ffn_sg', 'L0_ffn_su', 'L0_ffn_sd', 'L1_xattn_Wq', 'L1_xattn_Wk',
        'L1_xattn_gamma_raw', 'L1_ffn_factors', 'L1_ffn_bias', 'L2_xattn_Wq', 'L2_xattn_bq', 'L2_xattn_Wk',
        'L2_xattn_bk', 'L2_ffn_in_gamma', 'L2_ffn_in_beta', 'L2_ffn_agg_w', 'L2_ffn_agg_b', 'L2_ffn_pn_gamma',
        'L2_ffn_pn_beta', 'L2_ffn_d1_w', 'L2_ffn_d1_b', 'L2_ffn_d2_w', 'L2_ffn_d2_b', 'L2_ffn_bc_w', 'L2_ffn_bc_b',
        'L2_ffn_gate_w', 'L2_ffn_gate_b', 'L2_ffn_out_gamma', 'L2_ffn_out_beta', 'L3_ffn_w_up', 'L3_ffn_w_down']


def kernel(**inputs):
    import numpy as _np
    import concourse.bacc as _bacc
    from concourse import mybir as _mybir
    from concourse.bass_utils import run_bass_kernel_spmd as _run

    nc = _bacc.Bacc("TRN2", target_bir_lowering=False, num_devices=1)
    arrays, args = {}, []
    for name in _INS:
        a = _np.ascontiguousarray(inputs[name]).reshape(_np.shape(inputs[name]) or (1,))
        if a.dtype == _np.bool_:
            a = a.view(_np.int32)
        arrays[f"in_{name}_dram"] = a
        args.append(nc.dram_tensor(f"in_{name}_dram", a.shape, _mybir.dt.from_np(a.dtype), kind="ExternalInput").ap())
    args.append(nc.dram_tensor("out_0_dram", (B, S, D), F32, kind="ExternalOutput").ap())
    program(nc, *args)
    r = _run(nc, [arrays], core_ids=[0])
    return r.results[0]["out_0_dram"]
```

```python
from contextlib import ExitStack

import concourse.bass as bass
from concourse import mybir
from concourse.alu_op_type import AluOpType as ALU

F32 = mybir.dt.float32
F16 = mybir.dt.float16
BF16 = mybir.dt.bfloat16
U8 = mybir.dt.uint8
I32 = mybir.dt.int32
ACT = mybir.ActivationFunctionType
AX = mybir.AxisListType

P = 128
B, S, D = 4, 512, 512
C = 128
TPB = S // P
NT = B * TPB
KC = D // P
E, F, TOPK = 32, 192, 6
FSH = 384
UNITS = 56
ROWS_T = UNITS * S // P
NOWHERE = 1 << 20
W_SCALE = 64.0
K_SEL = int(S * 0.3)
NEG = -3.0e38
MASKED = -1.0e38
P_ASEM = 0.6
HID = 2048
K_STEPS = 4
QH, KVH, DH = 32, 8, 16
IUP = 1024
G_SCALE = 16.0
MAGIC = 1.5 * 2.0 ** 23


def tile_of(tensor, t):
    if isinstance(t, int):
        return tensor[:, t, :]
    return tensor[:, bass.ds(t, 1), :].rearrange("p a d -> p (a d)")


def hold(eng, semaphore, value):
    eng.wait_ge(semaphore, value)
    eng.sem_inc(Norm.held, 1)


class Norm:

    held = None

    def __init__(self, name, sb, sem, eps):
        self.eps = eps
        self.stats = sb(name + "_stats", [P, TPB, 6], F32)
        self.meanvar = sb(name + "_meanvar", [P, TPB, 2], F32)
        self.vareps = sb(name + "_vareps", [P, TPB], F32)
        self.rstd = sb(name + "_rstd", [P, TPB], F32)
        self.shift = sb(name + "_shift", [P, TPB], F32)
        self.stats_done = sem(name + "_stats_done")
        self.meanvar_done = sem(name + "_meanvar_done")
        self.vareps_done = sem(name + "_vareps_done")
        self.rstd_done = sem(name + "_rstd_done")
        self.shift_done = sem(name + "_shift_done")

    def on_vector(self, dve, source, b, before):
        if before is not None:
            hold(dve, before[0], before[1])
        for t in range(TPB):
            dve.bn_stats(self.stats[:, t, :], source(t)).then_inc(self.stats_done, 1)
        hold(dve, self.stats_done, TPB * b + TPB)
        for t in range(TPB):
            dve.bn_aggr(self.meanvar[:, t, :], self.stats[:, t, :]).then_inc(self.meanvar_done, 1)
        dve.wait_ge(self.meanvar_done, TPB * b + TPB)
        dve.tensor_scalar(self.vareps[:], self.meanvar[:, :, 1], self.eps, None, ALU.add)\
            .then_inc(self.vareps_done, 1)
        dve.wait_ge(self.rstd_done, b + 1)
        dve.scalar_tensor_tensor(out=self.shift[:], in0=self.meanvar[:, :, 0], scalar=-1.0, in1=self.rstd[:],
                                 op0=ALU.mult, op1=ALU.mult).then_inc(self.shift_done, 1)
        dve.wait_ge(self.shift_done, b + 1)

    def on_gpsimd(self, pool, half, b):
        pool.wait_ge(self.vareps_done, b + 1)
        pool.tensor_tensor(self.rstd[:], self.vareps[:], half[:, 0:TPB], ALU.pow).then_inc(self.rstd_done, 1)


def split_matmul(pe, out, lhs_hi, lhs_lo, rhs_hi, rhs_lo, first, last):
    pe.matmul(out, lhs_hi, rhs_hi, start=first, stop=False)
    pe.matmul(out, lhs_hi, rhs_lo, start=False, stop=False)
    return pe.matmul(out, lhs_lo, rhs_hi, start=False, stop=last)


def program(nc, x, ctx_512, mask_SxS2_bk1, mask_BxS2_bf0, L0_xattn_W, L0_xattn_b, L0_ffn_gate_w, L0_ffn_wg,
            L0_ffn_wu, L0_ffn_wd, L0_ffn_sg, L0_ffn_su, L0_ffn_sd, L1_xattn_Wq, L1_xattn_Wk,
            L1_xattn_gamma_raw, L1_ffn_factors, L1_ffn_bias, L2_xattn_Wq, L2_xattn_bq, L2_xattn_Wk,
            L2_xattn_bk, L2_ffn_in_gamma, L2_ffn_in_beta, L2_ffn_agg_w, L2_ffn_agg_b, L2_ffn_pn_gamma,
            L2_ffn_pn_beta, L2_ffn_d1_w, L2_ffn_d1_b, L2_ffn_d2_w, L2_ffn_d2_b, L2_ffn_bc_w, L2_ffn_bc_b,
            L2_ffn_gate_w, L2_ffn_gate_b, L2_ffn_out_gamma, L2_ffn_out_beta, L3_ffn_w_up, L3_ffn_w_down,
            out):
    x_d = x.rearrange("b (t p) d -> p (b t) d", p=P)
    out_d = out.rearrange("b (t p) d -> p (b t) d", p=P)
    ctx_d = ctx_512.rearrange("b (t p) d -> p (b t) d", p=P)

    with ExitStack() as whole:
        def sb(name, shape, dt=F32):
            return whole.enter_context(nc.sbuf_tensor(name, shape, dt))

        signals = []

        def sem(name):
            signals.append(nc.alloc_semaphore(name))
            return signals[-1]

        def psum_banks(scope, name, n, dt=F32):
            width = 512 if dt == F32 else 1024
            return [scope.enter_context(nc.psum_tensor(f"{name}{i}", [P, width], dt)) for i in range(n)]

        Norm.held = nc.alloc_semaphore("held")

        xres = sb("xres", [P, NT, D])
        ident = sb("ident", [P, P])
        ident_h = sb("ident_h", [P, P], F16)
        ident_b = sb("ident_b", [P, P], BF16)
        ones = sb("ones", [P, P])
        minus_half = sb("minus_half", [P, NT])
        gam = sb("gam", [P, 4])
        gate2_hi = sb("gate2_hi", [P, KC, D], F16)
        gate2_lo = sb("gate2_lo", [P, KC, D], F16)
        gate2_bias = sb("gate2_bias", [2, D], F16)
        ones_h = sb("ones_h", [2, P], F16)
        up_t = sb("up_t", [P, KC, IUP], BF16)
        dn_t = sb("dn_t", [P, IUP // P, D], BF16)
        tern = sb("tern", [P, 4])

        middle = whole.enter_context(ExitStack())
        def sbd(name, shape, dt=F32):
            return middle.enter_context(nc.sbuf_tensor(name, shape, dt))
        learned = sbd("learned", [P, NT, S])
        proj_hi = [None, None] + [sbd(f"proj_hi{i}", [P, B * S], F16) for i in (2, 3)]
        proj_lo = [None, None] + [sbd(f"proj_lo{i}", [P, B * S], F16) for i in (2, 3)]

        early = whole.enter_context(ExitStack())
        def sbe(name, shape, dt=F32):
            return early.enter_context(nc.sbuf_tensor(name, shape, dt))

        proj_hi[0], proj_lo[0] = [m[:].rearrange("p c e -> p (c e)") for m in (gate2_hi, gate2_lo)]
        halves_of_up = up_t[:].rearrange("p c e -> p (c e)").bitcast(F16)
        proj_hi[1], proj_lo[1] = halves_of_up[:, 0:B * S], halves_of_up[:, B * S:2 * B * S]
        hT_hi = sbe("hT_hi", [P, KC, B * S], F16)
        hT_lo = sbe("hT_lo", [P, KC, B * S], F16)
        scores = dn_t[:].rearrange("p k e -> p (k e)").bitcast(F32)[:, 0:NT * E].rearrange("p (t e) -> p t e", e=E)
        gate6 = sbe("gate6", [P, NT, TOPK])
        place = sbe("place", [P, NT, TOPK], I32)
        pairs = sbe("pairs", [P, NT, TOPK, 2], I32)
        unit_expert = sbe("unit_expert", [1, UNITS], I32)
        table_fill = sbe("table_fill", [P, 2 * ROWS_T], I32)
        h_rows = nc.dram_tensor("h_rows", (NT * P, D), F32).ap()
        table_d = nc.dram_tensor("slot_table", (P * ROWS_T, 2), I32).ap()
        choice_rows = nc.dram_tensor("choice_rows", (NT * P * TOPK, D), F32).ap()

        first = whole.enter_context(ExitStack())
        def sbe(name, shape, dt=F32):
            return first.enter_context(nc.sbuf_tensor(name, shape, dt))

        ctxs = sbe("ctxs", [P, NT, C])
        ctxT = sbe("ctxT", [P, B * S])
        proj_f = [sbe(f"proj_f{i}", [P, S]) for i in range(2)]
        w0 = sbe("w0", [P, 2])
        b0 = sbe("b0", [P, 1])
        wj_rep = sbe("wj_rep", [P, P])
        row_term = sbe("row_term", [P, NT])
        proj_w = sbe("proj_w", [P, 4, C])
        proj_wT = sbe("proj_wT", [P, 4, C])
        proj_b = sbe("proj_b", [P, 2])
        gate_f = sbe("gate_f", [P, KC, E])
        gate_hi = sbe("gate_hi", [P, KC, E], F16)
        gate_lo = sbe("gate_lo", [P, KC, E], F16)

        x_in = sem("x_in")
        small_in = sem("small_in")
        ctx_in = sem("ctx_in")
        gamma_in = sem("gamma_in")
        consts_zeroed = sem("consts_zeroed")
        consts_done = sem("consts_done")
        ctx_transposed = sem("ctx_transposed")
        ctxT_done = sem("ctxT_done")
        projT_ready = sem("projT_ready")
        projT_done = sem("projT_done")
        proj_ready = sem("proj_ready")
        proj_done = sem("proj_done")
        wj_done = sem("wj_done")
        row_ready = sem("row_ready")
        row_done = sem("row_done")
        gate_hi_done = sem("gate_hi_done")
        gate_lo_done = sem("gate_lo_done")
        gamma_sig = sem("gamma_sig")
        gamma_done = sem("gamma_done")
        proj_hi_done = sem("proj_hi_done")
        proj_lo_done = sem("proj_lo_done")

        with ExitStack() as scope, nc.Block() as block:
            pT = psum_banks(scope, "setupT", 4)
            pW = psum_banks(scope, "setupW", 1)[0]
            pP = psum_banks(scope, "setupP", 2)
            pR = psum_banks(scope, "setupR", 1)[0]

            @block.sync
            def _(sp):
                sp.dma_start(ctxs[:], ctx_d).then_inc(ctx_in, 16)
                for i, w in enumerate((L1_xattn_Wq, L1_xattn_Wk, L2_xattn_Wq, L2_xattn_Wk)):
                    sp.dma_start(proj_w[:, i, :], w[:]).then_inc(small_in, 16)
                for i in range(2):
                    sp.dma_start(w0[:, i:i + 1], L0_xattn_W[0, i * C:(i + 1) * C].rearrange("(p a) -> p a", a=1))\
                        .then_inc(small_in, 16)
                sp.dma_start(b0[:], L0_xattn_b.rearrange("(a c) -> a c", a=1).to_broadcast([P, 1]))\
                    .then_inc(small_in, 16)
                sp.dma_start(proj_b[:, 0:1], L2_xattn_bq.rearrange("(p a) -> p a", a=1)).then_inc(small_in, 16)
                sp.dma_start(proj_b[:, 1:2], L2_xattn_bk.rearrange("(p a) -> p a", a=1)).then_inc(small_in, 16)
                sp.dma_start(gate_f[:], L0_ffn_gate_w.rearrange("(p c) e -> p c e", c=KC)).then_inc(small_in, 16)
                sp.dma_start(gam[:, 0:1], L1_xattn_gamma_raw.rearrange("(a c) -> a c", a=1).to_broadcast([P, 1])).then_inc(gamma_in, 16)
                for b in range(B):
                    sp.dma_start(xres[:, TPB * b:TPB * (b + 1), :], x_d[:, TPB * b:TPB * (b + 1), :])\
                        .then_inc(x_in, 16)

            @block.gpsimd
            def _(pool):
                for m in (ident, ident_h, ident_b):
                    pool.memset(m[:], 0.0).then_inc(consts_zeroed, 1)
                pool.memset(ones[:], 1.0).then_inc(consts_done, 1)
                pool.memset(minus_half[:], -0.5).then_inc(consts_done, 1)
                pool.wait_ge(consts_zeroed, 3)
                for m in (ident, ident_h, ident_b):
                    pool.affine_select(out=m[:], in_=m[:], compare_op=ALU.not_equal, fill=1.0, base=0,
                                       pattern=[[-1, P]], channel_multiplier=1).then_inc(consts_done, 1)

            @block.tensor
            def _(pe):
                pe.wait_ge(consts_done, 5)
                pe.wait_ge(small_in, 160)
                for i in range(4):
                    m = pe.transpose(pW[:, i * C:(i + 1) * C], proj_w[:, i, :], ident[:])
                m.then_inc(projT_ready, 1)
                pe.wait_ge(ctx_in, 16)
                for b in range(B):
                    for t in range(TPB):
                        m = pe.transpose(pT[b][:, t * P:(t + 1) * P], ctxs[:, TPB * b + t, :], ident[:])
                    m.then_inc(ctx_transposed, 1)
                pe.wait_ge(ctxT_done, B)
                for t in range(NT):
                    m = pe.matmul(pR[:, t:t + 1], ctxT[:, t * P:(t + 1) * P], w0[:, 0:1], start=True, stop=True)
                m.then_inc(row_ready, 1)
                pe.wait_ge(projT_done, 1)
                n = 0
                for i in range(4):
                    for b in range(B):
                        if n >= 2:
                            pe.wait_ge(proj_done, n - 1)
                        pe.matmul(pP[n % 2][:], proj_wT[:, i, :], ctxT[:, b * S:(b + 1) * S],
                                  start=True, stop=True).then_inc(proj_ready, 1)
                        n += 1

            @block.scalar
            def _(act):
                act.wait_ge(gamma_in, 16)
                act.activation(gam[:, 1:2], gam[:, 0:1], ACT.Sigmoid).then_inc(gamma_sig, 1)
                act.wait_ge(small_in, 160)
                act.activation(gate_hi[:], gate_f[:], ACT.Copy).then_inc(gate_hi_done, 1)
                for b in range(B):
                    act.wait_ge(ctx_transposed, b + 1)
                    act.activation(ctxT[:, b * S:(b + 1) * S], pT[b][:], ACT.Copy).then_inc(ctxT_done, 1)
                n = 0
                for i in range(4):
                    for b in range(B):
                        act.wait_ge(proj_ready, n + 1)
                        if n >= 2:
                            act.wait_ge(proj_lo_done, n - 1)
                        act.activation(proj_f[n % 2][:], pP[n % 2][:], ACT.Identity,
                                       bias=0.0 if i < 2 else proj_b[:, i - 2:i - 1]).then_inc(proj_done, 1)
                        act.wait_ge(proj_done, n + 1)
                        act.activation(proj_hi[i][:, b * S:(b + 1) * S], proj_f[n % 2][:], ACT.Copy)\
                            .then_inc(proj_hi_done, 1)
                        n += 1

            @block.vector
            def _(dve):
                dve.wait_ge(small_in, 160)
                dve.wait_ge(consts_done, 5)
                dve.tensor_scalar(wj_rep[:], ones[:], w0[:, 1:2], None, ALU.mult).then_inc(wj_done, 1)
                dve.wait_ge(projT_ready, 1)
                dve.tensor_copy(proj_wT[:].rearrange("p a c -> p (a c)"), pW[:]).then_inc(projT_done, 1)
                dve.wait_ge(gate_hi_done, 1)
                dve.tensor_tensor(gate_lo[:], gate_f[:], gate_hi[:], ALU.subtract).then_inc(gate_lo_done, 1)
                dve.wait_ge(gamma_sig, 1)
                dve.tensor_scalar(gam[:, 2:3], gam[:, 1:2], 0.5, None, ALU.mult).then_inc(gamma_done, 1)
                dve.tensor_scalar(gam[:, 3:4], gam[:, 1:2], -1.0, 1.0, ALU.mult, ALU.add).then_inc(gamma_done, 1)
                dve.wait_ge(row_ready, 1)
                dve.tensor_scalar(row_term[:], pR[:, 0:NT], b0[:, 0:1], None, ALU.add).then_inc(row_done, 1)
                n = 0
                for i in range(4):
                    for b in range(B):
                        dve.wait_ge(proj_hi_done, n + 1)
                        dve.tensor_tensor(proj_lo[i][:, b * S:(b + 1) * S], proj_f[n % 2][:],
                                          proj_hi[i][:, b * S:(b + 1) * S], ALU.subtract).then_inc(proj_lo_done, 1)
                        n += 1


        col_ready = sem("col_ready")
        sig_done = sem("sig_done")
        l0_scale_done = sem("l0_scale_done")
        l0_norm_done = sem("l0_norm_done")
        x1_done = sem("x1_done")
        h_done = sem("h_done")
        hT_ready = sem("hT_ready")
        hT_hi_done = sem("hT_hi_done")
        hT_lo_done = sem("hT_lo_done")
        logits_ready = sem("logits_ready")
        scores_done = sem("scores_done")
        h_stored = sem("h_stored")

        with ExitStack() as scope:
            def sbl(name, shape, dt=F32):
                return scope.enter_context(nc.sbuf_tensor(name, shape, dt))
            l0_in = Norm("l0_in", sbl, sem, 1e-5)
            l0_out = Norm("l0_out", sbl, sem, 1e-5)
            sig = sbl("sig", [P, TPB, S])
            xn = sbl("xn", [P, TPB, D])
            h = xn
            l0_mul = sbl("l0_mul", [P, TPB])
            l0_add = sbl("l0_add", [P, TPB])
            pC = psum_banks(scope, "l0col", 1)[0]
            pH = psum_banks(scope, "l0hT", KC)
            pL = psum_banks(scope, "l0log", 1)[0]
            with nc.Fori(0, B) as b, nc.Block() as block:
                @block.tensor
                def _(pe):
                    pe.matmul(pC[:], wj_rep[:], ctxT[:, bass.ds(b * S, S)], start=True, stop=True)\
                        .then_inc(col_ready, 1)
                    pe.wait_ge(h_done, TPB * b + TPB)
                    for c in range(KC):
                        for t in range(TPB):
                            m = pe.transpose(pH[c][:, t * P:(t + 1) * P], h[:, t, c::KC], ident[:])
                        m.then_inc(hT_ready, 1)
                    pe.wait_ge(hT_lo_done, KC * b + KC)
                    for t in range(TPB):
                        for c in range(KC):
                            hi = hT_hi[:, c, bass.ds(b * S + t * P, P)]
                            lo = hT_lo[:, c, bass.ds(b * S + t * P, P)]
                            m = split_matmul(pe, pL[:, t * E:(t + 1) * E], hi, lo, gate_hi[:, c, :],
                                             gate_lo[:, c, :], c == 0, c == KC - 1)
                    m.then_inc(logits_ready, 1)

                @block.scalar
                def _(act):
                    act.wait_ge(col_ready, b + 1)
                    for t in range(TPB):
                        act.activation(sig[:, t, :], pC[:], ACT.Sigmoid, bias=row_term[:, bass.ds(b * TPB + t, 1)])\
                            .then_inc(sig_done, 1)
                    for c in range(KC):
                        act.wait_ge(hT_ready, KC * b + c + 1)
                        act.activation(hT_hi[:, c, bass.ds(b * S, S)], pH[c][:], ACT.Copy).then_inc(hT_hi_done, 1)
                    act.wait_ge(logits_ready, b + 1)
                    act.activation(scores[:, bass.ds(b * TPB, TPB), :].rearrange("p t e -> p (t e)"),
                                   pL[:, 0:TPB * E], ACT.Sigmoid).then_inc(scores_done, 1)

                @block.sync
                def _(sp):
                    sp.wait_ge(h_done, TPB * b + TPB)
                    sp.dma_start(h_rows.rearrange("(t p) d -> p t d", p=P)[:, bass.ds(b * TPB, TPB), :], h[:])\
                        .then_inc(h_stored, 16)
                    hold(sp, h_stored, 16 * b + 16)

                @block.gpsimd
                def _(pool):
                    l0_in.on_gpsimd(pool, minus_half, b)
                    l0_out.on_gpsimd(pool, minus_half, b)

                @block.vector
                def _(dve):
                    l0_in.on_vector(dve, lambda t: tile_of(xres, b * TPB + t), b, (x_in, 16 * B))
                    dve.tensor_scalar(l0_mul[:], l0_in.rstd[:], 1.0 - P_ASEM, 1.0, ALU.mult, ALU.add)\
                        .then_inc(l0_scale_done, 1)
                    dve.tensor_scalar(l0_add[:], l0_in.shift[:], 1.0 - P_ASEM, None, ALU.mult)\
                        .then_inc(l0_scale_done, 1)
                    dve.wait_ge(l0_scale_done, 2 * b + 2)
                    for t in range(TPB):
                        dve.tensor_scalar(xn[:, t, :], tile_of(xres, b * TPB + t), l0_mul[:, t:t + 1],
                                          l0_add[:, t:t + 1], ALU.mult, ALU.add).then_inc(l0_norm_done, 1)
                    dve.wait_ge(l0_norm_done, TPB * b + TPB)
                    for t in range(TPB):
                        dve.wait_ge(sig_done, TPB * b + t + 1)
                        dve.scalar_tensor_tensor(out=tile_of(xres, b * TPB + t), in0=sig[:, t, :], scalar=P_ASEM,
                                                 in1=xn[:, t, :], op0=ALU.mult, op1=ALU.add).then_inc(x1_done, 1)
                    l0_out.on_vector(dve, lambda t: tile_of(xres, b * TPB + t), b, (x1_done, TPB * b + TPB))
                    for t in range(TPB):
                        dve.tensor_scalar(h[:, t, :], tile_of(xres, b * TPB + t), l0_out.rstd[:, t:t + 1],
                                          l0_out.shift[:, t:t + 1], ALU.mult, ALU.add).then_inc(h_done, 1)
                    for c in range(KC):
                        dve.wait_ge(hT_hi_done, KC * b + c + 1)
                        dve.tensor_tensor(hT_lo[:, c, bass.ds(b * S, S)], pH[c][:], hT_hi[:, c, bass.ds(b * S, S)],
                                          ALU.subtract).then_inc(hT_lo_done, 1)

        first.close()

        route = sem("route")
        sel_done = sem("sel_done")
        ranked = sem("ranked")
        table_filled = sem("table_filled")
        route_consts = sem("route_consts")
        tables_ready = sem("tables_ready")
        with ExitStack() as scope, nc.Block() as block:
            def sbl(name, shape, dt=F32):
                return scope.enter_context(nc.sbuf_tensor(name, shape, dt))
            top8 = sbl("top8", [P, NT, 8])
            sel = sbl("sel", [P, NT, E])
            equal = sbl("equal", [P, NT, E])
            rank = sbl("rank", [P, NT, E])
            gates = sbl("gates", [P, NT, E])
            zero = sbl("zero_row", [P, E])
            room = sbl("room", [P, NT])
            weight = sbl("weight", [P, NT])
            before = sbl("before", [P, P])
            offset = sbl("offset", [P, NT + 1, E])
            slot = sbl("slot", [P, NT, E])
            units = sbl("units", [P, 4, E])
            units_end = sbl("units_end", [P, E])
            units_start = sbl("units_start", [P, E])
            pick = sbl("pick", [P, 2, NT, E])
            slot6 = sbl("slot6", [P, NT, TOPK])
            row6 = sbl("row6", [P, NT, TOPK])
            unit_no = sbl("unit_no", [1, UNITS], I32)
            unit_f = sbl("unit_f", [1, UNITS])
            ended = sbl("ended", [1, UNITS, E])
            unit_expert_f = sbl("unit_expert_f", [1, UNITS])
            pRank, pCount = psum_banks(scope, "route", 2)

            @block.gpsimd
            def _(pool):
                pool.memset(before[:], 0.0).then_inc(route_consts, 1)
                pool.memset(table_fill[:], NOWHERE).then_inc(route_consts, 1)
                pool.iota(unit_no[:], [[1, UNITS]], base=0, channel_multiplier=0).then_inc(route_consts, 1)
                pool.iota(pairs[:, :, :, 0], [[P, NT], [0, TOPK]], base=0, channel_multiplier=1).then_inc(route_consts, 1)
                pool.iota(pairs[:, :, :, 1], [[P * TOPK, NT], [1, TOPK]], base=0, channel_multiplier=TOPK)\
                    .then_inc(route_consts, 1)
                pool.wait_ge(route_consts, 5)
                pool.affine_select(out=before[:], in_=before[:], compare_op=ALU.is_ge, fill=1.0, base=0,
                                   pattern=[[-1, P]], channel_multiplier=1).then_inc(route_consts, 1)

            @block.sync
            def _(sp):
                sp.wait_ge(route_consts, 6)
                sp.dma_start(table_d.rearrange("(p s) w -> p (s w)", p=P), table_fill[:]).then_inc(table_filled, 16)
                sp.wait_ge(table_filled, 16)

            @block.tensor
            def _(pe):
                pe.wait_ge(sel_done, 1)
                pe.wait_ge(route_consts, 6)
                flat = sel[:].rearrange("p t e -> p (t e)")
                pe.matmul(pCount[:], ones[:], flat, start=True, stop=True).then_inc(ranked, 1)
                pe.matmul(pRank[:], before[:], flat, start=True, stop=True).then_inc(ranked, 1)

            @block.vector
            def _(dve):
                steps = [0]

                def done(*instructions):
                    for ins in instructions:
                        ins.then_inc(route, 1)
                        steps[0] += 1
                    dve.wait_ge(route, steps[0])

                done(*[dve.max(top8[:, t, :], scores[:, t, :]) for t in range(NT)],
                     dve.memset(zero[:], 0.0))
                least = top8[:, :, TOPK - 1:TOPK].to_broadcast([P, NT, E])
                done(dve.tensor_tensor(sel[:], scores[:], least, ALU.is_gt),
                     dve.tensor_tensor(equal[:], scores[:], least, ALU.is_equal))
                done(dve.tensor_reduce(room[:], sel[:], AX.X, ALU.add),
                     *[dve.tensor_tensor_scan(rank[:, t, :], equal[:, t, :], zero[:], 0.0, ALU.add, ALU.add)
                       for t in range(NT)])
                done(dve.tensor_scalar(room[:], room[:], -1.0, float(TOPK), ALU.mult, ALU.add))
                done(dve.tensor_tensor(rank[:], rank[:], room[:].unsqueeze(2).to_broadcast([P, NT, E]), ALU.is_le))
                done(dve.tensor_tensor(equal[:], equal[:], rank[:], ALU.mult))
                done(dve.tensor_tensor(sel[:], sel[:], equal[:], ALU.add))
                dve.sem_inc(sel_done, 1)
                done(dve.tensor_tensor(gates[:], sel[:], scores[:], ALU.mult),
                     *[dve.tensor_tensor_scan(rank[:, t, :], sel[:, t, :], zero[:], 0.0, ALU.add, ALU.add)
                       for t in range(NT)])
                done(dve.tensor_reduce(weight[:], gates[:], AX.X, ALU.add))
                done(dve.tensor_scalar(weight[:], weight[:], 1e-20, W_SCALE, ALU.add, ALU.mult))
                done(dve.reciprocal(weight[:], weight[:]))
                done(dve.tensor_tensor(gates[:], gates[:], weight[:].unsqueeze(2).to_broadcast([P, NT, E]), ALU.mult),
                     dve.memset(offset[:, 0, :], 0.0))
                dve.wait_ge(ranked, 2)
                for t in range(NT):
                    done(dve.tensor_tensor(offset[:, t + 1, :], offset[:, t, :], pCount[:, t * E:(t + 1) * E], ALU.add))
                count = offset[:, NT, :]
                done(dve.tensor_tensor(slot[:], offset[:, 0:NT, :], pRank[:].rearrange("p (t e) -> p t e", e=E), ALU.add),
                     dve.tensor_scalar(units[:, 0, :], count, 0.0, None, ALU.is_gt))
                for i in range(1, NT * P // S):
                    done(dve.scalar_tensor_tensor(out=units[:, i, :], in0=count, scalar=float(S * i),
                                                  in1=units[:, i - 1, :], op0=ALU.is_gt, op1=ALU.add))
                done(dve.tensor_tensor_scan(units_end[:], units[:, 3, :], zero[:], 0.0, ALU.add, ALU.add))
                done(dve.tensor_tensor(units_start[:], units_end[:], units[:, 3, :], ALU.subtract))
                done(dve.scalar_tensor_tensor(out=slot[:], in0=units_start[:].unsqueeze(1).to_broadcast([P, NT, E]),
                                              scalar=float(S), in1=slot[:], op0=ALU.mult, op1=ALU.add))
                for k in range(TOPK):
                    done(dve.scalar_tensor_tensor(out=equal[:], in0=rank[:], scalar=float(k + 1), in1=sel[:],
                                                  op0=ALU.is_equal, op1=ALU.mult))
                    done(dve.tensor_tensor(pick[:, 0, :, :], equal[:], slot[:], ALU.mult),
                         dve.tensor_tensor(pick[:, 1, :, :], equal[:], gates[:], ALU.mult))
                    done(dve.tensor_reduce(slot6[:, :, k], pick[:, 0, :, :], AX.X, ALU.add),
                         dve.tensor_reduce(gate6[:, :, k], pick[:, 1, :, :], AX.X, ALU.add))
                done(dve.tensor_scalar(row6[:], slot6[:], 1.0 / P, -(P - 1) / (2.0 * P), ALU.mult, ALU.add))
                done(dve.tensor_scalar(row6[:], row6[:], MAGIC, None, ALU.add))
                done(dve.tensor_scalar(row6[:], row6[:], MAGIC, 1.0 - P * ROWS_T, ALU.subtract, ALU.mult))
                done(dve.scalar_tensor_tensor(out=slot6[:], in0=slot6[:], scalar=float(ROWS_T), in1=row6[:],
                                              op0=ALU.mult, op1=ALU.add))
                done(dve.tensor_copy(place[:], slot6[:]))
                dve.wait_ge(route_consts, 6)
                done(dve.tensor_copy(unit_f[:], unit_no[:]))
                done(dve.tensor_tensor(ended[:], units_end[0:1, :].unsqueeze(1).to_broadcast([1, UNITS, E]),
                                       unit_f[:].unsqueeze(2).to_broadcast([1, UNITS, E]), ALU.is_le))
                done(dve.tensor_reduce(unit_expert_f[:], ended[:], AX.X, ALU.add))
                done(dve.tensor_scalar(unit_expert_f[:], unit_expert_f[:], E - 1.0, None, ALU.min))
                done(dve.tensor_copy(unit_expert[:], unit_expert_f[:]))
                dve.sem_inc(tables_ready, 1)

        w_in = sem("w_in")
        w_hi_done = sem("w_hi_done")
        w_lo_done = sem("w_lo_done")
        up_ready = sem("up_ready")
        silu_done = sem("silu_done")
        act_done = sem("act_done")
        act_hi_done = sem("act_hi_done")
        act_lo_done = sem("act_lo_done")
        down_ready = sem("down_ready")
        added = sem("added")
        sim_ready = sem("sim_ready")
        sim_copied = sem("sim_copied")
        sel_step = sem("sel_step")
        sim_sig_done = sem("sim_sig_done")
        learned_done = sem("learned_done")
        kept_done = sem("kept_done")
        table_written = sem("table_written")
        table_in = sem("table_in")
        gather_index = sem("gather_index")
        scatter_index = sem("scatter_index")
        gathered = [sem(f"gathered{t}") for t in range(TPB)]
        rows_zeroed = sem("rows_zeroed")
        xT_ready = sem("xT_ready")
        xT_hi_done = sem("xT_hi_done")
        xT_lo_done = sem("xT_lo_done")
        scattered = sem("scattered")

        GB = B
        SHARED = 2 * GB
        ROUNDS = (K_SEL - 1) // 8
        SEL_STEPS = 2 * ROUNDS + 1
        STEPS = 4
        SIM_SHARED = NT - UNITS // STEPS

        with ExitStack() as scope:
            def sbl(name, shape, dt=F32):
                return scope.enter_context(nc.sbuf_tensor(name, shape, dt))
            wup_f = sbl("wup_f", [P, KC, 2, F])
            wdn_f = sbl("wdn_f", [P, 2, D])
            wup_hi = [sbl(f"wup_hi{i}", [P, KC, 3 * P], F16) for i in range(4)]
            wup_lo = [sbl(f"wup_lo{i}", [P, KC, 3 * P], F16) for i in range(4)]
            wdn_hi = [sbl(f"wdn_hi{i}", [P, 2, D], F16) for i in range(4)]
            wdn_lo = [sbl(f"wdn_lo{i}", [P, 2, D], F16) for i in range(4)]
            silu_a = sbl("silu_a", [P, S])
            silu_c = sbl("silu_c", [P // 2, S])
            prod_a = sbl("prod_a", [P, S])
            prod_c = sbl("prod_c", [P // 2, S])
            acta_hi = sbl("acta_hi", [P, S], F16)
            acta_lo = sbl("acta_lo", [P, S], F16)
            actc = sbl("actc", [P, S], F16)
            sim, sim_work, sim_sig = [dn_t[:].rearrange("p k e -> p (k e)").bitcast(F32)[:, i * S:(i + 1) * S]
                                      for i in range(3)]
            sim_top = sbl("sim_top", [P, 8])
            table = sbl("table", [P, ROWS_T, 2], I32)
            gather_at = sbl("gather_at", [P, TPB, 2], I32)
            scatter_at = sbl("scatter_at", [P, TPB, 2], I32)
            pU = psum_banks(scope, "moeU", 3)
            pY = psum_banks(scope, "moeY", 4)
            pS = psum_banks(scope, "moeS", 1)[0]

            spare = hT_hi[:].rearrange("p c s -> p (c s)")
            xT = [[spare[:, (2 * par + half) * B * S:(2 * par + half + 1) * B * S].rearrange("p (c s) -> p c s", c=KC)
                   for half in range(2)] for par in range(2)]
            spare = hT_lo[:].rearrange("p c s -> p (c s)").bitcast(F32)
            rows = spare[:, 0:TPB * D].rearrange("p (t d) -> p t d", d=D)
            out_rows = spare[:, TPB * D:2 * TPB * D].rearrange("p (t d) -> p t d", d=D)

            def load(sp, wg, wu, wd):
                sp.dma_start(wup_f[:, :, 0, :], wg.rearrange("(p c) f -> p c f", c=KC)).then_inc(w_in, 16)
                sp.dma_start(wup_f[:, :, 1, :], wu.rearrange("(p c) f -> p c f", c=KC)).then_inc(w_in, 16)
                sp.dma_start(wdn_f[:, 0, :], wd[0:P, :]).then_inc(w_in, 16)
                for half in range(2):
                    sp.dma_start(wdn_f[64 * half:64 * half + 64, 1, :], wd[P:F, :]).then_inc(w_in, 16)

            def split_hi(act, buf, n):
                act.wait_ge(w_in, 80 * n + 80)
                f, h16 = wup_f, wup_hi[buf]
                act.activation(h16[:, :, 0:P], f[:, :, 0, 0:P], ACT.Copy, scale=W_SCALE).then_inc(w_hi_done, 1)
                act.activation(h16[:, :, P:2 * P], f[:, :, 1, 0:P], ACT.Copy, scale=W_SCALE).then_inc(w_hi_done, 1)
                act.activation(h16[:, :, 2 * P:3 * P].rearrange("p c (g f) -> p c g f", g=2), f[:, :, :, P:F],
                               ACT.Copy, scale=W_SCALE).then_inc(w_hi_done, 1)
                act.activation(wdn_hi[buf][:], wdn_f[:], ACT.Copy, scale=W_SCALE).then_inc(w_hi_done, 1)

            def split_lo(dve, buf, n):
                dve.wait_ge(w_hi_done, 4 * n + 4)
                f, h16, l16 = wup_f, wup_hi[buf], wup_lo[buf]
                for o, i0, i1 in ((l16[:, :, 0:P], f[:, :, 0, 0:P], h16[:, :, 0:P]),
                                  (l16[:, :, P:2 * P], f[:, :, 1, 0:P], h16[:, :, P:2 * P]),
                                  (l16[:, :, 2 * P:2 * P + 64], f[:, :, 0, P:F], h16[:, :, 2 * P:2 * P + 64]),
                                  (l16[:, :, 2 * P + 64:3 * P], f[:, :, 1, P:F], h16[:, :, 2 * P + 64:3 * P]),
                                  (wdn_lo[buf][:], wdn_f[:], wdn_hi[buf][:])):
                    dve.scalar_tensor_tensor(out=o, in0=i0, scalar=W_SCALE, in1=i1, op0=ALU.mult,
                                             op1=ALU.subtract).then_inc(w_lo_done, 1)

            def up_columns(pe, m, buf, col, bank, x_hi, x_lo, group):
                cols = slice(col * P, (col + 1) * P)
                toks = slice(group * S, (group + 1) * S)
                for c in range(KC):
                    mm = split_matmul(pe, pU[bank][:], wup_hi[buf][:, c, cols], wup_lo[buf][:, c, cols],
                                      x_hi[:, c, toks], x_lo[:, c, toks], c == 0, c == KC - 1)
                mm.then_inc(up_ready, 1)

            def down_tile(pe, m, buf, t):
                pe.wait_ge(added, TPB * m + t + 1)
                tok = slice(t * P, (t + 1) * P)
                pe.matmul(pY[t][:], acta_hi[:, tok], wdn_hi[buf][:, 0, :], start=True, stop=False)
                pe.matmul(pY[t][:], acta_hi[:, tok], wdn_lo[buf][:, 0, :], start=False, stop=False)
                pe.matmul(pY[t][:], acta_lo[:, tok], wdn_hi[buf][:, 0, :], start=False, stop=False)
                pe.matmul(pY[t][:], actc[:, tok], wdn_hi[buf][:, 1, :], start=False, stop=False)
                pe.matmul(pY[t][:], actc[0:64, tok], wdn_lo[buf][0:64, 1, :], start=False, stop=True)\
                    .then_inc(down_ready, 1)

            def similarity(pe, tile):
                split_matmul(pe, pS[:], proj_hi[0][:, bass.ds(tile * P, P)], proj_lo[0][:, bass.ds(tile * P, P)],
                             proj_hi[1][:, bass.ds((tile // TPB) * S, S)], proj_lo[1][:, bass.ds((tile // TPB) * S, S)],
                             True, True).then_inc(sim_ready, 1)

            def silu(act, m, which):
                out, src = ((silu_a, pU[0][:]), (silu_c, pU[2][0:64, :]))[which]
                act.wait_ge(up_ready, 3 * m + which + 1)
                act.activation(out[:], src, ACT.Silu, scale=1.0 / W_SCALE).then_inc(silu_done, 1)

            def product_hi(act, m, first=False):
                if not first:
                    act.wait_ge(down_ready, TPB * m)
                act.wait_ge(act_done, 2 * m + 1)
                act.activation(acta_hi[:], prod_a[:], ACT.Copy).then_inc(act_hi_done, 1)
                act.wait_ge(act_done, 2 * m + 2)
                act.activation(actc[0:64, :], prod_c[:], ACT.Copy).then_inc(act_hi_done, 1)

            def products(dve, m, first=False):
                dve.wait_ge(silu_done, 2 * m + 1)
                dve.wait_ge(up_ready, 3 * m + 3)
                if not first:
                    dve.wait_ge(act_lo_done, 2 * m)
                dve.scalar_tensor_tensor(out=prod_a[:], in0=pU[1][:], scalar=1.0 / W_SCALE, in1=silu_a[:],
                                         op0=ALU.mult, op1=ALU.mult).then_inc(act_done, 1)
                dve.wait_ge(silu_done, 2 * m + 2)
                dve.scalar_tensor_tensor(out=prod_c[:], in0=pU[2][64:128, :], scalar=1.0 / W_SCALE,
                                         in1=silu_c[:], op0=ALU.mult, op1=ALU.mult).then_inc(act_done, 1)

            def product_lo(dve, m):
                dve.wait_ge(act_hi_done, 2 * m + 1)
                dve.tensor_tensor(acta_lo[:], prod_a[:], acta_hi[:], ALU.subtract).then_inc(act_lo_done, 1)
                dve.wait_ge(act_hi_done, 2 * m + 2)
                dve.tensor_tensor(actc[64:128, :], prod_c[:], actc[0:64, :], ALU.subtract).then_inc(act_lo_done, 1)

            def take_similarity(dve, tile):
                dve.wait_ge(sim_ready, tile + 1)
                dve.tensor_scalar(sim, pS[:], 1.0 / (4.0 * 32.0 ** 0.5), None, ALU.mult).then_inc(sim_copied, 1)
                hold(dve, sim_copied, tile + 1)

            def search(dve, tile, first, last):
                for r in range(first, last):
                    step = SEL_STEPS * tile + 2 * r
                    src = sim if r == 0 else sim_work
                    if r >= 1:
                        hold(dve, sel_step, step)
                    dve.max(sim_top[:], src).then_inc(sel_step, 1)
                    if r < ROUNDS:
                        hold(dve, sel_step, step + 1)
                        dve.match_replace(sim_work, sim_top[:], src, NEG).then_inc(sel_step, 1)

            def keep(dve, tile):
                dve.wait_ge(sel_step, SEL_STEPS * tile + SEL_STEPS)
                dve.wait_ge(sim_sig_done, tile + 1)
                at = (K_SEL - 1) % 8
                dve.scalar_tensor_tensor(out=sim_work, in0=sim, scalar=sim_top[:, at:at + 1],
                                         in1=sim_sig, op0=ALU.is_ge, op1=ALU.mult).then_inc(kept_done, 1)
                dve.wait_ge(kept_done, tile + 1)
                dve.tensor_scalar(tile_of(learned, tile), sim_work, gam[:, 2:3], None, ALU.mult)\
                    .then_inc(learned_done, 1)

            def similarity_sigmoid(act, tile):
                act.wait_ge(sim_copied, tile + 1)
                act.activation(sim_sig, sim, ACT.Sigmoid).then_inc(sim_sig_done, 1)

            with nc.Block() as block:
                @block.sync
                def _(sp):
                    for n in range(2):
                        cols = slice(n * F, (n + 1) * F)
                        if n == 1:
                            sp.wait_ge(w_lo_done, 5)
                        load(sp, L0_ffn_sg[:, cols], L0_ffn_su[:, cols], L0_ffn_sd[cols, :])

                @block.gpsimd
                def _(pool):
                    for t in range(NT):
                        for k in range(TOPK):
                            pool.indirect_dma_start(out=table_d, out_offset=bass.IndirectOffsetOnAxis(
                                ap=place[:, t, k:k + 1], axis=0), in_=pairs[:, t, k, :], in_offset=None)\
                                .then_inc(table_written, 16)
                    pool.wait_ge(table_written, 16 * NT * TOPK)
                    pool.dma_start(table[:].rearrange("p s w -> p (s w)"),
                                   table_d.rearrange("(p s) w -> p (s w)", p=P)).then_inc(table_in, 16)

                @block.tensor
                def _(pe):
                    for m in range(SHARED):
                        n, g = m // GB, m % GB
                        if g == 0:
                            pe.wait_ge(w_lo_done, 5 * n + 5)
                        if m >= 1:
                            pe.wait_ge(act_done, 2 * m)
                        for col, bank in ((0, 0), (2, 2), (1, 1)):
                            up_columns(pe, m, 2 + n, col, bank, hT_hi, hT_lo, g)
                        if m >= 1:
                            pe.wait_ge(act_lo_done, 2 * m)
                            for t in range(TPB):
                                down_tile(pe, m - 1, 2 + (m - 1) // GB, t)
                        if g == 0:
                            if n == 1:
                                pe.wait_ge(sim_copied, 1)
                            similarity(pe, n)
                    pe.wait_ge(act_lo_done, 2 * SHARED)
                    for t in range(TPB):
                        down_tile(pe, SHARED - 1, 3, t)

                @block.scalar
                def _(act):
                    split_hi(act, 2, 0)
                    for m in range(SHARED):
                        n, g = m // GB, m % GB
                        silu(act, m, 0)
                        silu(act, m, 1)
                        product_hi(act, m, m == 0)
                        if m == 1:
                            split_hi(act, 3, 1)
                        if g == 1:
                            similarity_sigmoid(act, n)

                @block.vector
                def _(dve):
                    def add(m):
                        for t in range(TPB):
                            tile = TPB * (m % GB) + t
                            dve.wait_ge(down_ready, TPB * m + t + 1)
                            dve.scalar_tensor_tensor(out=xres[:, tile, :], in0=pY[t][:], scalar=1.0 / W_SCALE,
                                                     in1=xres[:, tile, :], op0=ALU.mult, op1=ALU.add).then_inc(added, 1)

                    dve.sem_inc(added, TPB)
                    split_lo(dve, 2, 0)
                    for m in range(SHARED):
                        n, g = m // GB, m % GB
                        products(dve, m, m == 0)
                        product_lo(dve, m)
                        if m == 1:
                            split_lo(dve, 3, 1)
                        if m >= 1:
                            add(m - 1)
                        if g == 0:
                            take_similarity(dve, n)
                        per = -(-(ROUNDS + 1) // GB)
                        search(dve, n, per * g, min(per * (g + 1), ROUNDS + 1))
                        if g == GB - 1:
                            keep(dve, n)
                    add(SHARED - 1)

            def transpose_tile(pe, t):
                for c in range(KC):
                    mm = pe.transpose(pS[:, c * P:(c + 1) * P], rows[:, t, c::KC], ident[:])
                mm.then_inc(xT_ready, 1)

            def pe_step(pe, u, j, ahead, tile):
                m = SHARED + u

                def transposes(t):
                    pe.wait_ge(gathered[t], 16 * (u + 3))
                    pe.wait_ge(xT_lo_done, TPB * (u + 2) + t)
                    transpose_tile(pe, t)

                if ahead >= 1:
                    pe.wait_ge(w_lo_done, 5 * (u + 3) + 5)
                    pe.wait_ge(act_done, 2 * m + 2)
                    pe.wait_ge(xT_lo_done, TPB * (u + 2))
                    for t, (col, bank) in enumerate(((0, 0), (2, 2), (1, 1))):
                        if j == 0 and t == 1:
                            pe.wait_ge(sim_copied, tile + 1)
                        if ahead == 2 and (j != 0 or t >= 1):
                            transposes(t - (j == 0))
                        up_columns(pe, m + 1, (j + 1) % 4, col, bank, *xT[(j + 1) % 2], 0)
                    if ahead == 2:
                        transposes(3 - (j == 0))
                if j >= 0:
                    pe.wait_ge(act_lo_done, 2 * m + 2)
                    for t in range(TPB):
                        if j == 0 and t == 2:
                            transposes(3)
                        down_tile(pe, m, j, t)
                if j in (-1, STEPS - 1) and ahead == 2:
                    pe.wait_ge(xT_lo_done, KC * (u + 2) + KC)
                    similarity(pe, tile + 1)

            def tokens_of(half, j, t):
                return xT[j % 2][half][:, :, t * P:(t + 1) * P]

            def tokens_hi(act, u, j, t):
                act.wait_ge(xT_ready, TPB * u + t + 1)
                act.activation(tokens_of(0, j, t), pS[:].rearrange("p (c s) -> p c s", c=KC), ACT.Copy)\
                    .then_inc(xT_hi_done, 1)

            def tokens_lo(dve, u, j, t):
                dve.wait_ge(xT_hi_done, TPB * u + t + 1)
                dve.tensor_tensor(tokens_of(1, j, t), pS[:].rearrange("p (c s) -> p c s", c=KC), tokens_of(0, j, t),
                                  ALU.subtract).then_inc(xT_lo_done, 1)

            def act_step(act, u, j, ahead, sigmoid, tile):
                m = SHARED + u
                two = ahead == 2
                if two and j != 0:
                    tokens_hi(act, u + 2, j + 2, 0)
                if two:
                    split_hi(act, (j + 2) % 4, u + 4)
                if ahead >= 1:
                    silu(act, m + 1, 0)
                if two:
                    tokens_hi(act, u + 2, j + 2, 0 if j == 0 else 1)
                if ahead >= 1:
                    silu(act, m + 1, 1)
                if two:
                    for t in range(1 if j == 0 else 2, TPB):
                        tokens_hi(act, u + 2, j + 2, t)
                if j >= 0:
                    if not isinstance(u, int) or u >= 1:
                        hold(act, scattered, 64 * u)
                    for t in range(TPB):
                        act.wait_ge(down_ready, TPB * m + t + 1)
                        act.activation(out_rows[:, t, :], pY[t][:], ACT.Copy).then_inc(added, 1)
                if ahead >= 1:
                    product_hi(act, m + 1)
                if sigmoid:
                    similarity_sigmoid(act, tile)

            def dve_step(dve, u, j, ahead, tile):
                m = SHARED + u
                per = -(-(ROUNDS + 1) // STEPS)

                def part_of_search(first, last):
                    if j >= 0:
                        search(dve, tile, min(per * j + first, ROUNDS + 1), min(per * j + last, ROUNDS + 1))

                if ahead == 2:
                    if j != 0:
                        tokens_lo(dve, u + 2, j + 2, 0)
                    split_lo(dve, (j + 2) % 4, u + 4)
                    if j == 0:
                        tokens_lo(dve, u + 2, j + 2, 0)
                if ahead == 2:
                    tokens_lo(dve, u + 2, j + 2, 1)
                part_of_search(0, 1)
                if ahead == 2:
                    tokens_lo(dve, u + 2, j + 2, 2)
                part_of_search(1, 2)
                if ahead >= 1:
                    products(dve, m + 1)
                if ahead == 2:
                    tokens_lo(dve, u + 2, j + 2, 3)
                part_of_search(2, 4)
                if ahead >= 1:
                    product_lo(dve, m + 1)
                part_of_search(4, per)
                if j == STEPS - 1:
                    keep(dve, tile)
                if j in (-1, STEPS - 1) and ahead == 2:
                    take_similarity(dve, tile + 1)

            def gather(pool, u, first=False):
                for t in range(TPB):
                    if not first:
                        hold(pool, xT_ready, TPB * u - TPB + t + 1)
                    pool.tensor_copy(gather_at[:, t, :], table[:, bass.ds(TPB * u + t, 1), :]
                                     .rearrange("p a w -> p (a w)")).then_inc(gather_index, 1)
                    hold(pool, gather_index, TPB * u + t + 1)
                    pool.indirect_dma_start(out=rows[:, t, :], out_offset=None, in_=h_rows,
                                            in_offset=bass.IndirectOffsetOnAxis(ap=gather_at[:, t, 0:1], axis=0),
                                            bounds_check=NT * P - 1, oob_is_err=False).then_inc(gathered[t], 16)

            def scatter(pool, u):
                if not isinstance(u, int) or u >= 1:
                    hold(pool, scattered, 64 * u)
                pool.tensor_copy(scatter_at[:], table[:, bass.ds(TPB * u, TPB), :]).then_inc(scatter_index, 1)
                hold(pool, scatter_index, u + 1)
                hold(pool, added, TPB * (SHARED + u) + 2 * TPB)
                for t in range(TPB):
                    pool.indirect_dma_start(out=choice_rows, out_offset=bass.IndirectOffsetOnAxis(
                        ap=scatter_at[:, t, 1:2], axis=0), in_=out_rows[:, t, :], in_offset=None,
                        bounds_check=NT * P * TOPK - 1, oob_is_err=False).then_inc(scattered, 16)

            LAST = UNITS // STEPS - 1

            def steps_of(it):
                for j in range(STEPS):
                    u = STEPS * it + j
                    yield u, j, min(2, UNITS - 1 - u) if isinstance(it, int) else 2

            with nc.Block() as block:
                @block.sync
                def _(sp):
                    def unit(u):
                        e = sp.value_load(unit_expert[0:1, bass.ds(u, 1)], min_val=0, max_val=E - 1)
                        sp.wait_ge(w_lo_done, 5 * (u + 2))
                        load(sp, *[w[bass.ds(e, 1)].rearrange("a r f -> (a r) f")
                                   for w in (L0_ffn_wg, L0_ffn_wu, L0_ffn_wd)])

                    with sp.Fori(0, UNITS) as u:
                        unit(u)

                @block.gpsimd
                def _(pool):
                    pool.memset(rows, 0.0).then_inc(rows_zeroed, 1)
                    pool.wait_ge(rows_zeroed, 1)
                    gather(pool, 0, first=True)
                    gather(pool, 1)
                    gather(pool, 2)

                    def iteration(it):
                        for u, j, ahead in steps_of(it):
                            more = not isinstance(u, int) or u + 3 < UNITS
                            if more:
                                gather(pool, u + 3)
                            scatter(pool, u)

                    iteration(0)
                    with pool.Fori(1, LAST) as it:
                        iteration(it)
                    iteration(LAST)
                    pool.wait_ge(scattered, 64 * UNITS)

                @block.tensor
                def _(pe):
                    for t in range(TPB):
                        pe.wait_ge(gathered[t], 16)
                        if t >= 1:
                            pe.wait_ge(xT_lo_done, t)
                        transpose_tile(pe, t)
                    pe_step(pe, -1, -1, 2, SIM_SHARED - 1)

                    def iteration(it):
                        for u, j, ahead in steps_of(it):
                            pe_step(pe, u, j, ahead, SIM_SHARED + it)

                    iteration(0)
                    with pe.Fori(1, LAST) as it:
                        iteration(it)
                    iteration(LAST)

                @block.scalar
                def _(act):
                    for c in range(KC):
                        tokens_hi(act, 0, 0, c)
                    split_hi(act, 0, 2)
                    act_step(act, -1, -1, 2, False, None)

                    def iteration(it):
                        for u, j, ahead in steps_of(it):
                            act_step(act, u, j, ahead, j == 0, SIM_SHARED + it)

                    iteration(0)
                    with act.Fori(1, LAST) as it:
                        iteration(it)
                    iteration(LAST)

                @block.vector
                def _(dve):
                    for c in range(KC):
                        tokens_lo(dve, 0, 0, c)
                    split_lo(dve, 0, 2)
                    dve_step(dve, -1, -1, 2, SIM_SHARED - 1)

                    def iteration(it):
                        for u, j, ahead in steps_of(it):
                            dve_step(dve, u, j, ahead, SIM_SHARED + it)

                    iteration(0)
                    with dve.Fori(1, LAST) as it:
                        iteration(it)
                    iteration(LAST)

        choices_in = [sem(f"choices_in{i}") for i in range(4)]
        choices_added = sem("choices_added")
        with ExitStack() as scope, nc.Block() as block:
            choice = [scope.enter_context(nc.sbuf_tensor(f"choice{i}", [P, TOPK, D], F32)) for i in range(4)]
            choice_tiles = choice_rows.rearrange("(t p k) d -> t p (k d)", p=P, k=TOPK)

            @block.sync
            def _(sp):
                for t in range(NT):
                    if t >= 4:
                        sp.wait_ge(choices_added, TOPK * (t - 3))
                    sp.dma_start(choice[t % 4][:].rearrange("p k d -> p (k d)"), choice_tiles[t]).then_inc(choices_in[t % 4], 16)

            @block.vector
            def _(dve):
                for t in range(NT):
                    dve.wait_ge(choices_in[t % 4], 16 * (t // 4 + 1))
                    for k in range(TOPK):
                        if t or k:
                            dve.wait_ge(choices_added, TOPK * t + k)
                        dve.scalar_tensor_tensor(out=xres[:, t, :], in0=choice[t % 4][:, k, :], scalar=gate6[:, t, k:k + 1],
                                                 in1=xres[:, t, :], op0=ALU.mult, op1=ALU.add).then_inc(choices_added, 1)

        early.close()
        nc.clear_and_free_semaphores(signals)
        nc.all_engine_barrier()
        mid = whole.enter_context(ExitStack())
        def sbm(name, shape, dt=F32):
            return mid.enter_context(nc.sbuf_tensor(name, shape, dt))
        mix_hi = sbm("mix_hi", [P, KC, D], F16)
        mix_lo = sbm("mix_lo", [P, KC, D], F16)
        mix_bias = sbm("mix_bias", [2, D], F16)
        mask_rows = sbm("mask_rows", [P, TPB, S])
        mask_keys = sbm("mask_keys", [P, B, S])

        weights_in = sem("weights_in")
        ones_set = sem("ones_set")
        prep = sem("prep")
        prep_hi = sem("prep_hi")
        halves_done = sem("halves_done")
        prep_tern = sem("prep_tern")
        tern_in = sem("tern_in")
        abs_done = sem("abs_done")
        total_ready = sem("total_ready")
        rounded = sem("rounded")
        turned = sem("turned")
        turn_copied = sem("turn_copied")
        bias_moved = sem("bias_moved")

        with ExitStack() as scope, nc.Block() as block:
            def sbl(name, shape, dt=F32):
                return scope.enter_context(nc.sbuf_tensor(name, shape, dt))
            factor = sbl("factor", [P, 8, KC, D // 4])
            mix_f = sbl("mix_f", [P, KC, D])
            mask_words = sbl("mask_words", [P, TPB, S // 4], I32)
            keys_words = sbl("keys_words", [P, B, S // 4], I32)
            gate2_f = sbl("gate2_f", [P, KC, D])
            row_scratch = sbl("row_scratch", [1, 2, D])
            bias_halves = sbl("bias_halves", [1, 2, 2, D], F16)

            @block.sync
            def _(sp):
                sp.dma_start(gate2_f[:], L2_ffn_gate_w.rearrange("(p c) e -> p c e", c=KC)).then_inc(weights_in, 16)
                sp.dma_start(mask_words[:], mask_SxS2_bk1.rearrange("(t p) s -> p t s", p=P)).then_inc(weights_in, 16)
                for b in range(B):
                    sp.dma_start(keys_words[:, b, :], mask_BxS2_bf0[b:b + 1, :].to_broadcast([P, S // 4]))\
                        .then_inc(weights_in, 16)
                for i, bias in enumerate((L1_ffn_bias, L2_ffn_gate_b)):
                    sp.dma_start(row_scratch[0:1, i, :], bias.rearrange("(a d) -> a d", a=1)).then_inc(weights_in, 16)
                for q in range(4):
                    if q >= 1:
                        sp.wait_ge(prep, 7 * q)
                    for r in range(8):
                        quarter = L1_ffn_factors[r].rearrange("(p c) e -> p c e", c=KC)[:, :, q * P:(q + 1) * P]
                        sp.dma_start(factor[:, r, :, :], quarter).then_inc(weights_in, 16)
                sp.wait_ge(halves_done, 1)
                for i, dst in enumerate((mix_bias, gate2_bias)):
                    for half in range(2):
                        sp.dma_start(dst[half:half + 1, :], bias_halves[0:1, i, half, :]).then_inc(bias_moved, 16)
                sp.wait_ge(bias_moved, 64)

            @block.scalar
            def _(act):
                act.wait_ge(prep, 28)
                act.activation(mix_hi[:], mix_f[:], ACT.Copy, scale=G_SCALE / 8.0 ** 0.5).then_inc(prep_hi, 1)
                act.activation(gate2_hi[:], gate2_f[:], ACT.Copy, scale=G_SCALE).then_inc(prep_hi, 1)

            @block.vector
            def _(dve):
                steps = [0]

                def done(*instructions):
                    for ins in instructions:
                        ins.then_inc(prep, 1)
                        steps[0] += 1
                    dve.wait_ge(prep, steps[0])

                for q in range(4):
                    dve.wait_ge(weights_in, 16 * (8 + 8 * (q + 1)))
                    part = mix_f[:, :, q * P:(q + 1) * P]
                    done(dve.tensor_tensor(part, factor[:, 0, :, :], factor[:, 1, :, :], ALU.add))
                    for r in range(2, 8):
                        done(dve.tensor_tensor(part, part, factor[:, r, :, :], ALU.add))
                dve.memset(ones_h[:], 1.0).then_inc(ones_set, 1)
                dve.wait_ge(prep_hi, 2)
                done(dve.scalar_tensor_tensor(out=mix_lo[:], in0=mix_f[:], scalar=G_SCALE / 8.0 ** 0.5,
                                              in1=mix_hi[:], op0=ALU.mult, op1=ALU.subtract),
                     dve.scalar_tensor_tensor(out=gate2_lo[:], in0=gate2_f[:], scalar=G_SCALE, in1=gate2_hi[:],
                                              op0=ALU.mult, op1=ALU.subtract))
                for i in range(2):
                    row = row_scratch[0:1, i, :]
                    done(dve.tensor_scalar(bias_halves[0:1, i, 0, :], row, G_SCALE, None, ALU.mult))
                    done(dve.scalar_tensor_tensor(out=bias_halves[0:1, i, 1, :], in0=row, scalar=G_SCALE,
                                                  in1=bias_halves[0:1, i, 0, :], op0=ALU.mult, op1=ALU.subtract))
                dve.sem_inc(halves_done, 1)
                done(dve.tensor_scalar(mask_rows[:], mask_words[:].bitcast(U8), MASKED, None, ALU.mult),
                     dve.tensor_scalar(mask_keys[:], keys_words[:].bitcast(U8), MASKED, None, ALU.mult))

        with ExitStack() as scope, nc.Block() as block:
            def sbl(name, shape, dt=F32):
                return scope.enter_context(nc.sbuf_tensor(name, shape, dt))
            tern_f = [sbl(f"tern_f{i}", [P, 8, D]) for i in range(2)]
            tern_b = sbl("tern_b", [P, 8, D], BF16)
            abs_sum = sbl("abs_sum", [P, 2])
            pA = psum_banks(scope, "prepA", 1)[0]
            pB = psum_banks(scope, "prepB", 4, BF16)

            @block.sync
            def _(sp):
                sp.dma_start(tern_f[0][:], L3_ffn_w_up.rearrange("(o p) i -> p o i", p=P)).then_inc(tern_in, 16)
                sp.dma_start(tern_f[1][:].rearrange("p (o j) i -> p o (j i)", o=4),
                             L3_ffn_w_down.rearrange("(o p) i -> p o i", p=P)).then_inc(tern_in, 16)

            @block.vector
            def _(dve):
                steps = [0]

                def done(*instructions):
                    for ins in instructions:
                        ins.then_inc(prep_tern, 1)
                        steps[0] += 1
                    dve.wait_ge(prep_tern, steps[0])

                for i in range(2):
                    dve.wait_ge(tern_in, 32)
                    flat = tern_f[i][:].rearrange("p o i -> p (o i)")
                    dve.tensor_reduce(abs_sum[:, i:i + 1], flat, AX.X, ALU.add, apply_absolute_value=True)\
                        .then_inc(abs_done, 1)
                    dve.wait_ge(total_ready, i + 1)
                    mean = tern[:, 2 * i + 1:2 * i + 2]
                    done(dve.tensor_scalar(mean, pA[:, i:i + 1], 1.0 / (IUP * D), 1e-5, ALU.mult, ALU.max))
                    done(dve.reciprocal(tern[:, 2 * i:2 * i + 1], mean))
                    done(dve.tensor_scalar(flat, flat, tern[:, 2 * i:2 * i + 1], 1.0, ALU.mult, ALU.min))
                    done(dve.tensor_scalar(flat, flat, -1.0, MAGIC, ALU.max, ALU.add))
                    dve.tensor_scalar(tern_b[:].rearrange("p o i -> p (o i)"), flat, MAGIC, None, ALU.subtract)\
                        .then_inc(rounded, 1)
                    for k in range(8):
                        dve.wait_ge(turned, 8 * i + k + 1)
                        dst = (up_t[:, :, k * P:(k + 1) * P], dn_t[:, k, :].rearrange("p (c o) -> p c o", c=4))[i]
                        dve.tensor_copy(dst, pB[k % 4][:, 0:D].rearrange("p (c o) -> p c o", c=4))\
                            .then_inc(turn_copied, 1)

            @block.tensor
            def _(pe):
                for i in range(2):
                    pe.wait_ge(abs_done, i + 1)
                    pe.matmul(pA[:, i:i + 1], ones[:], abs_sum[:, i:i + 1], start=True, stop=True)\
                        .then_inc(total_ready, 1)
                    pe.wait_ge(rounded, i + 1)
                    for k in range(8):
                        if 8 * i + k >= 4:
                            pe.wait_ge(turn_copied, 8 * i + k - 3)
                        for c in range(4):
                            if i == 0:
                                src = tern_b[:, k, c::KC]
                            else:
                                src = tern_b[:].rearrange("p (o j) i -> p o (j i)", o=4)[:, c, k::8]
                            m = pe.transpose(pB[k % 4][:, c * P:(c + 1) * P], src, ident_b[:])
                        m.then_inc(turned, 1)

        def transposed_split(pe, source, banks, ready):
            for c in range(KC):
                for t in range(TPB):
                    m = pe.transpose(banks[c][:, t * P:(t + 1) * P], source[:, t, c::KC], ident[:])
                m.then_inc(ready, 1)

        def dense(pe, out, t, a_hi, a_lo, w_hi, w_lo, bias):
            tok = slice(t * P, (t + 1) * P)
            for c in range(KC):
                split_matmul(pe, out, a_hi[:, c, tok], a_lo[:, c, tok], w_hi[:, c, :], w_lo[:, c, :], c == 0, False)
            return pe.matmul(out, ones_h[:], bias[:], start=False, stop=True)

        learned_copied = sem("learned_copied")
        learned_turned = sem("learned_turned")
        l1_scale_done = sem("l1_scale_done")
        l1_half = sem("l1_half")
        x3_done = sem("x3_done")
        n3_done = sem("n3_done")
        n3T_ready = sem("n3T_ready")
        n3T_hi_done = sem("n3T_hi_done")
        n3T_lo_done = sem("n3T_lo_done")
        mixed_ready = sem("mixed_ready")
        x4_done = sem("x4_done")
        n4_done = sem("n4_done")
        scores2_ready = sem("scores2_ready")
        scores2_step = sem("scores2_step")
        max2_done = sem("max2_done")
        negmax2_done = sem("negmax2_done")
        exp2_done = sem("exp2_done")
        recip2_done = sem("recip2_done")
        x5_done = sem("x5_done")

        with ExitStack() as scope:
            def sbl(name, shape, dt=F32):
                return scope.enter_context(nc.sbuf_tensor(name, shape, dt))
            l1_in = Norm("l1_in", sbl, sem, 1e-5)
            l1_mid = Norm("l1_mid", sbl, sem, 1e-5)
            l2_in = Norm("l2_in", sbl, sem, 1e-5)
            xw = sbl("xw", [P, TPB, D])
            lw = sbl("lw", [P, TPB, S])
            nrm = sbl("nrm", [P, TPB, D])
            nT_hi = sbl("nT_hi", [P, KC, S], F16)
            nT_lo = sbl("nT_lo", [P, KC, S], F16)
            mul1 = sbl("mul1", [P, TPB])
            add1 = sbl("add1", [P, TPB])
            max2 = sbl("max2", [P, TPB])
            negmax2 = sbl("negmax2", [P, TPB])
            sum2 = sbl("sum2", [P, TPB])
            recip2 = sbl("recip2", [P, TPB])
            live2 = sbl("live2", [P, TPB])
            pT = psum_banks(scope, "tail1T", 4)
            pG = psum_banks(scope, "tail1G", 4)
            with nc.Fori(0, B) as b, nc.Block() as block:
                @block.tensor
                def _(pe):
                    pe.wait_ge(learned_copied, TPB * b + TPB)
                    for t in range(TPB):
                        for j in range(TPB):
                            m = pe.transpose(pG[t][:, j * P:(j + 1) * P], lw[:, j, t * P:(t + 1) * P], ident[:])
                        m.then_inc(learned_turned, 1)
                    pe.wait_ge(n3_done, TPB * b + TPB)
                    transposed_split(pe, nrm, pT, n3T_ready)
                    pe.wait_ge(n3T_lo_done, KC * b + KC)
                    for t in range(TPB):
                        dense(pe, pG[t][:], t, nT_hi, nT_lo, mix_hi, mix_lo, mix_bias).then_inc(mixed_ready, 1)
                    for t in range(TPB):
                        rows, cols = bass.ds(b * S + t * P, P), bass.ds(b * S, S)
                        split_matmul(pe, pT[t][:], proj_hi[2][:, rows], proj_lo[2][:, rows], proj_hi[3][:, cols],
                                     proj_lo[3][:, cols], True, True).then_inc(scores2_ready, 1)

                @block.gpsimd
                def _(pool):
                    for norm in (l1_in, l1_mid, l2_in):
                        norm.on_gpsimd(pool, minus_half, b)

                @block.scalar
                def _(act):
                    for t in range(TPB):
                        act.activation(lw[:, t, :], tile_of(learned, b * TPB + t), ACT.Copy).then_inc(learned_copied, 1)
                    for c in range(KC):
                        act.wait_ge(n3T_ready, KC * b + c + 1)
                        act.activation(nT_hi[:, c, :], pT[c][:], ACT.Copy).then_inc(n3T_hi_done, 1)
                    act.wait_ge(negmax2_done, b + 1)
                    for t in range(TPB):
                        act.activation(lw[:, t, :], lw[:, t, :], ACT.Exp, bias=negmax2[:, t:t + 1],
                                       accum_out=sum2[:, t:t + 1]).then_inc(exp2_done, 1)

                @block.vector
                def _(dve):
                    l1_in.on_vector(dve, lambda t: tile_of(xres, b * TPB + t), b, None)
                    dve.tensor_scalar(mul1[:], l1_in.rstd[:], gam[:, 3:4], 1.0, ALU.mult, ALU.add).then_inc(l1_scale_done, 1)
                    dve.tensor_scalar(add1[:], l1_in.shift[:], gam[:, 3:4], None, ALU.mult).then_inc(l1_scale_done, 1)
                    dve.wait_ge(l1_scale_done, 2 * b + 2)
                    for t in range(TPB):
                        dve.wait_ge(learned_copied, TPB * b + t + 1)
                        dve.scalar_tensor_tensor(out=xw[:, t, :], in0=tile_of(xres, b * TPB + t), scalar=mul1[:, t:t + 1],
                                                 in1=lw[:, t, :], op0=ALU.mult, op1=ALU.add).then_inc(l1_half, 1)
                    dve.wait_ge(l1_half, TPB * b + TPB)
                    for t in range(TPB):
                        dve.wait_ge(learned_turned, TPB * b + t + 1)
                        dve.scalar_tensor_tensor(out=xw[:, t, :], in0=xw[:, t, :], scalar=add1[:, t:t + 1],
                                                 in1=pG[t][:], op0=ALU.add, op1=ALU.add).then_inc(x3_done, 1)
                    l1_mid.on_vector(dve, lambda t: xw[:, t, :], b, (x3_done, TPB * b + TPB))
                    for t in range(TPB):
                        dve.tensor_scalar(nrm[:, t, :], xw[:, t, :], l1_mid.rstd[:, t:t + 1],
                                          l1_mid.shift[:, t:t + 1], ALU.mult, ALU.add).then_inc(n3_done, 1)
                    for c in range(KC):
                        dve.wait_ge(n3T_hi_done, KC * b + c + 1)
                        dve.tensor_tensor(nT_lo[:, c, :], pT[c][:], nT_hi[:, c, :], ALU.subtract).then_inc(n3T_lo_done, 1)
                    for t in range(TPB):
                        dve.wait_ge(mixed_ready, TPB * b + t + 1)
                        dve.scalar_tensor_tensor(out=xw[:, t, :], in0=pG[t][:], scalar=1.0 / G_SCALE,
                                                 in1=xw[:, t, :], op0=ALU.mult, op1=ALU.add).then_inc(x4_done, 1)
                    l2_in.on_vector(dve, lambda t: xw[:, t, :], b, (x4_done, TPB * b + TPB))
                    for t in range(TPB):
                        dve.tensor_scalar(nrm[:, t, :], xw[:, t, :], l2_in.rstd[:, t:t + 1],
                                          l2_in.shift[:, t:t + 1], ALU.mult, ALU.add).then_inc(n4_done, 1)
                    dve.wait_ge(n4_done, TPB * b + TPB)
                    for t in range(TPB):
                        dve.wait_ge(scores2_ready, TPB * b + t + 1)
                        dve.scalar_tensor_tensor(out=lw[:, t, :], in0=pT[t][:], scalar=C ** -0.5, in1=nrm[:, t, :],
                                                 op0=ALU.mult, op1=ALU.mult).then_inc(scores2_step, 1)
                    dve.wait_ge(scores2_step, 2 * TPB * b + TPB)
                    for t in range(TPB):
                        dve.tensor_tensor(lw[:, t, :], lw[:, t, :], tile_of(mask_keys, b), ALU.add).then_inc(scores2_step, 1)
                    hold(dve, scores2_step, 2 * TPB * b + 2 * TPB)
                    for t in range(TPB):
                        dve.tensor_tensor_reduce(lw[:, t, :], lw[:, t, :], mask_rows[:, t, :], 1.0, NEG, ALU.add,
                                                 ALU.max, max2[:, t:t + 1]).then_inc(max2_done, 1)
                    dve.wait_ge(max2_done, TPB * b + TPB)
                    dve.tensor_scalar(negmax2[:], max2[:], -1.0, None, ALU.mult).then_inc(negmax2_done, 1)
                    dve.tensor_scalar(live2[:], max2[:], 0.5 * MASKED, None, ALU.is_ge).then_inc(recip2_done, 1)
                    dve.wait_ge(recip2_done, 4 * b + 1)
                    dve.wait_ge(exp2_done, TPB * b + TPB)
                    dve.tensor_tensor(sum2[:], sum2[:], live2[:], ALU.mult).then_inc(recip2_done, 1)
                    dve.wait_ge(recip2_done, 4 * b + 2)
                    dve.reciprocal(recip2[:], sum2[:]).then_inc(recip2_done, 1)
                    dve.wait_ge(recip2_done, 4 * b + 3)
                    dve.tensor_tensor(recip2[:], recip2[:], live2[:], ALU.mult).then_inc(recip2_done, 1)
                    dve.wait_ge(recip2_done, 4 * b + 4)
                    for t in range(TPB):
                        dve.scalar_tensor_tensor(out=tile_of(xres, b * TPB + t), in0=lw[:, t, :],
                                                 scalar=recip2[:, t:t + 1], in1=xw[:, t, :], op0=ALU.mult,
                                                 op1=ALU.add).then_inc(x5_done, 1)
        mid.close()
        middle.close()
        bc_rows = sb("bc_rows", [P, B, D])
        ctxs = sb("ctxs_again", [P, NT, C])
        out_gamma = sb("out_gamma", [P, D])
        out_beta = sb("out_beta", [P, D])
        values_hi = sb("values_hi", [P, NT, KVH, DH + 1], F16)
        values_lo = sb("values_lo", [P, NT, KVH, DH + 1], F16)

        th_in = sem("th_in")
        last_in = sem("last_in")
        values_done = sem("values_done")
        ctx_again = sem("ctx_again")
        th = sem("th")
        th_rstd = sem("th_rstd")
        last_ready = sem("last_ready")
        last_turned = sem("last_turned")
        agg_ready = sem("agg_ready")
        thn = sem("thn")
        sum_ready = sem("sum_ready")
        th_rstd_step = sem("th_rstd_step")
        d1_ready = sem("d1_ready")
        gelu_in = sem("gelu_in")
        gelu_done = sem("gelu_done")
        d2_ready = sem("d2_ready")
        bc_ready = sem("bc_ready")
        bc_done = sem("bc_done")
        HC = HID // P
        with ExitStack() as scope, nc.Block() as block:
            def sbl(name, shape, dt=F32):
                return scope.enter_context(nc.sbuf_tensor(name, shape, dt))
            d1_w = sbl("d1_w", [P, KC, HID])
            d2_w = sbl("d2_w", [P, HC, D])
            agg_w = sbl("agg_w", [P, KC, D])
            bc_w = sbl("bc_w", [P, KC, D])
            bc_b = sbl("bc_b", [P, D])
            d1_b = sbl("d1_b", [P, HC])
            vecs = sbl("vecs", [P, 4, KC])
            last = sbl("last", [B, D])
            in_rows = sbl("in_rows", [B, 2, D])
            last_stats = sbl("last_stats", [B, 6])
            last_mv = sbl("last_mv", [B, 2])
            last_ve = sbl("last_ve", [B, 1])
            last_rstd = sbl("last_rstd", [B, 1])
            lastT = sbl("lastT", [P, KC, B])
            thought = sbl("thought", [P, KC, B])
            part = sbl("part", [P, B])
            mean = sbl("mean", [P, B])
            centred = sbl("centred", [P, KC, B])
            square = sbl("square", [P, KC, B])
            ve = sbl("ve", [P, B])
            rstd = sbl("rstd", [P, B])
            tn = sbl("tn", [P, KC, B])
            hid_f = sbl("hid_f", [P, HC, B])
            hid = sbl("hid", [P, HC, B])
            th_rep = sbl("th_rep", [P, KC, B, P])
            pL = psum_banks(scope, "thL", 1)[0]
            pA = psum_banks(scope, "thA", 1)[0]
            pS = psum_banks(scope, "thS", 1)[0]
            pH = psum_banks(scope, "thH", 1)[0]
            pD = psum_banks(scope, "thD", 1)[0]
            pB = psum_banks(scope, "thB", 2)

            @block.sync
            def _(sp):
                sp.dma_start(ctxs[:], ctx_d).then_inc(ctx_again, 16)
                for b in range(B):
                    sp.dma_start(last[b:b + 1, :], xres[P - 1:P, TPB * b + TPB - 1, :]).then_inc(last_in, 16)
                for i, v in enumerate((L2_ffn_in_gamma, L2_ffn_in_beta)):
                    sp.dma_start(in_rows[:, i, :], v.rearrange("(a d) -> a d", a=1).to_broadcast([B, D])).then_inc(last_in, 16)
                sp.dma_start(agg_w[:], L2_ffn_agg_w.rearrange("(p c) e -> p c e", c=KC)).then_inc(last_in, 16)
                for i, v in enumerate((L2_ffn_agg_b, L2_ffn_pn_gamma, L2_ffn_pn_beta, L2_ffn_d2_b)):
                    sp.dma_start(vecs[:, i, :], v.rearrange("(p c) -> p c", c=KC)).then_inc(last_in, 16)
                sp.dma_start(d1_b[:], L2_ffn_d1_b.rearrange("(p m) -> p m", m=HC)).then_inc(last_in, 16)
                sp.dma_start(d1_w[:], L2_ffn_d1_w.rearrange("(p c) e -> p c e", c=KC)).then_inc(th_in, 16)
                sp.dma_start(d2_w[:], L2_ffn_d2_w.rearrange("(p m) e -> p m e", m=HC)).then_inc(th_in, 16)
                sp.dma_start(bc_w[:], L2_ffn_bc_w.rearrange("(p c) e -> p c e", c=KC)).then_inc(th_in, 16)
                for dst, v in ((bc_b, L2_ffn_bc_b), (out_gamma, L2_ffn_out_gamma), (out_beta, L2_ffn_out_beta)):
                    sp.dma_start(dst[:], v.rearrange("(a d) -> a d", a=1).to_broadcast([P, D])).then_inc(th_in, 16)
                sp.wait_ge(th_in, 96)

            @block.gpsimd
            def _(pool):
                heads = ctxs[:].rearrange("p t (g d) -> p t g d", d=DH)
                pool.wait_ge(ctx_again, 16)
                pool.memset(values_hi[:, :, :, DH:DH + 1], 1.0).then_inc(values_done, 1)
                pool.memset(values_lo[:, :, :, DH:DH + 1], 0.0).then_inc(values_done, 1)
                pool.tensor_copy(values_hi[:, :, :, 0:DH], heads).then_inc(values_done, 1)
                pool.wait_ge(values_done, 3)
                pool.tensor_tensor(values_lo[:, :, :, 0:DH], heads, values_hi[:, :, :, 0:DH], ALU.subtract)\
                    .then_inc(values_done, 1)
                for i in range(2):
                    pool.wait_ge(th, 4 * i + 3)
                    pool.tensor_tensor(last_rstd[:], last_ve[:], minus_half[0:B, 0:1], ALU.pow).then_inc(th_rstd, 1)
                with pool.Fori(0, K_STEPS) as k:
                    pool.wait_ge(thn, 11 * k + 6)
                    pool.tensor_tensor(rstd[:], ve[:], minus_half[:, 0:B], ALU.pow).then_inc(th_rstd_step, 1)

            @block.tensor
            def _(pe):
                pe.wait_ge(last_ready, 1)
                for c in range(KC):
                    m = pe.transpose(pL[:, c * B:(c + 1) * B], last[:, c::KC], ident[0:B, 0:B])
                m.then_inc(last_turned, 1)
                pe.wait_ge(th, 11)
                for o in range(KC):
                    for c in range(KC):
                        m = pe.matmul(pA[:, o * B:(o + 1) * B], agg_w[:, c, o::KC], lastT[:, c, :],
                                      start=c == 0, stop=c == KC - 1)
                m.then_inc(agg_ready, 1)
                pe.wait_ge(th_in, 96)
                with pe.Fori(0, K_STEPS) as k:
                    pe.wait_ge(thn, 11 * k + 1)
                    pe.matmul(pS[:, 0:B], ones[:], part[:], start=True, stop=True).then_inc(sum_ready, 1)
                    pe.wait_ge(thn, 11 * k + 5)
                    pe.matmul(pS[:, B:2 * B], ones[:], part[:], start=True, stop=True).then_inc(sum_ready, 1)
                    pe.wait_ge(thn, 11 * k + 9)
                    for m in range(HC):
                        for c in range(KC):
                            mm = pe.matmul(pH[:, m * B:(m + 1) * B], d1_w[:, c, m::HC], tn[:, c, :],
                                           start=c == 0, stop=c == KC - 1)
                    mm.then_inc(d1_ready, 1)
                    pe.wait_ge(gelu_done, k + 1)
                    for o in range(KC):
                        for m in range(HC):
                            mm = pe.matmul(pD[:, o * B:(o + 1) * B], d2_w[:, m, o::KC], hid[:, m, :],
                                           start=m == 0, stop=m == HC - 1)
                    mm.then_inc(d2_ready, 1)
                pe.wait_ge(bc_ready, 1)
                for b in range(B):
                    if b >= 2:
                        pe.wait_ge(bc_done, b - 1)
                    for c in range(KC):
                        mm = pe.matmul(pB[b % 2][:], th_rep[:, c, b, :], bc_w[:, c, :], start=c == 0, stop=c == KC - 1)
                    mm.then_inc(bc_ready, 1)

            @block.scalar
            def _(act):
                with act.Fori(0, K_STEPS) as k:
                    act.wait_ge(gelu_in, k + 1)
                    act.activation(hid[:], hid_f[:], ACT.Gelu).then_inc(gelu_done, 1)

            @block.vector
            def _(dve):
                steps = [0]

                def done(*instructions):
                    for ins in instructions:
                        ins.then_inc(th, 1)
                        steps[0] += 1
                    dve.wait_ge(th, steps[0])

                dve.wait_ge(last_in, 16 * 12)
                for i, eps in enumerate((1e-5, 1e-6)):
                    done(dve.bn_stats(last_stats[:], last[:]))
                    done(dve.bn_aggr(last_mv[:], last_stats[:]))
                    done(dve.tensor_scalar(last_ve[:], last_mv[:, 1:2], eps, None, ALU.add))
                    dve.wait_ge(th_rstd, i + 1)
                    done(dve.tensor_scalar(last[:], last[:], last_mv[:, 0:1], last_rstd[:, 0:1], ALU.subtract, ALU.mult))
                done(dve.tensor_tensor(last[:], last[:], in_rows[:, 0, :], ALU.mult))
                done(dve.tensor_tensor(last[:], last[:], in_rows[:, 1, :], ALU.add))
                dve.sem_inc(last_ready, 1)
                dve.wait_ge(last_turned, 1)
                done(dve.tensor_copy(lastT[:].rearrange("p c b -> p (c b)"), pL[:, 0:KC * B]))
                dve.wait_ge(agg_ready, 1)

                def vec(i):
                    return vecs[:, i, :].unsqueeze(2).to_broadcast([P, KC, B])

                def per_batch(v):
                    return v[:].unsqueeze(1).to_broadcast([P, KC, B])

                done(dve.tensor_tensor(thought[:], pA[:, 0:KC * B].rearrange("p (c b) -> p c b", b=B), vec(0), ALU.add))
                with dve.Fori(0, K_STEPS) as k:
                    n = [0]

                    def step(ins):
                        ins.then_inc(thn, 1)
                        n[0] += 1
                        hold(dve, thn, 11 * k + n[0])

                    step(dve.tensor_reduce(part[:], thought[:].rearrange("p c b -> p b c"), AX.X, ALU.add))
                    dve.wait_ge(sum_ready, 2 * k + 1)
                    step(dve.tensor_scalar(mean[:], pS[:, 0:B], 1.0 / D, None, ALU.mult))
                    step(dve.tensor_tensor(centred[:], thought[:], per_batch(mean), ALU.subtract))
                    step(dve.tensor_tensor(square[:], centred[:], centred[:], ALU.mult))
                    step(dve.tensor_reduce(part[:], square[:].rearrange("p c b -> p b c"), AX.X, ALU.add))
                    dve.wait_ge(sum_ready, 2 * k + 2)
                    step(dve.tensor_scalar(ve[:], pS[:, B:2 * B], 1.0 / D, 1e-6, ALU.mult, ALU.add))
                    dve.wait_ge(th_rstd_step, k + 1)
                    step(dve.tensor_tensor(tn[:], centred[:], per_batch(rstd), ALU.mult))
                    step(dve.tensor_tensor(tn[:], tn[:], vec(1), ALU.mult))
                    step(dve.tensor_tensor(tn[:], tn[:], vec(2), ALU.add))
                    dve.wait_ge(d1_ready, k + 1)
                    dve.tensor_tensor(hid_f[:], pH[:, 0:HC * B].rearrange("p (m b) -> p m b", b=B),
                                      d1_b[:].unsqueeze(2).to_broadcast([P, HC, B]), ALU.add).then_inc(gelu_in, 1)
                    dve.wait_ge(d2_ready, k + 1)
                    step(dve.tensor_tensor(thought[:], thought[:], pD[:, 0:KC * B].rearrange("p (c b) -> p c b", b=B),
                                           ALU.add))
                    step(dve.tensor_tensor(thought[:], thought[:], vec(3), ALU.add))
                dve.tensor_copy(th_rep[:], thought[:].unsqueeze(3).to_broadcast([P, KC, B, P])).then_inc(bc_ready, 1)
                for b in range(B):
                    dve.wait_ge(bc_ready, b + 2)
                    dve.tensor_tensor(bc_rows[:, b, :], pB[b % 2][:], bc_b[:], ALU.add).then_inc(bc_done, 1)

        PAIR = QH // 2
        SLOT = 64
        ROWS = 3 * DH
        x5_copied = sem("x5_copied")
        n5_done = sem("n5_done")
        n5T_ready = sem("n5T_ready")
        n5T_hi_done = sem("n5T_hi_done")
        n5T_lo_done = sem("n5T_lo_done")
        gate_ready = sem("gate_ready")
        gate_done = sem("gate_done")
        gated = sem("gated")
        x6_step = sem("x6_step")
        n6_done = sem("n6_done")
        q_hi_done = sem("q_hi_done")
        q_lo_done = sem("q_lo_done")
        q_pad_done = sem("q_pad_done")
        k_hi_done = sem("k_hi_done")
        k_lo_done = sem("k_lo_done")
        kT_ready = sem("kT_ready")
        kT_done = sem("kT_done")
        qT_ready = sem("qT_ready")
        qT_done = sem("qT_done")
        qT_odd_done = sem("qT_odd_done")
        s_ready = sem("s_ready")
        max_done = sem("max_done")
        negmax_done = sem("negmax_done")
        negmaxT_ready = sem("negmaxT_ready")
        negmaxT_done = sem("negmaxT_done")
        negmax_moved = sem("negmax_moved")
        sT_ready = sem("sT_ready")
        exp_done = sem("exp_done")
        probs_hi0_done = sem("probs_hi0_done")
        probs_hi1_done = sem("probs_hi1_done")
        probs_lo_done = sem("probs_lo_done")
        pv_ready = sem("pv_ready")
        recip_done = sem("recip_done")
        weighed_done = sem("weighed_done")
        x7_done = sem("x7_done")
        n7_done = sem("n7_done")
        amax_done = sem("amax_done")
        scale_step = sem("scale_step")
        quant_step = sem("quant_step")
        q7_done = sem("q7_done")
        q7T_ready = sem("q7T_ready")
        q7T_done = sem("q7T_done")
        hid_ready = sem("hid_ready")
        relu_done = sem("relu_done")
        hmax_done = sem("hmax_done")
        hscale_step = sem("hscale_step")
        hsq_done = sem("hsq_done")
        hquant_step = sem("hquant_step")
        hq_done = sem("hq_done")
        hqT_ready = sem("hqT_ready")
        hqT_done = sem("hqT_done")
        y_ready = sem("y_ready")
        x8_done = sem("x8_done")
        stored = sem("stored")
        k_ones_done = sem("k_ones_done")

        with ExitStack() as scope:
            def sbl(name, shape, dt=F32, scope=scope):
                return scope.enter_context(nc.sbuf_tensor(name, shape, dt))
            l2_ffn = Norm("l2_ffn", sbl, sem, 1e-5)
            l2_out = Norm("l2_out", sbl, sem, 1e-6)
            l3_in = Norm("l3_in", sbl, sem, 1e-5)
            l3_mid = Norm("l3_mid", sbl, sem, 1e-5)
            xw = sbl("xw2", [P, TPB, D])
            nrm = sbl("nrm2", [P, TPB, D])
            with nc.Fori(0, B) as b:
                attn = ExitStack()
                def sba(name, shape, dt=F32):
                    return attn.enter_context(nc.sbuf_tensor(name, shape, dt))
                q_rows = sba("q_rows", [P, TPB, QH, SLOT], F16)
                k_rows = sba("k_rows", [P, TPB, KVH, 2, SLOT], F16)
                qT = sba("qT", [P, PAIR, S], F16)
                kT = sba("kT", [P, KVH, S], F16)
                maxes = sba("maxes", [P, TPB, QH])
                negmax = sba("negmax", [P, TPB, QH], F16)
                negmaxT = sba("negmaxT", [QH, S], F16)

                with ExitStack() as inner, nc.Block() as block:
                    gate = inner.enter_context(nc.sbuf_tensor("gate", [P, TPB, D], F32))
                    n5T_hi = inner.enter_context(nc.sbuf_tensor("n5T_hi", [P, KC, S], F16))
                    n5T_lo = inner.enter_context(nc.sbuf_tensor("n5T_lo", [P, KC, S], F16))
                    pT = psum_banks(inner, "gateT", 4)
                    pG = psum_banks(inner, "gateG", 4)

                    @block.gpsimd
                    def _(pool):
                        l2_ffn.on_gpsimd(pool, minus_half, b)
                        l2_out.on_gpsimd(pool, minus_half, b)
                        l3_in.on_gpsimd(pool, minus_half, b)
                        pool.memset(q_rows[:, :, :, ROWS:SLOT], 0.0).then_inc(q_pad_done, 1)
                        pool.memset(k_rows[:, :, :, :, ROWS:SLOT], 0.0).then_inc(q_pad_done, 1)
                        for t in range(TPB):
                            src = ctxs[:, bass.ds(b * TPB + t, 1), :].rearrange("p a (g d) -> p (a g) d", d=DH)
                            for dup in range(2):
                                for i in range(2):
                                    pool.tensor_copy(k_rows[:, t, :, dup, i * DH:(i + 1) * DH], src).then_inc(k_hi_done, 1)
                        hold(pool, q_pad_done, 2 * b + 2)
                        pool.memset(k_rows[:, :, :, :, ROWS:ROWS + 1], 1.0).then_inc(k_ones_done, 1)
                        hold(pool, k_hi_done, 16 * b + 16)
                        for t in range(TPB):
                            src = ctxs[:, bass.ds(b * TPB + t, 1), :].rearrange("p a (g d) -> p (a g) d", d=DH)
                            for dup in range(2):
                                pool.tensor_tensor(k_rows[:, t, :, dup, 2 * DH:ROWS], src, k_rows[:, t, :, dup, 0:DH],
                                                   ALU.subtract).then_inc(k_lo_done, 1)

                    @block.tensor
                    def _(pe):
                        pe.wait_ge(n5_done, TPB * b + TPB)
                        transposed_split(pe, nrm, pT, n5T_ready)
                        pe.wait_ge(n5T_lo_done, KC * b + KC)
                        for t in range(TPB):
                            dense(pe, pG[t][:], t, n5T_hi, n5T_lo, gate2_hi, gate2_lo, gate2_bias)\
                                .then_inc(gate_ready, 1)
                        pe.wait_ge(k_lo_done, 8 * b + 8)
                        pe.wait_ge(k_ones_done, b + 1)
                        for g in range(KVH):
                            bank = pT[g // 2][:].bitcast(F16)
                            for t in range(TPB):
                                at = (g % 2) * S + t * P
                                m = pe.transpose(bank[:, at:at + P], k_rows[:, t, g, :, :].rearrange("p e r -> p (e r)"),
                                                 ident_h[:])
                            if g % 2:
                                m.then_inc(kT_ready, 1)

                    @block.scalar
                    def _(act):
                        for t in range(TPB):
                            act.activation(xw[:, t, :], tile_of(xres, b * TPB + t), ACT.Copy).then_inc(x5_copied, 1)
                        for c in range(KC):
                            act.wait_ge(n5T_ready, KC * b + c + 1)
                            act.activation(n5T_hi[:, c, :], pT[c][:], ACT.Copy).then_inc(n5T_hi_done, 1)
                        for t in range(TPB):
                            act.wait_ge(gate_ready, TPB * b + t + 1)
                            act.activation(gate[:, t, :], pG[t][:], ACT.Sigmoid, scale=1.0 / G_SCALE).then_inc(gate_done, 1)
                        for i in range(KVH // 2):
                            act.wait_ge(kT_ready, KVH // 2 * b + i + 1)
                            act.activation(kT[:, 2 * i:2 * i + 2, :].rearrange("p g s -> p (g s)"),
                                           pT[i][:].bitcast(F16), ACT.Copy).then_inc(kT_done, 1)
                        for t in range(TPB):
                            act.wait_ge(n6_done, TPB * b + t + 1)
                            src = nrm[:, t, :].rearrange("p (h d) -> p h d", d=DH)
                            act.activation(q_rows[:, t, :, 0:DH], src, ACT.Copy).then_inc(q_hi_done, 1)
                            act.activation(q_rows[:, t, :, 2 * DH:ROWS], src, ACT.Copy).then_inc(q_hi_done, 1)

                    @block.vector
                    def _(dve):
                        l2_ffn.on_vector(dve, lambda t: tile_of(xres, b * TPB + t), b, None)
                        for t in range(TPB):
                            dve.tensor_scalar(nrm[:, t, :], tile_of(xres, b * TPB + t), l2_ffn.rstd[:, t:t + 1],
                                              l2_ffn.shift[:, t:t + 1], ALU.mult, ALU.add).then_inc(n5_done, 1)
                        for c in range(KC):
                            dve.wait_ge(n5T_hi_done, KC * b + c + 1)
                            dve.tensor_tensor(n5T_lo[:, c, :], pT[c][:], n5T_hi[:, c, :], ALU.subtract)\
                                .then_inc(n5T_lo_done, 1)
                        for t in range(TPB):
                            dve.wait_ge(gate_done, TPB * b + t + 1)
                            dve.tensor_tensor(gate[:, t, :], gate[:, t, :], tile_of(bc_rows, b), ALU.mult).then_inc(gated, 1)
                        dve.wait_ge(gated, 2 * TPB * b + TPB)
                        dve.tensor_tensor(gate[:], gate[:], nrm[:], ALU.add).then_inc(x6_step, 1)
                        l2_out.on_vector(dve, lambda t: gate[:, t, :], b, (x6_step, 4 * b + 1))
                        for t in range(TPB):
                            dve.tensor_scalar(gate[:, t, :], gate[:, t, :], l2_out.rstd[:, t:t + 1],
                                              l2_out.shift[:, t:t + 1], ALU.mult, ALU.add).then_inc(gated, 1)
                        hold(dve, gated, 2 * TPB * b + 2 * TPB)
                        gamma = out_gamma[:].unsqueeze(1).to_broadcast([P, TPB, D])
                        beta = out_beta[:].unsqueeze(1).to_broadcast([P, TPB, D])
                        dve.tensor_tensor(gate[:], gate[:], gamma, ALU.mult).then_inc(x6_step, 1)
                        dve.wait_ge(x5_copied, TPB * b + TPB)
                        dve.tensor_tensor(xw[:], xw[:], beta, ALU.add).then_inc(x6_step, 1)
                        dve.wait_ge(x6_step, 4 * b + 3)
                        dve.tensor_tensor(xw[:], xw[:], gate[:], ALU.add).then_inc(x6_step, 1)
                        l3_in.on_vector(dve, lambda t: xw[:, t, :], b, (x6_step, 4 * b + 4))
                        for t in range(TPB):
                            dve.tensor_scalar(nrm[:, t, :], xw[:, t, :], l3_in.rstd[:, t:t + 1],
                                              l3_in.shift[:, t:t + 1], ALU.mult, ALU.add).then_inc(n6_done, 1)
                        for t in range(TPB):
                            dve.wait_ge(q_hi_done, 2 * TPB * b + 2 * t + 1)
                            dve.tensor_tensor(q_rows[:, t, :, DH:2 * DH], nrm[:, t, :].rearrange("p (h d) -> p h d", d=DH),
                                              q_rows[:, t, :, 0:DH], ALU.subtract).then_inc(q_lo_done, 1)

                with ExitStack() as inner:
                    with nc.Block() as block:
                        pQ = psum_banks(inner, "qT", 8, F16)

                        @block.tensor
                        def _(pe):
                            for j in range(PAIR):
                                for t in range(TPB):
                                    at = (j % 2) * S + t * P
                                    m = pe.transpose(pQ[j // 2][:, at:at + P],
                                                     q_rows[:, t, 2 * j:2 * j + 2, :].rearrange("p e r -> p (e r)"),
                                                     ident_h[:])
                                if j % 2:
                                    m.then_inc(qT_ready, 1)

                        def copy_out(eng, i):
                            return (qT[:, 2 * i:2 * i + 2, :].rearrange("p j s -> p (j s)"), pQ[i][:])

                        @block.scalar
                        def _(act):
                            for i in range(0, 8, 2):
                                act.wait_ge(qT_ready, 8 * b + i + 1)
                                act.activation(*copy_out(act, i), ACT.Copy).then_inc(qT_done, 1)

                        @block.vector
                        def _(dve):
                            for i in range(1, 8, 2):
                                dve.wait_ge(qT_ready, 8 * b + i + 1)
                                dve.tensor_copy(*copy_out(dve, i)).then_inc(qT_odd_done, 1)

                def rows_of(head, n):
                    return slice(SLOT * (head % 2), SLOT * (head % 2) + n)

                with ExitStack() as inner, nc.Block() as block:
                    pS = [inner.enter_context(nc.psum_tensor(f"pS{i}", [P, TPB, S], F32)) for i in range(2)]

                    @block.tensor
                    def _(pe):
                        for h in range(QH):
                            if h >= 2:
                                pe.wait_ge(max_done, QH * b + h - 1)
                            r = rows_of(h, ROWS)
                            for t in range(TPB):
                                m = pe.matmul(pS[h % 2][:, t, :], qT[r, h // 2, t * P:(t + 1) * P],
                                              kT[r, h // 4, :], start=True, stop=True)
                            m.then_inc(s_ready, 1)
                        pe.wait_ge(negmax_done, b + 1)
                        for t in range(TPB):
                            m = pe.transpose(pS[0][:, 0, :].bitcast(F16)[0:QH, t * P:(t + 1) * P], negmax[:, t, :],
                                             ident_h[:])
                        m.then_inc(negmaxT_ready, 1)

                    @block.vector
                    def _(dve):
                        for h in range(QH):
                            dve.wait_ge(s_ready, QH * b + h + 1)
                            at = (h % 2) * PAIR + h // 2
                            dve.tensor_reduce(maxes[:, :, at:at + 1], pS[h % 2][:], AX.X, ALU.max).then_inc(max_done, 1)
                        dve.wait_ge(max_done, QH * b + QH)
                        dve.tensor_scalar(negmax[:], maxes[:], -1.0, None, ALU.mult).then_inc(negmax_done, 1)
                        dve.wait_ge(negmaxT_ready, b + 1)
                        dve.tensor_copy(negmaxT[:], pS[0][:, 0, :].bitcast(F16)[0:QH, 0:S]).then_inc(negmaxT_done, 1)

                    @block.sync
                    def _(sp):
                        for parity in range(2):
                            sp.wait_ge(negmaxT_done, b + 1)
                            row = SLOT * parity + ROWS
                            sp.dma_start(qT[row:row + 1, :, :], negmaxT[parity * PAIR:(parity + 1) * PAIR, :])\
                                .then_inc(negmax_moved, 16)

                with ExitStack() as inner, nc.Block() as block:
                    probs, probs_hi, probs_lo = [
                        [inner.enter_context(nc.sbuf_tensor(f"{name}{i}", [P, TPB, S], dt)) for i in range(2)]
                        for name, dt in (("probs", F32), ("probs_hi", F16), ("probs_lo", F16))]
                    recip = inner.enter_context(nc.sbuf_tensor("recip", [P, 16], F32))
                    weighed = inner.enter_context(nc.sbuf_tensor("weighed", [P, 16, DH], F32))
                    pX = [inner.enter_context(nc.psum_tensor(f"pX{i}", [P, 2, S], F32)) for i in range(3)]
                    pO = psum_banks(inner, "pO", 2)
                    W = DH + 1

                    @block.tensor
                    def _(pe):
                        pe.wait_ge(negmax_moved, 32 * b + 32)

                        def scores(h):
                            for half in range(2):
                                n = 2 * h + half
                                if n >= 3:
                                    pe.wait_ge(exp_done, 2 * QH * b + n - 2)
                                r = rows_of(h, ROWS + 1)
                                for i in range(2):
                                    kt = 2 * half + i
                                    m = pe.matmul(pX[n % 3][:, i, :], kT[r, h // 4, kt * P:(kt + 1) * P],
                                                  qT[r, h // 2, :], start=True, stop=True)
                                m.then_inc(sT_ready, 1)

                        def weigh(h):
                            pe.wait_ge(probs_lo_done, 2 * QH * b + 2 * h + 2)
                            if h % 4 == 0 and h >= 8:
                                pe.wait_ge(weighed_done, KVH * b + h // 4 - 1)
                            for qt in range(TPB):
                                at = ((h % 4) * TPB + qt) * W
                                for kt in range(TPB):
                                    v_hi, v_lo = [v[:, bass.ds(b * TPB + kt, 1), h // 4, :].rearrange("p a w -> p (a w)")
                                                  for v in (values_hi, values_lo)]
                                    q = slice(qt * P, (qt + 1) * P)
                                    m = split_matmul(pe, pO[h // 4 % 2][:, at:at + W], probs_hi[h % 2][:, kt, q],
                                                     probs_lo[h % 2][:, kt, q], v_hi, v_lo, kt == 0, kt == TPB - 1)
                            m.then_inc(pv_ready, 1)

                        for h in range(QH):
                            scores(h)
                            if h >= 1:
                                weigh(h - 1)
                        weigh(QH - 1)

                    @block.scalar
                    def _(act):
                        def high(h):
                            if h >= 2:
                                act.wait_ge(pv_ready, QH * b + h - 1)
                            act.wait_ge(exp_done, 2 * QH * b + 2 * h + 1)
                            act.activation(probs_hi[h % 2][:, 0:2, :], probs[h % 2][:, 0:2, :], ACT.Copy)\
                                .then_inc(probs_hi0_done, 1)

                        for h in range(QH):
                            for half in range(2):
                                n = 2 * h + half
                                if h >= 2:
                                    act.wait_ge(probs_lo_done, 2 * QH * b + n - 3)
                                act.wait_ge(sT_ready, 2 * QH * b + n + 1)
                                act.activation(probs[h % 2][:, 2 * half:2 * half + 2, :], pX[n % 3][:], ACT.Exp,
                                               scale=DH ** -0.5).then_inc(exp_done, 1)
                            high(h)

                    @block.vector
                    def _(dve):
                        def normalise(g):
                            dve.wait_ge(pv_ready, QH * b + 4 * g + 4)
                            o = pO[g % 2][:, 0:16 * W].rearrange("p (q w) -> p q w", w=W)
                            dve.reciprocal(recip[:].unsqueeze(2), o[:, :, DH:W]).then_inc(recip_done, 1)
                            if g >= 1:
                                dve.wait_ge(x7_done, KVH * b + g)
                            dve.wait_ge(recip_done, KVH * b + g + 1)
                            dve.tensor_tensor(weighed[:], o[:, :, 0:DH], recip[:].unsqueeze(2).to_broadcast([P, 16, DH]),
                                              ALU.mult).then_inc(weighed_done, 1)
                            dve.wait_ge(weighed_done, KVH * b + g + 1)
                            x = xw[:, :, g * 4 * DH:(g + 1) * 4 * DH].rearrange("p t (h d) -> p t h d", d=DH)
                            dve.tensor_tensor(x, x, weighed[:].rearrange("p (h t) d -> p t h d", t=TPB), ALU.add)\
                                .then_inc(x7_done, 1)

                        for h in range(QH):
                            if h >= 2:
                                dve.wait_ge(pv_ready, QH * b + h - 1)
                            dve.wait_ge(exp_done, 2 * QH * b + 2 * h + 2)
                            full, hi, lo = probs[h % 2], probs_hi[h % 2], probs_lo[h % 2]
                            dve.tensor_copy(hi[:, 2:4, :], full[:, 2:4, :]).then_inc(probs_hi1_done, 1)
                            dve.wait_ge(probs_hi0_done, QH * b + h + 1)
                            dve.tensor_tensor(lo[:, 0:2, :], full[:, 0:2, :], hi[:, 0:2, :], ALU.subtract)\
                                .then_inc(probs_lo_done, 1)
                            dve.wait_ge(probs_hi1_done, QH * b + h + 1)
                            dve.tensor_tensor(lo[:, 2:4, :], full[:, 2:4, :], hi[:, 2:4, :], ALU.subtract)\
                                .then_inc(probs_lo_done, 1)
                            if h % 4 == 1 and h >= 5:
                                normalise(h // 4 - 1)
                        normalise(KVH - 1)
                attn.close()

                with ExitStack() as inner, nc.Block() as block:
                    def sbf(name, shape, dt=F32):
                        return inner.enter_context(nc.sbuf_tensor(name, shape, dt))
                    q7 = sbf("q7", [P, TPB, D], BF16)
                    q7T = sbf("q7T", [P, KC, S], BF16)
                    hid = sbf("hidden", [P, TPB, IUP])
                    hq = sbf("hq", [P, TPB, IUP], BF16)
                    hqT = sbf("hqT", [P, IUP // P, S], BF16)
                    amax, scale7, deq7, hmax, hscale, hdeq = [sbf(n, [P, TPB]) for n in
                                                              ("amax", "scale7", "deq7", "hmax", "hscale", "hdeq")]
                    pT = psum_banks(inner, "ffnT", 4)
                    pU = psum_banks(inner, "ffnU", 4)

                    @block.gpsimd
                    def _(pool):
                        l3_mid.on_gpsimd(pool, minus_half, b)

                    @block.tensor
                    def _(pe):
                        pe.wait_ge(q7_done, b + 1)
                        for c in range(KC):
                            for t in range(TPB):
                                m = pe.transpose(pT[c][:].bitcast(BF16)[:, t * P:(t + 1) * P], q7[:, t, c::KC], ident_b[:])
                            m.then_inc(q7T_ready, 1)
                        pe.wait_ge(q7T_done, KC * b + KC)
                        for t in range(TPB):
                            for half in range(2):
                                n = 2 * t + half
                                if n >= 4:
                                    pe.wait_ge(relu_done, 8 * b + n - 3)
                                for c in range(KC):
                                    m = pe.matmul(pU[n % 4][:], q7T[:, c, t * P:(t + 1) * P],
                                                  up_t[:, c, half * D:(half + 1) * D], start=c == 0, stop=c == KC - 1)
                                m.then_inc(hid_ready, 1)
                        pe.wait_ge(hq_done, TPB * b + TPB)
                        for k in range(8):
                            if k >= 4:
                                pe.wait_ge(hqT_done, 8 * b + k - 3)
                            for t in range(TPB):
                                m = pe.transpose(pT[k % 4][:].bitcast(BF16)[:, t * P:(t + 1) * P], hq[:, t, k::8], ident_b[:])
                            m.then_inc(hqT_ready, 1)
                        pe.wait_ge(hqT_done, 8 * b + 8)
                        for t in range(TPB):
                            for k in range(8):
                                m = pe.matmul(pU[t][:], hqT[:, k, t * P:(t + 1) * P], dn_t[:, k, :], start=k == 0, stop=k == 7)
                            m.then_inc(y_ready, 1)

                    @block.scalar
                    def _(act):
                        for c in range(KC):
                            act.wait_ge(q7T_ready, KC * b + c + 1)
                            act.activation(q7T[:, c, :], pT[c][:].bitcast(BF16)[:, 0:S], ACT.Copy).then_inc(q7T_done, 1)
                        for t in range(TPB):
                            for half in range(2):
                                n = 2 * t + half
                                act.wait_ge(hid_ready, 8 * b + n + 1)
                                act.activation(hid[:, t, half * D:(half + 1) * D], pU[n % 4][:], ACT.Relu,
                                               scale=deq7[:, t:t + 1]).then_inc(relu_done, 1)
                        for t in range(TPB):
                            act.wait_ge(hmax_done, TPB * b + t + 1)
                            act.activation(hid[:, t, :], hid[:, t, :], ACT.Square).then_inc(hsq_done, 1)
                        for k in range(8):
                            act.wait_ge(hqT_ready, 8 * b + k + 1)
                            act.activation(hqT[:, k, :], pT[k % 4][:].bitcast(BF16)[:, 0:S], ACT.Copy).then_inc(hqT_done, 1)

                    @block.vector
                    def _(dve):
                        l3_mid.on_vector(dve, lambda t: xw[:, t, :], b, None)
                        for t in range(TPB):
                            dve.tensor_scalar(nrm[:, t, :], xw[:, t, :], l3_mid.rstd[:, t:t + 1],
                                              l3_mid.shift[:, t:t + 1], ALU.mult, ALU.add).then_inc(n7_done, 1)
                        dve.wait_ge(n7_done, TPB * b + TPB)
                        dve.tensor_reduce(amax[:], nrm[:], AX.X, ALU.max, apply_absolute_value=True).then_inc(amax_done, 1)
                        dve.wait_ge(amax_done, b + 1)

                        def scales(top, scale, deq, mean, counter):
                            dve.tensor_scalar(top[:], top[:], 1e-5, None, ALU.max).then_inc(counter, 1)
                            dve.wait_ge(counter, 4 * b + 1)
                            dve.reciprocal(scale[:], top[:]).then_inc(counter, 1)
                            dve.wait_ge(counter, 4 * b + 2)
                            dve.tensor_scalar(scale[:], scale[:], 127.0, None, ALU.mult).then_inc(counter, 1)
                            dve.tensor_scalar(deq[:], top[:], 1.0 / 127.0, mean, ALU.mult, ALU.mult).then_inc(counter, 1)
                            dve.wait_ge(counter, 4 * b + 4)

                        scales(amax, scale7, deq7, tern[:, 1:2], scale_step)
                        for t in range(TPB):
                            dve.tensor_scalar(nrm[:, t, :], nrm[:, t, :], scale7[:, t:t + 1], 127.0, ALU.mult, ALU.min)\
                                .then_inc(quant_step, 1)
                        dve.wait_ge(quant_step, 5 * b + 4)
                        dve.tensor_scalar(nrm[:], nrm[:], -127.0, MAGIC, ALU.max, ALU.add).then_inc(quant_step, 1)
                        dve.wait_ge(quant_step, 5 * b + 5)
                        dve.tensor_scalar(q7[:], nrm[:], MAGIC, None, ALU.subtract).then_inc(q7_done, 1)
                        for t in range(TPB):
                            dve.wait_ge(relu_done, 8 * b + 2 * t + 2)
                            dve.tensor_reduce(hmax[:, t:t + 1], hid[:, t, :], AX.X, ALU.max).then_inc(hmax_done, 1)
                        dve.wait_ge(hmax_done, TPB * b + TPB)
                        dve.tensor_tensor(hmax[:], hmax[:], hmax[:], ALU.mult).then_inc(hquant_step, 1)
                        dve.wait_ge(hquant_step, 9 * b + 1)
                        scales(hmax, hscale, hdeq, tern[:, 3:4], hscale_step)
                        for t in range(TPB):
                            dve.wait_ge(hsq_done, TPB * b + t + 1)
                            dve.tensor_scalar(hid[:, t, :], hid[:, t, :], hscale[:, t:t + 1], 127.0, ALU.mult, ALU.min)\
                                .then_inc(hquant_step, 1)
                        for t in range(TPB):
                            dve.wait_ge(hquant_step, 9 * b + 2 + t)
                            dve.tensor_scalar(hid[:, t, :], hid[:, t, :], -127.0, MAGIC, ALU.max, ALU.add)\
                                .then_inc(hquant_step, 1)
                        for t in range(TPB):
                            dve.wait_ge(hquant_step, 9 * b + 6 + t)
                            dve.tensor_scalar(hq[:, t, :], hid[:, t, :], MAGIC, None, ALU.subtract).then_inc(hq_done, 1)
                        for t in range(TPB):
                            dve.wait_ge(y_ready, TPB * b + t + 1)
                            dve.scalar_tensor_tensor(out=nrm[:, t, :], in0=pU[t][:], scalar=hdeq[:, t:t + 1],
                                                     in1=xw[:, t, :], op0=ALU.mult, op1=ALU.add).then_inc(x8_done, 1)

                    @block.sync
                    def _(sp):
                        for t in range(TPB):
                            sp.wait_ge(x8_done, TPB * b + t + 1)
                            sp.dma_start(out_d[:, bass.ds(b * TPB + t, 1), :], nrm[:, t:t + 1, :]).then_inc(stored, 16)
                        sp.wait_ge(stored, 16 * TPB * b + 16 * TPB)
                        sp.sem_inc(Norm.held, 1)




_INS = ['x', 'ctx_512', 'mask_SxS2_bk1', 'mask_BxS2_bf0', 'L0_xattn_W', 'L0_xattn_b', 'L0_ffn_gate_w', 'L0_ffn_wg',
        'L0_ffn_wu', 'L0_ffn_wd', 'L0_ffn_sg', 'L0_ffn_su', 'L0_ffn_sd', 'L1_xattn_Wq', 'L1_xattn_Wk',
        'L1_xattn_gamma_raw', 'L1_ffn_factors', 'L1_ffn_bias', 'L2_xattn_Wq', 'L2_xattn_bq', 'L2_xattn_Wk',
        'L2_xattn_bk', 'L2_ffn_in_gamma', 'L2_ffn_in_beta', 'L2_ffn_agg_w', 'L2_ffn_agg_b', 'L2_ffn_pn_gamma',
        'L2_ffn_pn_beta', 'L2_ffn_d1_w', 'L2_ffn_d1_b', 'L2_ffn_d2_w', 'L2_ffn_d2_b', 'L2_ffn_bc_w', 'L2_ffn_bc_b',
        'L2_ffn_gate_w', 'L2_ffn_gate_b', 'L2_ffn_out_gamma', 'L2_ffn_out_beta', 'L3_ffn_w_up', 'L3_ffn_w_down']


def kernel(**inputs):
    import numpy as _np
    import concourse.bacc as _bacc
    from concourse import mybir as _mybir
    from concourse.bass_utils import run_bass_kernel_spmd as _run

    nc = _bacc.Bacc("TRN2", target_bir_lowering=False, num_devices=1)
    arrays, args = {}, []
    for name in _INS:
        a = _np.ascontiguousarray(inputs[name]).reshape(_np.shape(inputs[name]) or (1,))
        if a.dtype == _np.bool_:
            a = a.view(_np.int32)
        arrays[f"in_{name}_dram"] = a
        args.append(nc.dram_tensor(f"in_{name}_dram", a.shape, _mybir.dt.from_np(a.dtype), kind="ExternalInput").ap())
    args.append(nc.dram_tensor("out_0_dram", (B, S, D), F32, kind="ExternalOutput").ap())
    program(nc, *args)
    r = _run(nc, [arrays], core_ids=[0])
    return r.results[0]["out_0_dram"]
```

```python
from contextlib import ExitStack

import concourse.bass as bass
from concourse import mybir
from concourse.alu_op_type import AluOpType as ALU

F32 = mybir.dt.float32
F16 = mybir.dt.float16
BF16 = mybir.dt.bfloat16
U8 = mybir.dt.uint8
I32 = mybir.dt.int32
ACT = mybir.ActivationFunctionType
AX = mybir.AxisListType

P = 128
B, S, D = 4, 512, 512
C = 128
TPB = S // P
NT = B * TPB
KC = D // P
E, F, TOPK = 32, 192, 6
FSH = 384
UNITS = 56
ROWS_T = UNITS * S // P
NOWHERE = 1 << 20
W_SCALE = 64.0
K_SEL = int(S * 0.3)
NEG = -3.0e38
MASKED = -1.0e38
P_ASEM = 0.6
HID = 2048
K_STEPS = 4
QH, KVH, DH = 32, 8, 16
IUP = 1024
G_SCALE = 16.0
MAGIC = 1.5 * 2.0 ** 23


def tile_of(tensor, t):
    if isinstance(t, int):
        return tensor[:, t, :]
    return tensor[:, bass.ds(t, 1), :].rearrange("p a d -> p (a d)")


def hold(eng, semaphore, value):
    eng.wait_ge(semaphore, value)
    eng.sem_inc(Norm.held, 1)


class Norm:

    held = None

    def __init__(self, name, sb, sem, eps):
        self.eps = eps
        self.stats = sb(name + "_stats", [P, TPB, 6], F32)
        self.meanvar = sb(name + "_meanvar", [P, TPB, 2], F32)
        self.vareps = sb(name + "_vareps", [P, TPB], F32)
        self.rstd = sb(name + "_rstd", [P, TPB], F32)
        self.shift = sb(name + "_shift", [P, TPB], F32)
        self.stats_done = sem(name + "_stats_done")
        self.meanvar_done = sem(name + "_meanvar_done")
        self.vareps_done = sem(name + "_vareps_done")
        self.rstd_done = sem(name + "_rstd_done")
        self.shift_done = sem(name + "_shift_done")

    def on_vector(self, dve, source, b, before):
        if before is not None:
            hold(dve, before[0], before[1])
        for t in range(TPB):
            dve.bn_stats(self.stats[:, t, :], source(t)).then_inc(self.stats_done, 1)
        hold(dve, self.stats_done, TPB * b + TPB)
        for t in range(TPB):
            dve.bn_aggr(self.meanvar[:, t, :], self.stats[:, t, :]).then_inc(self.meanvar_done, 1)
        dve.wait_ge(self.meanvar_done, TPB * b + TPB)
        dve.tensor_scalar(self.vareps[:], self.meanvar[:, :, 1], self.eps, None, ALU.add)\
            .then_inc(self.vareps_done, 1)
        dve.wait_ge(self.rstd_done, b + 1)
        dve.scalar_tensor_tensor(out=self.shift[:], in0=self.meanvar[:, :, 0], scalar=-1.0, in1=self.rstd[:],
                                 op0=ALU.mult, op1=ALU.mult).then_inc(self.shift_done, 1)
        dve.wait_ge(self.shift_done, b + 1)

    def on_gpsimd(self, pool, half, b):
        pool.wait_ge(self.vareps_done, b + 1)
        pool.tensor_tensor(self.rstd[:], self.vareps[:], half[:, 0:TPB], ALU.pow).then_inc(self.rstd_done, 1)


def split_matmul(pe, out, lhs_hi, lhs_lo, rhs_hi, rhs_lo, first, last):
    pe.matmul(out, lhs_hi, rhs_hi, start=first, stop=False)
    pe.matmul(out, lhs_hi, rhs_lo, start=False, stop=False)
    return pe.matmul(out, lhs_lo, rhs_hi, start=False, stop=last)


def program(nc, x, ctx_512, mask_SxS2_bk1, mask_BxS2_bf0, L0_xattn_W, L0_xattn_b, L0_ffn_gate_w, L0_ffn_wg,
            L0_ffn_wu, L0_ffn_wd, L0_ffn_sg, L0_ffn_su, L0_ffn_sd, L1_xattn_Wq, L1_xattn_Wk,
            L1_xattn_gamma_raw, L1_ffn_factors, L1_ffn_bias, L2_xattn_Wq, L2_xattn_bq, L2_xattn_Wk,
            L2_xattn_bk, L2_ffn_in_gamma, L2_ffn_in_beta, L2_ffn_agg_w, L2_ffn_agg_b, L2_ffn_pn_gamma,
            L2_ffn_pn_beta, L2_ffn_d1_w, L2_ffn_d1_b, L2_ffn_d2_w, L2_ffn_d2_b, L2_ffn_bc_w, L2_ffn_bc_b,
            L2_ffn_gate_w, L2_ffn_gate_b, L2_ffn_out_gamma, L2_ffn_out_beta, L3_ffn_w_up, L3_ffn_w_down,
            out):
    x_d = x.rearrange("b (t p) d -> p (b t) d", p=P)
    out_d = out.rearrange("b (t p) d -> p (b t) d", p=P)
    ctx_d = ctx_512.rearrange("b (t p) d -> p (b t) d", p=P)

    with ExitStack() as whole:
        def sb(name, shape, dt=F32):
            return whole.enter_context(nc.sbuf_tensor(name, shape, dt))

        signals = []

        def sem(name):
            signals.append(nc.alloc_semaphore(name))
            return signals[-1]

        def psum_banks(scope, name, n, dt=F32):
            width = 512 if dt == F32 else 1024
            return [scope.enter_context(nc.psum_tensor(f"{name}{i}", [P, width], dt)) for i in range(n)]

        Norm.held = nc.alloc_semaphore("held")

        xres = sb("xres", [P, NT, D])
        ident = sb("ident", [P, P])
        ident_h = sb("ident_h", [P, P], F16)
        ident_b = sb("ident_b", [P, P], BF16)
        ones = sb("ones", [P, P])
        minus_half = sb("minus_half", [P, NT])
        gam = sb("gam", [P, 4])
        gate2_hi = sb("gate2_hi", [P, KC, D], F16)
        gate2_lo = sb("gate2_lo", [P, KC, D], F16)
        gate2_bias = sb("gate2_bias", [2, D], F16)
        ones_h = sb("ones_h", [2, P], F16)
        up_t = sb("up_t", [P, KC, IUP], BF16)
        dn_t = sb("dn_t", [P, IUP // P, D], BF16)
        tern = sb("tern", [P, 4])

        middle = whole.enter_context(ExitStack())
        def sbd(name, shape, dt=F32):
            return middle.enter_context(nc.sbuf_tensor(name, shape, dt))
        gate6 = sbd("gate6", [P, NT, TOPK])
        learned = sbd("learned", [P, NT, S])
        proj_hi = [None, None] + [sbd(f"proj_hi{i}", [P, B * S], F16) for i in (2, 3)]
        proj_lo = [None, None] + [sbd(f"proj_lo{i}", [P, B * S], F16) for i in (2, 3)]

        early = whole.enter_context(ExitStack())
        def sbe(name, shape, dt=F32):
            return early.enter_context(nc.sbuf_tensor(name, shape, dt))

        proj_hi[0], proj_lo[0] = [m[:].rearrange("p c e -> p (c e)") for m in (gate2_hi, gate2_lo)]
        halves_of_up = up_t[:].rearrange("p c e -> p (c e)").bitcast(F16)
        proj_hi[1], proj_lo[1] = halves_of_up[:, 0:B * S], halves_of_up[:, B * S:2 * B * S]
        hT_hi = sbe("hT_hi", [P, KC, B * S], F16)
        hT_lo = sbe("hT_lo", [P, KC, B * S], F16)
        scores = dn_t[:].rearrange("p k e -> p (k e)").bitcast(F32)[:, 0:NT * E].rearrange("p (t e) -> p t e", e=E)
        place = sbe("place", [P, NT, TOPK], I32)
        pairs = sbe("pairs", [P, NT, TOPK, 2], I32)
        unit_expert = sbe("unit_expert", [1, UNITS], I32)
        table_fill = sbe("table_fill", [P, 2 * ROWS_T], I32)
        h_rows = nc.dram_tensor("h_rows", (NT * P, D), F32).ap()
        table_d = nc.dram_tensor("slot_table", (P * ROWS_T, 2), I32).ap()
        choice_rows = nc.dram_tensor("choice_rows", (NT * P * TOPK, D), F32).ap()

        first = whole.enter_context(ExitStack())
        def sbe(name, shape, dt=F32):
            return first.enter_context(nc.sbuf_tensor(name, shape, dt))

        ctxs = sbe("ctxs", [P, NT, C])
        ctxT = sbe("ctxT", [P, B * S])
        proj_f = [sbe(f"proj_f{i}", [P, S]) for i in range(2)]
        w0 = sbe("w0", [P, 2])
        b0 = sbe("b0", [P, 1])
        wj_rep = sbe("wj_rep", [P, P])
        row_term = sbe("row_term", [P, NT])
        proj_w = sbe("proj_w", [P, 4, C])
        proj_wT = sbe("proj_wT", [P, 4, C])
        proj_b = sbe("proj_b", [P, 2])
        gate_f = sbe("gate_f", [P, KC, E])
        gate_hi = sbe("gate_hi", [P, KC, E], F16)
        gate_lo = sbe("gate_lo", [P, KC, E], F16)

        x_in = sem("x_in")
        small_in = sem("small_in")
        ctx_in = sem("ctx_in")
        gamma_in = sem("gamma_in")
        consts_zeroed = sem("consts_zeroed")
        consts_done = sem("consts_done")
        ctx_transposed = sem("ctx_transposed")
        ctxT_done = sem("ctxT_done")
        projT_ready = sem("projT_ready")
        projT_done = sem("projT_done")
        proj_ready = sem("proj_ready")
        proj_done = sem("proj_done")
        wj_done = sem("wj_done")
        row_ready = sem("row_ready")
        row_done = sem("row_done")
        gate_hi_done = sem("gate_hi_done")
        gate_lo_done = sem("gate_lo_done")
        gamma_sig = sem("gamma_sig")
        gamma_done = sem("gamma_done")
        proj_hi_done = sem("proj_hi_done")
        proj_lo_done = sem("proj_lo_done")

        with ExitStack() as scope, nc.Block() as block:
            pT = psum_banks(scope, "setupT", 4)
            pW = psum_banks(scope, "setupW", 1)[0]
            pP = psum_banks(scope, "setupP", 2)
            pR = psum_banks(scope, "setupR", 1)[0]

            @block.sync
            def _(sp):
                sp.dma_start(ctxs[:], ctx_d).then_inc(ctx_in, 16)
                for i, w in enumerate((L1_xattn_Wq, L1_xattn_Wk, L2_xattn_Wq, L2_xattn_Wk)):
                    sp.dma_start(proj_w[:, i, :], w[:]).then_inc(small_in, 16)
                for i in range(2):
                    sp.dma_start(w0[:, i:i + 1], L0_xattn_W[0, i * C:(i + 1) * C].rearrange("(p a) -> p a", a=1))\
                        .then_inc(small_in, 16)
                sp.dma_start(b0[:], L0_xattn_b.rearrange("(a c) -> a c", a=1).to_broadcast([P, 1]))\
                    .then_inc(small_in, 16)
                sp.dma_start(proj_b[:, 0:1], L2_xattn_bq.rearrange("(p a) -> p a", a=1)).then_inc(small_in, 16)
                sp.dma_start(proj_b[:, 1:2], L2_xattn_bk.rearrange("(p a) -> p a", a=1)).then_inc(small_in, 16)
                sp.dma_start(gate_f[:], L0_ffn_gate_w.rearrange("(p c) e -> p c e", c=KC)).then_inc(small_in, 16)
                sp.dma_start(gam[:, 0:1], L1_xattn_gamma_raw.rearrange("(a c) -> a c", a=1).to_broadcast([P, 1])).then_inc(gamma_in, 16)
                for b in range(B):
                    sp.dma_start(xres[:, TPB * b:TPB * (b + 1), :], x_d[:, TPB * b:TPB * (b + 1), :])\
                        .then_inc(x_in, 16)

            @block.gpsimd
            def _(pool):
                for m in (ident, ident_h, ident_b):
                    pool.memset(m[:], 0.0).then_inc(consts_zeroed, 1)
                pool.memset(ones[:], 1.0).then_inc(consts_done, 1)
                pool.memset(minus_half[:], -0.5).then_inc(consts_done, 1)
                pool.wait_ge(consts_zeroed, 3)
                for m in (ident, ident_h, ident_b):
                    pool.affine_select(out=m[:], in_=m[:], compare_op=ALU.not_equal, fill=1.0, base=0,
                                       pattern=[[-1, P]], channel_multiplier=1).then_inc(consts_done, 1)

            @block.tensor
            def _(pe):
                pe.wait_ge(consts_done, 5)
                pe.wait_ge(small_in, 160)
                for i in range(4):
                    m = pe.transpose(pW[:, i * C:(i + 1) * C], proj_w[:, i, :], ident[:])
                m.then_inc(projT_ready, 1)
                pe.wait_ge(ctx_in, 16)
                for b in range(B):
                    for t in range(TPB):
                        m = pe.transpose(pT[b][:, t * P:(t + 1) * P], ctxs[:, TPB * b + t, :], ident[:])
                    m.then_inc(ctx_transposed, 1)
                pe.wait_ge(ctxT_done, B)
                for t in range(NT):
                    m = pe.matmul(pR[:, t:t + 1], ctxT[:, t * P:(t + 1) * P], w0[:, 0:1], start=True, stop=True)
                m.then_inc(row_ready, 1)
                pe.wait_ge(projT_done, 1)
                n = 0
                for i in range(4):
                    for b in range(B):
                        if n >= 2:
                            pe.wait_ge(proj_done, n - 1)
                        pe.matmul(pP[n % 2][:], proj_wT[:, i, :], ctxT[:, b * S:(b + 1) * S],
                                  start=True, stop=True).then_inc(proj_ready, 1)
                        n += 1

            @block.scalar
            def _(act):
                act.wait_ge(gamma_in, 16)
                act.activation(gam[:, 1:2], gam[:, 0:1], ACT.Sigmoid).then_inc(gamma_sig, 1)
                act.wait_ge(small_in, 160)
                act.activation(gate_hi[:], gate_f[:], ACT.Copy).then_inc(gate_hi_done, 1)
                for b in range(B):
                    act.wait_ge(ctx_transposed, b + 1)
                    act.activation(ctxT[:, b * S:(b + 1) * S], pT[b][:], ACT.Copy).then_inc(ctxT_done, 1)
                n = 0
                for i in range(4):
                    for b in range(B):
                        act.wait_ge(proj_ready, n + 1)
                        if n >= 2:
                            act.wait_ge(proj_lo_done, n - 1)
                        act.activation(proj_f[n % 2][:], pP[n % 2][:], ACT.Identity,
                                       bias=0.0 if i < 2 else proj_b[:, i - 2:i - 1]).then_inc(proj_done, 1)
                        act.wait_ge(proj_done, n + 1)
                        act.activation(proj_hi[i][:, b * S:(b + 1) * S], proj_f[n % 2][:], ACT.Copy)\
                            .then_inc(proj_hi_done, 1)
                        n += 1

            @block.vector
            def _(dve):
                dve.wait_ge(small_in, 160)
                dve.wait_ge(consts_done, 5)
                dve.tensor_scalar(wj_rep[:], ones[:], w0[:, 1:2], None, ALU.mult).then_inc(wj_done, 1)
                dve.wait_ge(projT_ready, 1)
                dve.tensor_copy(proj_wT[:].rearrange("p a c -> p (a c)"), pW[:]).then_inc(projT_done, 1)
                dve.wait_ge(gate_hi_done, 1)
                dve.tensor_tensor(gate_lo[:], gate_f[:], gate_hi[:], ALU.subtract).then_inc(gate_lo_done, 1)
                dve.wait_ge(gamma_sig, 1)
                dve.tensor_scalar(gam[:, 2:3], gam[:, 1:2], 0.5, None, ALU.mult).then_inc(gamma_done, 1)
                dve.tensor_scalar(gam[:, 3:4], gam[:, 1:2], -1.0, 1.0, ALU.mult, ALU.add).then_inc(gamma_done, 1)
                dve.wait_ge(row_ready, 1)
                dve.tensor_scalar(row_term[:], pR[:, 0:NT], b0[:, 0:1], None, ALU.add).then_inc(row_done, 1)
                n = 0
                for i in range(4):
                    for b in range(B):
                        dve.wait_ge(proj_hi_done, n + 1)
                        dve.tensor_tensor(proj_lo[i][:, b * S:(b + 1) * S], proj_f[n % 2][:],
                                          proj_hi[i][:, b * S:(b + 1) * S], ALU.subtract).then_inc(proj_lo_done, 1)
                        n += 1


        col_ready = sem("col_ready")
        sig_done = sem("sig_done")
        l0_scale_done = sem("l0_scale_done")
        l0_norm_done = sem("l0_norm_done")
        x1_done = sem("x1_done")
        h_done = sem("h_done")
        hT_ready = sem("hT_ready")
        hT_hi_done = sem("hT_hi_done")
        hT_lo_done = sem("hT_lo_done")
        logits_ready = sem("logits_ready")
        scores_done = sem("scores_done")
        h_stored = sem("h_stored")

        with ExitStack() as scope:
            def sbl(name, shape, dt=F32):
                return scope.enter_context(nc.sbuf_tensor(name, shape, dt))
            l0_in = Norm("l0_in", sbl, sem, 1e-5)
            l0_out = Norm("l0_out", sbl, sem, 1e-5)
            sig = sbl("sig", [P, TPB, S])
            xn = sbl("xn", [P, TPB, D])
            h = xn
            l0_mul = sbl("l0_mul", [P, TPB])
            l0_add = sbl("l0_add", [P, TPB])
            pC = psum_banks(scope, "l0col", 1)[0]
            pH = psum_banks(scope, "l0hT", KC)
            pL = psum_banks(scope, "l0log", 1)[0]
            with nc.Fori(0, B) as b, nc.Block() as block:
                @block.tensor
                def _(pe):
                    pe.matmul(pC[:], wj_rep[:], ctxT[:, bass.ds(b * S, S)], start=True, stop=True)\
                        .then_inc(col_ready, 1)
                    pe.wait_ge(h_done, TPB * b + TPB)
                    for c in range(KC):
                        for t in range(TPB):
                            m = pe.transpose(pH[c][:, t * P:(t + 1) * P], h[:, t, c::KC], ident[:])
                        m.then_inc(hT_ready, 1)
                    pe.wait_ge(hT_lo_done, KC * b + KC)
                    for t in range(TPB):
                        for c in range(KC):
                            hi = hT_hi[:, c, bass.ds(b * S + t * P, P)]
                            lo = hT_lo[:, c, bass.ds(b * S + t * P, P)]
                            m = split_matmul(pe, pL[:, t * E:(t + 1) * E], hi, lo, gate_hi[:, c, :],
                                             gate_lo[:, c, :], c == 0, c == KC - 1)
                    m.then_inc(logits_ready, 1)

                @block.scalar
                def _(act):
                    act.wait_ge(col_ready, b + 1)
                    for t in range(TPB):
                        act.activation(sig[:, t, :], pC[:], ACT.Sigmoid, bias=row_term[:, bass.ds(b * TPB + t, 1)])\
                            .then_inc(sig_done, 1)
                    for c in range(KC):
                        act.wait_ge(hT_ready, KC * b + c + 1)
                        act.activation(hT_hi[:, c, bass.ds(b * S, S)], pH[c][:], ACT.Copy).then_inc(hT_hi_done, 1)
                    act.wait_ge(logits_ready, b + 1)
                    act.activation(scores[:, bass.ds(b * TPB, TPB), :].rearrange("p t e -> p (t e)"),
                                   pL[:, 0:TPB * E], ACT.Sigmoid).then_inc(scores_done, 1)

                @block.sync
                def _(sp):
                    sp.wait_ge(h_done, TPB * b + TPB)
                    sp.dma_start(h_rows.rearrange("(t p) d -> p t d", p=P)[:, bass.ds(b * TPB, TPB), :], h[:])\
                        .then_inc(h_stored, 16)
                    hold(sp, h_stored, 16 * b + 16)

                @block.gpsimd
                def _(pool):
                    l0_in.on_gpsimd(pool, minus_half, b)
                    l0_out.on_gpsimd(pool, minus_half, b)

                @block.vector
                def _(dve):
                    l0_in.on_vector(dve, lambda t: tile_of(xres, b * TPB + t), b, (x_in, 16 * B))
                    dve.tensor_scalar(l0_mul[:], l0_in.rstd[:], 1.0 - P_ASEM, 1.0, ALU.mult, ALU.add)\
                        .then_inc(l0_scale_done, 1)
                    dve.tensor_scalar(l0_add[:], l0_in.shift[:], 1.0 - P_ASEM, None, ALU.mult)\
                        .then_inc(l0_scale_done, 1)
                    dve.wait_ge(l0_scale_done, 2 * b + 2)
                    for t in range(TPB):
                        dve.tensor_scalar(xn[:, t, :], tile_of(xres, b * TPB + t), l0_mul[:, t:t + 1],
                                          l0_add[:, t:t + 1], ALU.mult, ALU.add).then_inc(l0_norm_done, 1)
                    dve.wait_ge(l0_norm_done, TPB * b + TPB)
                    for t in range(TPB):
                        dve.wait_ge(sig_done, TPB * b + t + 1)
                        dve.scalar_tensor_tensor(out=tile_of(xres, b * TPB + t), in0=sig[:, t, :], scalar=P_ASEM,
                                                 in1=xn[:, t, :], op0=ALU.mult, op1=ALU.add).then_inc(x1_done, 1)
                    l0_out.on_vector(dve, lambda t: tile_of(xres, b * TPB + t), b, (x1_done, TPB * b + TPB))
                    for t in range(TPB):
                        dve.tensor_scalar(h[:, t, :], tile_of(xres, b * TPB + t), l0_out.rstd[:, t:t + 1],
                                          l0_out.shift[:, t:t + 1], ALU.mult, ALU.add).then_inc(h_done, 1)
                    for c in range(KC):
                        dve.wait_ge(hT_hi_done, KC * b + c + 1)
                        dve.tensor_tensor(hT_lo[:, c, bass.ds(b * S, S)], pH[c][:], hT_hi[:, c, bass.ds(b * S, S)],
                                          ALU.subtract).then_inc(hT_lo_done, 1)

        first.close()

        route = sem("route")
        sel_done = sem("sel_done")
        ranked = sem("ranked")
        table_filled = sem("table_filled")
        route_consts = sem("route_consts")
        tables_ready = sem("tables_ready")
        with ExitStack() as scope, nc.Block() as block:
            def sbl(name, shape, dt=F32):
                return scope.enter_context(nc.sbuf_tensor(name, shape, dt))
            top8 = sbl("top8", [P, NT, 8])
            sel = sbl("sel", [P, NT, E])
            equal = sbl("equal", [P, NT, E])
            rank = sbl("rank", [P, NT, E])
            gates = sbl("gates", [P, NT, E])
            zero = sbl("zero_row", [P, E])
            room = sbl("room", [P, NT])
            weight = sbl("weight", [P, NT])
            before = sbl("before", [P, P])
            offset = sbl("offset", [P, NT + 1, E])
            slot = sbl("slot", [P, NT, E])
            units = sbl("units", [P, 4, E])
            units_end = sbl("units_end", [P, E])
            units_start = sbl("units_start", [P, E])
            pick = sbl("pick", [P, 2, NT, E])
            slot6 = sbl("slot6", [P, NT, TOPK])
            row6 = sbl("row6", [P, NT, TOPK])
            unit_no = sbl("unit_no", [1, UNITS], I32)
            unit_f = sbl("unit_f", [1, UNITS])
            ended = sbl("ended", [1, UNITS, E])
            unit_expert_f = sbl("unit_expert_f", [1, UNITS])
            pRank, pCount = psum_banks(scope, "route", 2)

            @block.gpsimd
            def _(pool):
                pool.memset(before[:], 0.0).then_inc(route_consts, 1)
                pool.memset(table_fill[:], NOWHERE).then_inc(route_consts, 1)
                pool.iota(unit_no[:], [[1, UNITS]], base=0, channel_multiplier=0).then_inc(route_consts, 1)
                pool.iota(pairs[:, :, :, 0], [[P, NT], [0, TOPK]], base=0, channel_multiplier=1).then_inc(route_consts, 1)
                pool.iota(pairs[:, :, :, 1], [[P * TOPK, NT], [1, TOPK]], base=0, channel_multiplier=TOPK)\
                    .then_inc(route_consts, 1)
                pool.wait_ge(route_consts, 5)
                pool.affine_select(out=before[:], in_=before[:], compare_op=ALU.is_ge, fill=1.0, base=0,
                                   pattern=[[-1, P]], channel_multiplier=1).then_inc(route_consts, 1)

            @block.sync
            def _(sp):
                sp.wait_ge(route_consts, 6)
                sp.dma_start(table_d.rearrange("(p s) w -> p (s w)", p=P), table_fill[:]).then_inc(table_filled, 16)
                sp.wait_ge(table_filled, 16)

            @block.tensor
            def _(pe):
                pe.wait_ge(sel_done, 1)
                pe.wait_ge(route_consts, 6)
                flat = sel[:].rearrange("p t e -> p (t e)")
                pe.matmul(pCount[:], ones[:], flat, start=True, stop=True).then_inc(ranked, 1)
                pe.matmul(pRank[:], before[:], flat, start=True, stop=True).then_inc(ranked, 1)

            @block.vector
            def _(dve):
                steps = [0]

                def done(*instructions):
                    for ins in instructions:
                        ins.then_inc(route, 1)
                        steps[0] += 1
                    dve.wait_ge(route, steps[0])

                done(*[dve.max(top8[:, t, :], scores[:, t, :]) for t in range(NT)],
                     dve.memset(zero[:], 0.0))
                least = top8[:, :, TOPK - 1:TOPK].to_broadcast([P, NT, E])
                done(dve.tensor_tensor(sel[:], scores[:], least, ALU.is_gt),
                     dve.tensor_tensor(equal[:], scores[:], least, ALU.is_equal))
                done(dve.tensor_reduce(room[:], sel[:], AX.X, ALU.add),
                     *[dve.tensor_tensor_scan(rank[:, t, :], equal[:, t, :], zero[:], 0.0, ALU.add, ALU.add)
                       for t in range(NT)])
                done(dve.tensor_scalar(room[:], room[:], -1.0, float(TOPK), ALU.mult, ALU.add))
                done(dve.tensor_tensor(rank[:], rank[:], room[:].unsqueeze(2).to_broadcast([P, NT, E]), ALU.is_le))
                done(dve.tensor_tensor(equal[:], equal[:], rank[:], ALU.mult))
                done(dve.tensor_tensor(sel[:], sel[:], equal[:], ALU.add))
                dve.sem_inc(sel_done, 1)
                done(dve.tensor_tensor(gates[:], sel[:], scores[:], ALU.mult),
                     *[dve.tensor_tensor_scan(rank[:, t, :], sel[:, t, :], zero[:], 0.0, ALU.add, ALU.add)
                       for t in range(NT)])
                done(dve.tensor_reduce(weight[:], gates[:], AX.X, ALU.add))
                done(dve.tensor_scalar(weight[:], weight[:], 1e-20, W_SCALE, ALU.add, ALU.mult))
                done(dve.reciprocal(weight[:], weight[:]))
                done(dve.tensor_tensor(gates[:], gates[:], weight[:].unsqueeze(2).to_broadcast([P, NT, E]), ALU.mult),
                     dve.memset(offset[:, 0, :], 0.0))
                dve.wait_ge(ranked, 2)
                for t in range(NT):
                    done(dve.tensor_tensor(offset[:, t + 1, :], offset[:, t, :], pCount[:, t * E:(t + 1) * E], ALU.add))
                count = offset[:, NT, :]
                done(dve.tensor_tensor(slot[:], offset[:, 0:NT, :], pRank[:].rearrange("p (t e) -> p t e", e=E), ALU.add),
                     dve.tensor_scalar(units[:, 0, :], count, 0.0, None, ALU.is_gt))
                for i in range(1, NT * P // S):
                    done(dve.scalar_tensor_tensor(out=units[:, i, :], in0=count, scalar=float(S * i),
                                                  in1=units[:, i - 1, :], op0=ALU.is_gt, op1=ALU.add))
                done(dve.tensor_tensor_scan(units_end[:], units[:, 3, :], zero[:], 0.0, ALU.add, ALU.add))
                done(dve.tensor_tensor(units_start[:], units_end[:], units[:, 3, :], ALU.subtract))
                done(dve.scalar_tensor_tensor(out=slot[:], in0=units_start[:].unsqueeze(1).to_broadcast([P, NT, E]),
                                              scalar=float(S), in1=slot[:], op0=ALU.mult, op1=ALU.add))
                for k in range(TOPK):
                    done(dve.scalar_tensor_tensor(out=equal[:], in0=rank[:], scalar=float(k + 1), in1=sel[:],
                                                  op0=ALU.is_equal, op1=ALU.mult))
                    done(dve.tensor_tensor(pick[:, 0, :, :], equal[:], slot[:], ALU.mult),
                         dve.tensor_tensor(pick[:, 1, :, :], equal[:], gates[:], ALU.mult))
                    done(dve.tensor_reduce(slot6[:, :, k], pick[:, 0, :, :], AX.X, ALU.add),
                         dve.tensor_reduce(gate6[:, :, k], pick[:, 1, :, :], AX.X, ALU.add))
                done(dve.tensor_scalar(row6[:], slot6[:], 1.0 / P, -(P - 1) / (2.0 * P), ALU.mult, ALU.add))
                done(dve.tensor_scalar(row6[:], row6[:], MAGIC, None, ALU.add))
                done(dve.tensor_scalar(row6[:], row6[:], MAGIC, 1.0 - P * ROWS_T, ALU.subtract, ALU.mult))
                done(dve.scalar_tensor_tensor(out=slot6[:], in0=slot6[:], scalar=float(ROWS_T), in1=row6[:],
                                              op0=ALU.mult, op1=ALU.add))
                done(dve.tensor_copy(place[:], slot6[:]))
                dve.wait_ge(route_consts, 6)
                done(dve.tensor_copy(unit_f[:], unit_no[:]))
                done(dve.tensor_tensor(ended[:], units_end[0:1, :].unsqueeze(1).to_broadcast([1, UNITS, E]),
                                       unit_f[:].unsqueeze(2).to_broadcast([1, UNITS, E]), ALU.is_le))
                done(dve.tensor_reduce(unit_expert_f[:], ended[:], AX.X, ALU.add))
                done(dve.tensor_scalar(unit_expert_f[:], unit_expert_f[:], E - 1.0, None, ALU.min))
                done(dve.tensor_copy(unit_expert[:], unit_expert_f[:]))
                dve.sem_inc(tables_ready, 1)

        w_in = sem("w_in")
        w_hi_done = sem("w_hi_done")
        w_lo_done = sem("w_lo_done")
        up_ready = sem("up_ready")
        silu_done = sem("silu_done")
        act_done = sem("act_done")
        act_hi_done = sem("act_hi_done")
        act_lo_done = sem("act_lo_done")
        down_ready = sem("down_ready")
        added = sem("added")
        sim_ready = sem("sim_ready")
        sim_copied = sem("sim_copied")
        sim_taken = sem("sim_taken")
        sel_step = sem("sel_step")
        sim_sig_done = sem("sim_sig_done")
        learned_done = sem("learned_done")
        kept_done = sem("kept_done")
        table_written = sem("table_written")
        table_in = sem("table_in")
        gather_index = sem("gather_index")
        scatter_index = sem("scatter_index")
        gathered = [sem(f"gathered{t}") for t in range(TPB)]
        rows_zeroed = sem("rows_zeroed")
        xT_ready = sem("xT_ready")
        xT_hi_done = sem("xT_hi_done")
        xT_lo_done = sem("xT_lo_done")
        scattered = sem("scattered")

        GB = B
        SHARED = 2 * GB
        ROUNDS = (K_SEL - 1) // 8
        SEL_STEPS = 2 * ROUNDS + 1
        STEPS = 4
        SIM_SHARED = NT - UNITS // STEPS

        with ExitStack() as scope:
            def sbl(name, shape, dt=F32):
                return scope.enter_context(nc.sbuf_tensor(name, shape, dt))
            wup_f = sbl("wup_f", [P, KC, 2, F])
            wdn_f = sbl("wdn_f", [P, 2, D])
            wup_hi = [sbl(f"wup_hi{i}", [P, KC, 3 * P], F16) for i in range(4)]
            wup_lo = [sbl(f"wup_lo{i}", [P, KC, 3 * P], F16) for i in range(4)]
            wdn_hi = [sbl(f"wdn_hi{i}", [P, 2, D], F16) for i in range(4)]
            wdn_lo = [sbl(f"wdn_lo{i}", [P, 2, D], F16) for i in range(4)]
            silu_a = sbl("silu_a", [P, S])
            silu_c = sbl("silu_c", [P // 2, S])
            prod_a = sbl("prod_a", [P, S])
            prod_c = sbl("prod_c", [P // 2, S])
            acta_hi = sbl("acta_hi", [P, S], F16)
            acta_lo = sbl("acta_lo", [P, S], F16)
            actc = sbl("actc", [P, S], F16)
            sim, sim_work, sim_sig, sim_next = [dn_t[:].rearrange("p k e -> p (k e)").bitcast(F32)[:, i * S:(i + 1) * S]
                                                for i in range(4)]
            sim_top = sbl("sim_top", [P, 8])
            table = sbl("table", [P, ROWS_T, 2], I32)
            gather_at = sbl("gather_at", [P, TPB, 2], I32)
            scatter_at = sbl("scatter_at", [P, TPB, 2], I32)
            pU = psum_banks(scope, "moeU", 3)
            pY = psum_banks(scope, "moeY", 4)
            pS = psum_banks(scope, "moeS", 1)[0]

            spare = hT_hi[:].rearrange("p c s -> p (c s)")
            xT = [[spare[:, (2 * par + half) * B * S:(2 * par + half + 1) * B * S].rearrange("p (c s) -> p c s", c=KC)
                   for half in range(2)] for par in range(2)]
            spare = hT_lo[:].rearrange("p c s -> p (c s)").bitcast(F32)
            rows = spare[:, 0:TPB * D].rearrange("p (t d) -> p t d", d=D)
            out_rows = spare[:, TPB * D:2 * TPB * D].rearrange("p (t d) -> p t d", d=D)

            def load(sp, wg, wu, wd):
                sp.dma_start(wup_f[:, :, 0, :], wg.rearrange("(p c) f -> p c f", c=KC)).then_inc(w_in, 16)
                sp.dma_start(wup_f[:, :, 1, :], wu.rearrange("(p c) f -> p c f", c=KC)).then_inc(w_in, 16)
                sp.dma_start(wdn_f[:, 0, :], wd[0:P, :]).then_inc(w_in, 16)
                for half in range(2):
                    sp.dma_start(wdn_f[64 * half:64 * half + 64, 1, :], wd[P:F, :]).then_inc(w_in, 16)

            def split_hi(act, buf, n):
                act.wait_ge(w_in, 80 * n + 80)
                f, h16 = wup_f, wup_hi[buf]
                act.activation(h16[:, :, 0:P], f[:, :, 0, 0:P], ACT.Copy, scale=W_SCALE).then_inc(w_hi_done, 1)
                act.activation(h16[:, :, P:2 * P], f[:, :, 1, 0:P], ACT.Copy, scale=W_SCALE).then_inc(w_hi_done, 1)
                act.activation(h16[:, :, 2 * P:3 * P].rearrange("p c (g f) -> p c g f", g=2), f[:, :, :, P:F],
                               ACT.Copy, scale=W_SCALE).then_inc(w_hi_done, 1)
                act.activation(wdn_hi[buf][:], wdn_f[:], ACT.Copy, scale=W_SCALE).then_inc(w_hi_done, 1)

            def split_lo(dve, buf, n):
                dve.wait_ge(w_hi_done, 4 * n + 4)
                f, h16, l16 = wup_f, wup_hi[buf], wup_lo[buf]
                for o, i0, i1 in ((l16[:, :, 0:P], f[:, :, 0, 0:P], h16[:, :, 0:P]),
                                  (l16[:, :, P:2 * P], f[:, :, 1, 0:P], h16[:, :, P:2 * P]),
                                  (l16[:, :, 2 * P:2 * P + 64], f[:, :, 0, P:F], h16[:, :, 2 * P:2 * P + 64]),
                                  (l16[:, :, 2 * P + 64:3 * P], f[:, :, 1, P:F], h16[:, :, 2 * P + 64:3 * P]),
                                  (wdn_lo[buf][:], wdn_f[:], wdn_hi[buf][:])):
                    dve.scalar_tensor_tensor(out=o, in0=i0, scalar=W_SCALE, in1=i1, op0=ALU.mult,
                                             op1=ALU.subtract).then_inc(w_lo_done, 1)

            def up_columns(pe, m, buf, col, bank, x_hi, x_lo, group, midway=lambda: None):
                cols = slice(col * P, (col + 1) * P)
                toks = slice(group * S, (group + 1) * S)
                for c in range(KC):
                    if c == KC // 2:
                        midway()
                    mm = split_matmul(pe, pU[bank][:], wup_hi[buf][:, c, cols], wup_lo[buf][:, c, cols],
                                      x_hi[:, c, toks], x_lo[:, c, toks], c == 0, c == KC - 1)
                mm.then_inc(up_ready, 1)

            def down_tile(pe, m, buf, t):
                pe.wait_ge(added, TPB * m + t + 1)
                tok = slice(t * P, (t + 1) * P)
                pe.matmul(pY[t][:], acta_hi[:, tok], wdn_hi[buf][:, 0, :], start=True, stop=False)
                pe.matmul(pY[t][:], acta_hi[:, tok], wdn_lo[buf][:, 0, :], start=False, stop=False)
                pe.matmul(pY[t][:], acta_lo[:, tok], wdn_hi[buf][:, 0, :], start=False, stop=False)
                pe.matmul(pY[t][:], actc[:, tok], wdn_hi[buf][:, 1, :], start=False, stop=False)
                pe.matmul(pY[t][:], actc[0:64, tok], wdn_lo[buf][0:64, 1, :], start=False, stop=True)\
                    .then_inc(down_ready, 1)

            def similarity(pe, tile):
                split_matmul(pe, pS[:], proj_hi[0][:, bass.ds(tile * P, P)], proj_lo[0][:, bass.ds(tile * P, P)],
                             proj_hi[1][:, bass.ds((tile // TPB) * S, S)], proj_lo[1][:, bass.ds((tile // TPB) * S, S)],
                             True, True).then_inc(sim_ready, 1)

            def silu(act, m, which):
                out, src = ((silu_a, pU[0][:]), (silu_c, pU[2][0:64, :]))[which]
                act.wait_ge(up_ready, 3 * m + which + 1)
                act.activation(out[:], src, ACT.Silu, scale=1.0 / W_SCALE).then_inc(silu_done, 1)

            def product_hi(act, m, first=False):
                if not first:
                    act.wait_ge(down_ready, TPB * m)
                act.wait_ge(act_done, 2 * m + 1)
                act.activation(acta_hi[:], prod_a[:], ACT.Copy).then_inc(act_hi_done, 1)
                act.wait_ge(act_done, 2 * m + 2)
                act.activation(actc[0:64, :], prod_c[:], ACT.Copy).then_inc(act_hi_done, 1)

            def products(dve, m, first=False):
                dve.wait_ge(silu_done, 2 * m + 1)
                dve.wait_ge(up_ready, 3 * m + 3)
                if not first:
                    dve.wait_ge(act_lo_done, 2 * m)
                dve.scalar_tensor_tensor(out=prod_a[:], in0=pU[1][:], scalar=1.0 / W_SCALE, in1=silu_a[:],
                                         op0=ALU.mult, op1=ALU.mult).then_inc(act_done, 1)
                dve.wait_ge(silu_done, 2 * m + 2)
                dve.scalar_tensor_tensor(out=prod_c[:], in0=pU[2][64:128, :], scalar=1.0 / W_SCALE,
                                         in1=silu_c[:], op0=ALU.mult, op1=ALU.mult).then_inc(act_done, 1)

            def product_lo(dve, m):
                dve.wait_ge(act_hi_done, 2 * m + 1)
                dve.tensor_tensor(acta_lo[:], prod_a[:], acta_hi[:], ALU.subtract).then_inc(act_lo_done, 1)
                dve.wait_ge(act_hi_done, 2 * m + 2)
                dve.tensor_tensor(actc[64:128, :], prod_c[:], actc[0:64, :], ALU.subtract).then_inc(act_lo_done, 1)

            def copy_similarity(act, tile):
                act.wait_ge(sim_ready, tile + 1)
                if not isinstance(tile, int) or tile >= 1:
                    act.wait_ge(sim_taken, tile)
                act.activation(sim_next, pS[:], ACT.Copy, scale=1.0 / (4.0 * 32.0 ** 0.5)).then_inc(sim_copied, 1)

            def take_similarity(dve, tile):
                hold(dve, sim_copied, tile + 1)
                dve.tensor_copy(sim, sim_next).then_inc(sim_taken, 1)
                hold(dve, sim_taken, tile + 1)

            def search(dve, tile, first, last):
                for r in range(first, last):
                    step = SEL_STEPS * tile + 2 * r
                    src = sim if r == 0 else sim_work
                    if r >= 1:
                        hold(dve, sel_step, step)
                    dve.max(sim_top[:], src).then_inc(sel_step, 1)
                    if r < ROUNDS:
                        hold(dve, sel_step, step + 1)
                        dve.match_replace(sim_work, sim_top[:], src, NEG).then_inc(sel_step, 1)

            def keep(dve, tile):
                dve.wait_ge(sel_step, SEL_STEPS * tile + SEL_STEPS)
                dve.wait_ge(sim_sig_done, tile + 1)
                at = (K_SEL - 1) % 8
                dve.scalar_tensor_tensor(out=sim_work, in0=sim, scalar=sim_top[:, at:at + 1],
                                         in1=sim_sig, op0=ALU.is_ge, op1=ALU.mult).then_inc(kept_done, 1)
                dve.wait_ge(kept_done, tile + 1)
                dve.tensor_scalar(tile_of(learned, tile), sim_work, gam[:, 2:3], None, ALU.mult)\
                    .then_inc(learned_done, 1)

            def similarity_sigmoid(act, tile):
                act.wait_ge(sim_taken, tile + 1)
                act.activation(sim_sig, sim, ACT.Sigmoid).then_inc(sim_sig_done, 1)

            with nc.Block() as block:
                @block.sync
                def _(sp):
                    for n in range(2):
                        cols = slice(n * F, (n + 1) * F)
                        if n == 1:
                            sp.wait_ge(w_lo_done, 5)
                        load(sp, L0_ffn_sg[:, cols], L0_ffn_su[:, cols], L0_ffn_sd[cols, :])

                @block.gpsimd
                def _(pool):
                    for t in range(NT):
                        for k in range(TOPK):
                            pool.indirect_dma_start(out=table_d, out_offset=bass.IndirectOffsetOnAxis(
                                ap=place[:, t, k:k + 1], axis=0), in_=pairs[:, t, k, :], in_offset=None)\
                                .then_inc(table_written, 16)
                    pool.wait_ge(table_written, 16 * NT * TOPK)
                    pool.dma_start(table[:].rearrange("p s w -> p (s w)"),
                                   table_d.rearrange("(p s) w -> p (s w)", p=P)).then_inc(table_in, 16)

                @block.tensor
                def _(pe):
                    for m in range(SHARED):
                        n, g = m // GB, m % GB
                        if g == 0:
                            pe.wait_ge(w_lo_done, 5 * n + 5)
                        if m >= 1:
                            pe.wait_ge(act_done, 2 * m)
                        for col, bank in ((0, 0), (2, 2), (1, 1)):
                            up_columns(pe, m, 2 + n, col, bank, hT_hi, hT_lo, g)
                        if m >= 1:
                            pe.wait_ge(act_lo_done, 2 * m)
                            for t in range(TPB):
                                down_tile(pe, m - 1, 2 + (m - 1) // GB, t)
                        if g == 0:
                            if n == 1:
                                pe.wait_ge(sim_copied, 1)
                            similarity(pe, n)
                    pe.wait_ge(act_lo_done, 2 * SHARED)
                    for t in range(TPB):
                        down_tile(pe, SHARED - 1, 3, t)

                @block.scalar
                def _(act):
                    split_hi(act, 2, 0)
                    for m in range(SHARED):
                        n, g = m // GB, m % GB
                        silu(act, m, 0)
                        silu(act, m, 1)
                        product_hi(act, m, m == 0)
                        if g == 0:
                            copy_similarity(act, n)
                        if m == 1:
                            split_hi(act, 3, 1)
                        if g == 1:
                            similarity_sigmoid(act, n)

                @block.vector
                def _(dve):
                    def add(m):
                        for t in range(TPB):
                            tile = TPB * (m % GB) + t
                            dve.wait_ge(down_ready, TPB * m + t + 1)
                            dve.scalar_tensor_tensor(out=xres[:, tile, :], in0=pY[t][:], scalar=1.0 / W_SCALE,
                                                     in1=xres[:, tile, :], op0=ALU.mult, op1=ALU.add).then_inc(added, 1)

                    dve.sem_inc(added, TPB)
                    split_lo(dve, 2, 0)
                    for m in range(SHARED):
                        n, g = m // GB, m % GB
                        products(dve, m, m == 0)
                        product_lo(dve, m)
                        if m == 1:
                            split_lo(dve, 3, 1)
                        if m >= 1:
                            add(m - 1)
                        if g == 0:
                            take_similarity(dve, n)
                        per = -(-(ROUNDS + 1) // GB)
                        search(dve, n, per * g, min(per * (g + 1), ROUNDS + 1))
                        if g == GB - 1:
                            keep(dve, n)
                    add(SHARED - 1)

            def transpose_tile(pe, t):
                for c in range(KC):
                    mm = pe.transpose(pS[:, c * P:(c + 1) * P], rows[:, t, c::KC], ident[:])
                mm.then_inc(xT_ready, 1)

            def pe_step(pe, u, j, ahead, tile):
                m = SHARED + u

                def transposes(t):
                    pe.wait_ge(gathered[t], 16 * (u + 3))
                    pe.wait_ge(xT_lo_done, TPB * (u + 2) + t)
                    transpose_tile(pe, t)

                if ahead >= 1:
                    pe.wait_ge(w_lo_done, 5 * (u + 3) + 5)
                    pe.wait_ge(act_done, 2 * m + 2)
                    pe.wait_ge(xT_lo_done, TPB * (u + 2))
                    for t, (col, bank) in enumerate(((0, 0), (2, 2), (1, 1))):
                        def midway():
                            if j == 0 and t == 0:
                                pe.wait_ge(sim_copied, tile + 1)
                            if ahead == 2:
                                transposes(t)

                        up_columns(pe, m + 1, (j + 1) % 4, col, bank, *xT[(j + 1) % 2], 0, midway)
                if j >= 0:
                    pe.wait_ge(act_lo_done, 2 * m + 2)
                    for t in range(TPB):
                        if t == 1 and ahead == 2:
                            transposes(3)
                        down_tile(pe, m, j, t)
                elif ahead == 2:
                    transposes(3)
                if j in (-1, STEPS - 1) and ahead == 2:
                    pe.wait_ge(xT_lo_done, KC * (u + 2) + KC)
                    similarity(pe, tile + 1)

            def tokens_of(half, j, t):
                return xT[j % 2][half][:, :, t * P:(t + 1) * P]

            def tokens_hi(act, u, j, t):
                act.wait_ge(xT_ready, TPB * u + t + 1)
                act.activation(tokens_of(0, j, t), pS[:].rearrange("p (c s) -> p c s", c=KC), ACT.Copy)\
                    .then_inc(xT_hi_done, 1)

            def tokens_lo(dve, u, j, t):
                dve.wait_ge(xT_hi_done, TPB * u + t + 1)
                dve.tensor_tensor(tokens_of(1, j, t), pS[:].rearrange("p (c s) -> p c s", c=KC), tokens_of(0, j, t),
                                  ALU.subtract).then_inc(xT_lo_done, 1)

            def act_step(act, u, j, ahead, sigmoid, tile):
                m = SHARED + u
                two = ahead == 2
                if two:
                    tokens_hi(act, u + 2, j + 2, 0)
                    split_hi(act, (j + 2) % 4, u + 4)
                if ahead >= 1:
                    silu(act, m + 1, 0)
                if two:
                    tokens_hi(act, u + 2, j + 2, 1)
                if ahead >= 1:
                    silu(act, m + 1, 1)
                if two:
                    tokens_hi(act, u + 2, j + 2, 2)
                    tokens_hi(act, u + 2, j + 2, 3)
                if sigmoid:
                    similarity_sigmoid(act, tile)
                if j >= 0:
                    if not isinstance(u, int) or u >= 1:
                        hold(act, scattered, 64 * u)
                    for t in range(TPB):
                        act.wait_ge(down_ready, TPB * m + t + 1)
                        act.activation(out_rows[:, t, :], pY[t][:], ACT.Copy).then_inc(added, 1)
                if ahead >= 1:
                    product_hi(act, m + 1)
                if j in (-1, STEPS - 1) and ahead == 2:
                    copy_similarity(act, tile + 1)

            def dve_step(dve, u, j, ahead, tile):
                m = SHARED + u
                per = -(-(ROUNDS + 1) // STEPS)

                def part_of_search(first, last):
                    if j >= 0:
                        search(dve, tile, min(per * j + first, ROUNDS + 1), min(per * j + last, ROUNDS + 1))

                if ahead == 2:
                    tokens_lo(dve, u + 2, j + 2, 0)
                    split_lo(dve, (j + 2) % 4, u + 4)
                if j == 0:
                    take_similarity(dve, tile)
                if ahead == 2:
                    tokens_lo(dve, u + 2, j + 2, 1)
                part_of_search(0, 1)
                if ahead == 2:
                    tokens_lo(dve, u + 2, j + 2, 2)
                part_of_search(1, 2)
                if ahead >= 1:
                    products(dve, m + 1)
                if ahead == 2:
                    tokens_lo(dve, u + 2, j + 2, 3)
                part_of_search(2, per)
                if ahead >= 1:
                    product_lo(dve, m + 1)
                if j == STEPS - 1:
                    keep(dve, tile)

            def gather(pool, u, first=False):
                for t in range(TPB):
                    if not first:
                        hold(pool, xT_ready, TPB * u - TPB + t + 1)
                    pool.tensor_copy(gather_at[:, t, :], table[:, bass.ds(TPB * u + t, 1), :]
                                     .rearrange("p a w -> p (a w)")).then_inc(gather_index, 1)
                    hold(pool, gather_index, TPB * u + t + 1)
                    pool.indirect_dma_start(out=rows[:, t, :], out_offset=None, in_=h_rows,
                                            in_offset=bass.IndirectOffsetOnAxis(ap=gather_at[:, t, 0:1], axis=0),
                                            bounds_check=NT * P - 1, oob_is_err=False).then_inc(gathered[t], 16)

            def scatter(pool, u):
                if not isinstance(u, int) or u >= 1:
                    hold(pool, scattered, 64 * u)
                pool.tensor_copy(scatter_at[:], table[:, bass.ds(TPB * u, TPB), :]).then_inc(scatter_index, 1)
                hold(pool, scatter_index, u + 1)
                hold(pool, added, TPB * (SHARED + u) + 2 * TPB)
                for t in range(TPB):
                    pool.indirect_dma_start(out=choice_rows, out_offset=bass.IndirectOffsetOnAxis(
                        ap=scatter_at[:, t, 1:2], axis=0), in_=out_rows[:, t, :], in_offset=None,
                        bounds_check=NT * P * TOPK - 1, oob_is_err=False).then_inc(scattered, 16)

            LAST = UNITS // STEPS - 1

            def steps_of(it):
                for j in range(STEPS):
                    u = STEPS * it + j
                    yield u, j, min(2, UNITS - 1 - u) if isinstance(it, int) else 2

            with nc.Block() as block:
                @block.sync
                def _(sp):
                    def unit(u):
                        e = sp.value_load(unit_expert[0:1, bass.ds(u, 1)], min_val=0, max_val=E - 1)
                        sp.wait_ge(w_lo_done, 5 * (u + 2))
                        load(sp, *[w[bass.ds(e, 1)].rearrange("a r f -> (a r) f")
                                   for w in (L0_ffn_wg, L0_ffn_wu, L0_ffn_wd)])

                    with sp.Fori(0, UNITS) as u:
                        unit(u)

                @block.gpsimd
                def _(pool):
                    pool.memset(rows, 0.0).then_inc(rows_zeroed, 1)
                    pool.wait_ge(rows_zeroed, 1)
                    gather(pool, 0, first=True)
                    gather(pool, 1)
                    gather(pool, 2)

                    def iteration(it):
                        for u, j, ahead in steps_of(it):
                            more = not isinstance(u, int) or u + 3 < UNITS
                            if more:
                                gather(pool, u + 3)
                            scatter(pool, u)

                    iteration(0)
                    with pool.Fori(1, LAST) as it:
                        iteration(it)
                    iteration(LAST)
                    pool.wait_ge(scattered, 64 * UNITS)

                @block.tensor
                def _(pe):
                    for t in range(TPB):
                        pe.wait_ge(gathered[t], 16)
                        if t >= 1:
                            pe.wait_ge(xT_lo_done, t)
                        transpose_tile(pe, t)
                    pe_step(pe, -1, -1, 2, SIM_SHARED - 1)

                    def iteration(it):
                        for u, j, ahead in steps_of(it):
                            pe_step(pe, u, j, ahead, SIM_SHARED + it)

                    iteration(0)
                    with pe.Fori(1, LAST) as it:
                        iteration(it)
                    iteration(LAST)

                @block.scalar
                def _(act):
                    for c in range(KC):
                        tokens_hi(act, 0, 0, c)
                    split_hi(act, 0, 2)
                    act_step(act, -1, -1, 2, False, SIM_SHARED - 1)

                    def iteration(it):
                        for u, j, ahead in steps_of(it):
                            act_step(act, u, j, ahead, j == 0, SIM_SHARED + it)

                    iteration(0)
                    with act.Fori(1, LAST) as it:
                        iteration(it)
                    iteration(LAST)

                @block.vector
                def _(dve):
                    for c in range(KC):
                        tokens_lo(dve, 0, 0, c)
                    split_lo(dve, 0, 2)
                    dve_step(dve, -1, -1, 2, SIM_SHARED - 1)

                    def iteration(it):
                        for u, j, ahead in steps_of(it):
                            dve_step(dve, u, j, ahead, SIM_SHARED + it)

                    iteration(0)
                    with dve.Fori(1, LAST) as it:
                        iteration(it)
                    iteration(LAST)

        early.close()
        nc.clear_and_free_semaphores(signals)
        nc.all_engine_barrier()
        mid = whole.enter_context(ExitStack())
        def sbm(name, shape, dt=F32):
            return mid.enter_context(nc.sbuf_tensor(name, shape, dt))
        mix_hi = sbm("mix_hi", [P, KC, D], F16)
        mix_lo = sbm("mix_lo", [P, KC, D], F16)
        mix_bias = sbm("mix_bias", [2, D], F16)
        mask_rows = sbm("mask_rows", [P, TPB, S])
        mask_keys = sbm("mask_keys", [P, B, S])

        weights_in = sem("weights_in")
        factor_in = sem("factor_in")
        factor_sum = sem("factor_sum")
        choices_in = [sem("choices_in_even"), sem("choices_in_odd")]
        choices_added = sem("choices_added")
        ones_set = sem("ones_set")
        prep = sem("prep")
        prep_hi = sem("prep_hi")
        halves_done = sem("halves_done")
        prep_tern = sem("prep_tern")
        tern_in = sem("tern_in")
        abs_done = sem("abs_done")
        total_ready = sem("total_ready")
        rounded = sem("rounded")
        turned = sem("turned")
        turn_copied = sem("turn_copied")
        bias_moved = sem("bias_moved")

        with ExitStack() as scope, nc.Block() as block:
            def sbl(name, shape, dt=F32):
                return scope.enter_context(nc.sbuf_tensor(name, shape, dt))
            factor = sbl("factor", [P, 8, KC, D // 4])
            choice = [sbl(f"choice{i}", [P, TOPK, D]) for i in range(2)]
            choice_tiles = choice_rows.rearrange("(t p k) d -> t p (k d)", p=P, k=TOPK)
            mix_f = sbl("mix_f", [P, KC, D])
            mask_words = sbl("mask_words", [P, TPB, S // 4], I32)
            keys_words = sbl("keys_words", [P, B, S // 4], I32)
            gate2_f = sbl("gate2_f", [P, KC, D])
            row_scratch = sbl("row_scratch", [1, 2, D])
            bias_halves = sbl("bias_halves", [1, 2, 2, D], F16)

            @block.sync
            def _(sp):
                def small_loads():
                    sp.dma_start(gate2_f[:], L2_ffn_gate_w.rearrange("(p c) e -> p c e", c=KC)).then_inc(weights_in, 16)
                    sp.dma_start(mask_words[:], mask_SxS2_bk1.rearrange("(t p) s -> p t s", p=P)).then_inc(weights_in, 16)
                    for b in range(B):
                        sp.dma_start(keys_words[:, b, :], mask_BxS2_bf0[b:b + 1, :].to_broadcast([P, S // 4]))\
                            .then_inc(weights_in, 16)
                    for i, bias in enumerate((L1_ffn_bias, L2_ffn_gate_b)):
                        sp.dma_start(row_scratch[0:1, i, :], bias.rearrange("(a d) -> a d", a=1)).then_inc(weights_in, 16)

                for tile in range(NT):
                    if tile >= 2:
                        sp.wait_ge(choices_added, TOPK * (tile - 1))
                    sp.dma_start(choice[tile % 2][:].rearrange("p k d -> p (k d)"), choice_tiles[tile])\
                        .then_inc(choices_in[tile % 2], 16)
                    if tile == 3:
                        small_loads()
                sp.wait_ge(halves_done, 1)
                for i, dst in enumerate((mix_bias, gate2_bias)):
                    for half in range(2):
                        sp.dma_start(dst[half:half + 1, :], bias_halves[0:1, i, half, :]).then_inc(bias_moved, 16)
                sp.wait_ge(bias_moved, 64)

            @block.scalar
            def _(act):
                for q in range(4):
                    if q >= 1:
                        act.wait_ge(factor_sum, 7 * q)
                    for r in range(8):
                        quarter = L1_ffn_factors[r].rearrange("(p c) e -> p c e", c=KC)[:, :, q * P:(q + 1) * P]
                        act.dma_start(factor[:, r, :, :], quarter).then_inc(factor_in, 16)
                act.wait_ge(factor_sum, 28)
                act.activation(mix_hi[:], mix_f[:], ACT.Copy, scale=G_SCALE / 8.0 ** 0.5).then_inc(prep_hi, 1)
                act.wait_ge(weights_in, 128)
                act.activation(gate2_hi[:], gate2_f[:], ACT.Copy, scale=G_SCALE).then_inc(prep_hi, 1)

            @block.gpsimd
            def _(pool):
                for q in range(4):
                    pool.wait_ge(factor_in, 16 * 8 * (q + 1))
                    part = mix_f[:, :, q * P:(q + 1) * P]
                    for r in range(1, 8):
                        if r >= 2:
                            pool.wait_ge(factor_sum, 7 * q + r - 1)
                        pool.tensor_tensor(part, factor[:, 0, :, :] if r == 1 else part, factor[:, r, :, :], ALU.add)\
                            .then_inc(factor_sum, 1)

            @block.vector
            def _(dve):
                steps = [0]

                def done(*instructions):
                    for ins in instructions:
                        ins.then_inc(prep, 1)
                        steps[0] += 1
                    dve.wait_ge(prep, steps[0])

                for tile in range(NT):
                    dve.wait_ge(choices_in[tile % 2], 16 * (tile // 2 + 1))
                    for n in range(TOPK):
                        if tile or n:
                            dve.wait_ge(choices_added, TOPK * tile + n)
                        dve.scalar_tensor_tensor(out=xres[:, tile, :], in0=choice[tile % 2][:, n, :],
                                                 scalar=gate6[:, tile, n:n + 1], in1=xres[:, tile, :],
                                                 op0=ALU.mult, op1=ALU.add).then_inc(choices_added, 1)
                dve.memset(ones_h[:], 1.0).then_inc(ones_set, 1)
                dve.wait_ge(weights_in, 128)
                dve.wait_ge(prep_hi, 2)
                done(dve.scalar_tensor_tensor(out=mix_lo[:], in0=mix_f[:], scalar=G_SCALE / 8.0 ** 0.5,
                                              in1=mix_hi[:], op0=ALU.mult, op1=ALU.subtract),
                     dve.scalar_tensor_tensor(out=gate2_lo[:], in0=gate2_f[:], scalar=G_SCALE, in1=gate2_hi[:],
                                              op0=ALU.mult, op1=ALU.subtract))
                for i in range(2):
                    row = row_scratch[0:1, i, :]
                    done(dve.tensor_scalar(bias_halves[0:1, i, 0, :], row, G_SCALE, None, ALU.mult))
                    done(dve.scalar_tensor_tensor(out=bias_halves[0:1, i, 1, :], in0=row, scalar=G_SCALE,
                                                  in1=bias_halves[0:1, i, 0, :], op0=ALU.mult, op1=ALU.subtract))
                dve.sem_inc(halves_done, 1)
                done(dve.tensor_scalar(mask_rows[:], mask_words[:].bitcast(U8), MASKED, None, ALU.mult),
                     dve.tensor_scalar(mask_keys[:], keys_words[:].bitcast(U8), MASKED, None, ALU.mult))

        with ExitStack() as scope, nc.Block() as block:
            def sbl(name, shape, dt=F32):
                return scope.enter_context(nc.sbuf_tensor(name, shape, dt))
            tern_f = [sbl(f"tern_f{i}", [P, 8, D]) for i in range(2)]
            tern_b = sbl("tern_b", [P, 8, D], BF16)
            abs_sum = sbl("abs_sum", [P, 2])
            pA = psum_banks(scope, "prepA", 1)[0]
            pB = psum_banks(scope, "prepB", 4, BF16)

            @block.sync
            def _(sp):
                sp.dma_start(tern_f[0][:], L3_ffn_w_up.rearrange("(o p) i -> p o i", p=P)).then_inc(tern_in, 16)
                sp.dma_start(tern_f[1][:].rearrange("p (o j) i -> p o (j i)", o=4),
                             L3_ffn_w_down.rearrange("(o p) i -> p o i", p=P)).then_inc(tern_in, 16)

            @block.vector
            def _(dve):
                steps = [0]

                def done(*instructions):
                    for ins in instructions:
                        ins.then_inc(prep_tern, 1)
                        steps[0] += 1
                    dve.wait_ge(prep_tern, steps[0])

                for i in range(2):
                    dve.wait_ge(tern_in, 32)
                    flat = tern_f[i][:].rearrange("p o i -> p (o i)")
                    dve.tensor_reduce(abs_sum[:, i:i + 1], flat, AX.X, ALU.add, apply_absolute_value=True)\
                        .then_inc(abs_done, 1)
                    dve.wait_ge(total_ready, i + 1)
                    mean = tern[:, 2 * i + 1:2 * i + 2]
                    done(dve.tensor_scalar(mean, pA[:, i:i + 1], 1.0 / (IUP * D), 1e-5, ALU.mult, ALU.max))
                    done(dve.reciprocal(tern[:, 2 * i:2 * i + 1], mean))
                    done(dve.tensor_scalar(flat, flat, tern[:, 2 * i:2 * i + 1], 1.0, ALU.mult, ALU.min))
                    done(dve.tensor_scalar(flat, flat, -1.0, MAGIC, ALU.max, ALU.add))
                    dve.tensor_scalar(tern_b[:].rearrange("p o i -> p (o i)"), flat, MAGIC, None, ALU.subtract)\
                        .then_inc(rounded, 1)
                    for k in range(8):
                        dve.wait_ge(turned, 8 * i + k + 1)
                        dst = (up_t[:, :, k * P:(k + 1) * P], dn_t[:, k, :].rearrange("p (c o) -> p c o", c=4))[i]
                        dve.tensor_copy(dst, pB[k % 4][:, 0:D].rearrange("p (c o) -> p c o", c=4))\
                            .then_inc(turn_copied, 1)

            @block.tensor
            def _(pe):
                for i in range(2):
                    pe.wait_ge(abs_done, i + 1)
                    pe.matmul(pA[:, i:i + 1], ones[:], abs_sum[:, i:i + 1], start=True, stop=True)\
                        .then_inc(total_ready, 1)
                    pe.wait_ge(rounded, i + 1)
                    for k in range(8):
                        if 8 * i + k >= 4:
                            pe.wait_ge(turn_copied, 8 * i + k - 3)
                        for c in range(4):
                            if i == 0:
                                src = tern_b[:, k, c::KC]
                            else:
                                src = tern_b[:].rearrange("p (o j) i -> p o (j i)", o=4)[:, c, k::8]
                            m = pe.transpose(pB[k % 4][:, c * P:(c + 1) * P], src, ident_b[:])
                        m.then_inc(turned, 1)

        def transposed_split(pe, source, banks, ready):
            for c in range(KC):
                for t in range(TPB):
                    m = pe.transpose(banks[c][:, t * P:(t + 1) * P], source[:, t, c::KC], ident[:])
                m.then_inc(ready, 1)

        def dense(pe, out, t, a_hi, a_lo, w_hi, w_lo, bias):
            tok = slice(t * P, (t + 1) * P)
            for c in range(KC):
                split_matmul(pe, out, a_hi[:, c, tok], a_lo[:, c, tok], w_hi[:, c, :], w_lo[:, c, :], c == 0, False)
            return pe.matmul(out, ones_h[:], bias[:], start=False, stop=True)

        learned_copied = sem("learned_copied")
        learned_turned = sem("learned_turned")
        l1_scale_done = sem("l1_scale_done")
        l1_half = sem("l1_half")
        x3_done = sem("x3_done")
        n3_done = sem("n3_done")
        n3T_ready = sem("n3T_ready")
        n3T_hi_done = sem("n3T_hi_done")
        n3T_lo_done = sem("n3T_lo_done")
        mixed_ready = sem("mixed_ready")
        x4_done = sem("x4_done")
        n4_done = sem("n4_done")
        scores2_ready = sem("scores2_ready")
        scores2_step = sem("scores2_step")
        max2_done = sem("max2_done")
        negmax2_done = sem("negmax2_done")
        exp2_done = sem("exp2_done")
        recip2_done = sem("recip2_done")
        x5_done = sem("x5_done")

        with ExitStack() as scope:
            def sbl(name, shape, dt=F32):
                return scope.enter_context(nc.sbuf_tensor(name, shape, dt))
            l1_in = Norm("l1_in", sbl, sem, 1e-5)
            l1_mid = Norm("l1_mid", sbl, sem, 1e-5)
            l2_in = Norm("l2_in", sbl, sem, 1e-5)
            xw = sbl("xw", [P, TPB, D])
            lw = sbl("lw", [P, TPB, S])
            nrm = sbl("nrm", [P, TPB, D])
            nT_hi = sbl("nT_hi", [P, KC, S], F16)
            nT_lo = sbl("nT_lo", [P, KC, S], F16)
            mul1 = sbl("mul1", [P, TPB])
            add1 = sbl("add1", [P, TPB])
            max2 = sbl("max2", [P, TPB])
            negmax2 = sbl("negmax2", [P, TPB])
            sum2 = sbl("sum2", [P, TPB])
            recip2 = sbl("recip2", [P, TPB])
            live2 = sbl("live2", [P, TPB])
            pT = psum_banks(scope, "tail1T", 4)
            pG = psum_banks(scope, "tail1G", 4)
            with nc.Fori(0, B) as b, nc.Block() as block:
                @block.tensor
                def _(pe):
                    pe.wait_ge(learned_copied, TPB * b + TPB)
                    for t in range(TPB):
                        for j in range(TPB):
                            m = pe.transpose(pG[t][:, j * P:(j + 1) * P], lw[:, j, t * P:(t + 1) * P], ident[:])
                        m.then_inc(learned_turned, 1)
                    pe.wait_ge(n3_done, TPB * b + TPB)
                    transposed_split(pe, nrm, pT, n3T_ready)
                    pe.wait_ge(n3T_lo_done, KC * b + KC)
                    for t in range(TPB):
                        dense(pe, pG[t][:], t, nT_hi, nT_lo, mix_hi, mix_lo, mix_bias).then_inc(mixed_ready, 1)
                    for t in range(TPB):
                        rows, cols = bass.ds(b * S + t * P, P), bass.ds(b * S, S)
                        split_matmul(pe, pT[t][:], proj_hi[2][:, rows], proj_lo[2][:, rows], proj_hi[3][:, cols],
                                     proj_lo[3][:, cols], True, True).then_inc(scores2_ready, 1)

                @block.gpsimd
                def _(pool):
                    for norm in (l1_in, l1_mid, l2_in):
                        norm.on_gpsimd(pool, minus_half, b)

                @block.scalar
                def _(act):
                    for t in range(TPB):
                        act.activation(lw[:, t, :], tile_of(learned, b * TPB + t), ACT.Copy).then_inc(learned_copied, 1)
                    for c in range(KC):
                        act.wait_ge(n3T_ready, KC * b + c + 1)
                        act.activation(nT_hi[:, c, :], pT[c][:], ACT.Copy).then_inc(n3T_hi_done, 1)
                    act.wait_ge(negmax2_done, b + 1)
                    for t in range(TPB):
                        act.activation(lw[:, t, :], lw[:, t, :], ACT.Exp, bias=negmax2[:, t:t + 1],
                                       accum_out=sum2[:, t:t + 1]).then_inc(exp2_done, 1)

                @block.vector
                def _(dve):
                    l1_in.on_vector(dve, lambda t: tile_of(xres, b * TPB + t), b, None)
                    dve.tensor_scalar(mul1[:], l1_in.rstd[:], gam[:, 3:4], 1.0, ALU.mult, ALU.add).then_inc(l1_scale_done, 1)
                    dve.tensor_scalar(add1[:], l1_in.shift[:], gam[:, 3:4], None, ALU.mult).then_inc(l1_scale_done, 1)
                    dve.wait_ge(l1_scale_done, 2 * b + 2)
                    for t in range(TPB):
                        dve.wait_ge(learned_copied, TPB * b + t + 1)
                        dve.scalar_tensor_tensor(out=xw[:, t, :], in0=tile_of(xres, b * TPB + t), scalar=mul1[:, t:t + 1],
                                                 in1=lw[:, t, :], op0=ALU.mult, op1=ALU.add).then_inc(l1_half, 1)
                    dve.wait_ge(l1_half, TPB * b + TPB)
                    for t in range(TPB):
                        dve.wait_ge(learned_turned, TPB * b + t + 1)
                        dve.scalar_tensor_tensor(out=xw[:, t, :], in0=xw[:, t, :], scalar=add1[:, t:t + 1],
                                                 in1=pG[t][:], op0=ALU.add, op1=ALU.add).then_inc(x3_done, 1)
                    l1_mid.on_vector(dve, lambda t: xw[:, t, :], b, (x3_done, TPB * b + TPB))
                    for t in range(TPB):
                        dve.tensor_scalar(nrm[:, t, :], xw[:, t, :], l1_mid.rstd[:, t:t + 1],
                                          l1_mid.shift[:, t:t + 1], ALU.mult, ALU.add).then_inc(n3_done, 1)
                    for c in range(KC):
                        dve.wait_ge(n3T_hi_done, KC * b + c + 1)
                        dve.tensor_tensor(nT_lo[:, c, :], pT[c][:], nT_hi[:, c, :], ALU.subtract).then_inc(n3T_lo_done, 1)
                    for t in range(TPB):
                        dve.wait_ge(mixed_ready, TPB * b + t + 1)
                        dve.scalar_tensor_tensor(out=xw[:, t, :], in0=pG[t][:], scalar=1.0 / G_SCALE,
                                                 in1=xw[:, t, :], op0=ALU.mult, op1=ALU.add).then_inc(x4_done, 1)
                    l2_in.on_vector(dve, lambda t: xw[:, t, :], b, (x4_done, TPB * b + TPB))
                    for t in range(TPB):
                        dve.tensor_scalar(nrm[:, t, :], xw[:, t, :], l2_in.rstd[:, t:t + 1],
                                          l2_in.shift[:, t:t + 1], ALU.mult, ALU.add).then_inc(n4_done, 1)
                    dve.wait_ge(n4_done, TPB * b + TPB)
                    for t in range(TPB):
                        dve.wait_ge(scores2_ready, TPB * b + t + 1)
                        dve.scalar_tensor_tensor(out=lw[:, t, :], in0=pT[t][:], scalar=C ** -0.5, in1=nrm[:, t, :],
                                                 op0=ALU.mult, op1=ALU.mult).then_inc(scores2_step, 1)
                    dve.wait_ge(scores2_step, 2 * TPB * b + TPB)
                    for t in range(TPB):
                        dve.tensor_tensor(lw[:, t, :], lw[:, t, :], tile_of(mask_keys, b), ALU.add).then_inc(scores2_step, 1)
                    hold(dve, scores2_step, 2 * TPB * b + 2 * TPB)
                    for t in range(TPB):
                        dve.tensor_tensor_reduce(lw[:, t, :], lw[:, t, :], mask_rows[:, t, :], 1.0, NEG, ALU.add,
                                                 ALU.max, max2[:, t:t + 1]).then_inc(max2_done, 1)
                    dve.wait_ge(max2_done, TPB * b + TPB)
                    dve.tensor_scalar(negmax2[:], max2[:], -1.0, None, ALU.mult).then_inc(negmax2_done, 1)
                    dve.tensor_scalar(live2[:], max2[:], 0.5 * MASKED, None, ALU.is_ge).then_inc(recip2_done, 1)
                    dve.wait_ge(recip2_done, 4 * b + 1)
                    dve.wait_ge(exp2_done, TPB * b + TPB)
                    dve.tensor_tensor(sum2[:], sum2[:], live2[:], ALU.mult).then_inc(recip2_done, 1)
                    dve.wait_ge(recip2_done, 4 * b + 2)
                    dve.reciprocal(recip2[:], sum2[:]).then_inc(recip2_done, 1)
                    dve.wait_ge(recip2_done, 4 * b + 3)
                    dve.tensor_tensor(recip2[:], recip2[:], live2[:], ALU.mult).then_inc(recip2_done, 1)
                    dve.wait_ge(recip2_done, 4 * b + 4)
                    for t in range(TPB):
                        dve.scalar_tensor_tensor(out=tile_of(xres, b * TPB + t), in0=lw[:, t, :],
                                                 scalar=recip2[:, t:t + 1], in1=xw[:, t, :], op0=ALU.mult,
                                                 op1=ALU.add).then_inc(x5_done, 1)
        mid.close()
        middle.close()
        bc_rows = sb("bc_rows", [P, B, D])
        ctxs = sb("ctxs_again", [P, NT, C])
        out_gamma = sb("out_gamma", [P, D])
        out_beta = sb("out_beta", [P, D])
        values_hi = sb("values_hi", [P, NT, KVH, DH + 1], F16)
        values_lo = sb("values_lo", [P, NT, KVH, DH + 1], F16)

        th_in = sem("th_in")
        last_in = sem("last_in")
        values_done = sem("values_done")
        ctx_again = sem("ctx_again")
        th = sem("th")
        th_rstd = sem("th_rstd")
        last_ready = sem("last_ready")
        last_turned = sem("last_turned")
        agg_ready = sem("agg_ready")
        thn = sem("thn")
        th_rstd_step = sem("th_rstd_step")
        tn_turned = sem("tn_turned")
        d1_ready = sem("d1_ready")
        gelu_in = sem("gelu_in")
        gelu_done = sem("gelu_done")
        hid_turned = sem("hid_turned")
        hidT_done = sem("hidT_done")
        d2_ready = sem("d2_ready")
        final_turned = sem("final_turned")
        bc_ready = sem("bc_ready")
        bc_row_done = sem("bc_row_done")
        spread_ready = sem("spread_ready")
        bc_done = sem("bc_done")
        HC = HID // P
        STEPS_TH = 9
        with ExitStack() as scope, nc.Block() as block:
            def sbl(name, shape, dt=F32):
                return scope.enter_context(nc.sbuf_tensor(name, shape, dt))
            d1_w = sbl("d1_w", [P, KC, HID])
            d2_w = sbl("d2_w", [P, HC, D])
            agg_w = sbl("agg_w", [P, KC, D])
            bc_w = sbl("bc_w", [P, KC, D])
            d1_b = sbl("d1_b", [B, HID])
            vecs = sbl("vecs", [B, 7, D])
            last = sbl("last", [B, D])
            thought = sbl("thought", [B, D])
            tn = sbl("tn", [B, D])
            stats = sbl("th_stats", [B, 6])
            meanvar = sbl("th_meanvar", [B, 2])
            vareps = sbl("th_vareps", [B, 1])
            rstd = sbl("th_rstd_b", [B, 1])
            turned = sbl("th_turned", [P, KC, B])
            hid = sbl("hid", [B, HID])
            hidT = sbl("hidT", [P, HC, B])
            bc_row = sbl("bc_row", [B, D])
            chosen = sbl("chosen", [B, B, P])
            pL = psum_banks(scope, "thL", 1)[0]
            pD = psum_banks(scope, "thD", 1)[0]
            pH = psum_banks(scope, "thH", HID // D)
            pB = psum_banks(scope, "thB", 2)

            @block.sync
            def _(sp):
                sp.dma_start(ctxs[:], ctx_d).then_inc(ctx_again, 16)
                for b in range(B):
                    sp.dma_start(last[b:b + 1, :], xres[P - 1:P, TPB * b + TPB - 1, :]).then_inc(last_in, 16)
                for i, v in enumerate((L2_ffn_in_gamma, L2_ffn_in_beta, L2_ffn_agg_b, L2_ffn_pn_gamma, L2_ffn_pn_beta,
                                       L2_ffn_d2_b, L2_ffn_bc_b)):
                    sp.dma_start(vecs[:, i, :], v.rearrange("(a d) -> a d", a=1).to_broadcast([B, D])).then_inc(last_in, 16)
                sp.dma_start(agg_w[:], L2_ffn_agg_w.rearrange("(p c) e -> p c e", c=KC)).then_inc(last_in, 16)
                sp.dma_start(d1_b[:], L2_ffn_d1_b.rearrange("(a d) -> a d", a=1).to_broadcast([B, HID])).then_inc(th_in, 16)
                sp.dma_start(d1_w[:], L2_ffn_d1_w.rearrange("(p c) e -> p c e", c=KC)).then_inc(th_in, 16)
                sp.dma_start(d2_w[:], L2_ffn_d2_w.rearrange("(p m) e -> p m e", m=HC)).then_inc(th_in, 16)
                sp.dma_start(bc_w[:], L2_ffn_bc_w.rearrange("(p c) e -> p c e", c=KC)).then_inc(th_in, 16)
                for dst, v in ((out_gamma, L2_ffn_out_gamma), (out_beta, L2_ffn_out_beta)):
                    sp.dma_start(dst[:], v.rearrange("(a d) -> a d", a=1).to_broadcast([P, D])).then_inc(th_in, 16)
                sp.wait_ge(th_in, 96)

            @block.gpsimd
            def _(pool):
                heads = ctxs[:].rearrange("p t (g d) -> p t g d", d=DH)
                pool.wait_ge(ctx_again, 16)
                pool.memset(values_hi[:, :, :, DH:DH + 1], 1.0).then_inc(values_done, 1)
                pool.memset(values_lo[:, :, :, DH:DH + 1], 0.0).then_inc(values_done, 1)
                pool.tensor_copy(values_hi[:, :, :, 0:DH], heads).then_inc(values_done, 1)
                pool.wait_ge(values_done, 3)
                pool.tensor_tensor(values_lo[:, :, :, 0:DH], heads, values_hi[:, :, :, 0:DH], ALU.subtract)\
                    .then_inc(values_done, 1)
                for i in range(2):
                    pool.wait_ge(th, 4 * i + 3)
                    pool.tensor_tensor(rstd[:], vareps[:], minus_half[0:B, 0:1], ALU.pow).then_inc(th_rstd, 1)
                with pool.Fori(0, K_STEPS) as k:
                    pool.wait_ge(thn, STEPS_TH * k + 3)
                    pool.tensor_tensor(rstd[:], vareps[:], minus_half[0:B, 0:1], ALU.pow).then_inc(th_rstd_step, 1)

            @block.tensor
            def _(pe):
                def turn(rows, ready):
                    for c in range(KC):
                        m = pe.transpose(pL[:, c * B:(c + 1) * B], rows[:, c::KC], ident[0:B, 0:B])
                    m.then_inc(ready, 1)

                def dense_rows(out, rowsT, chunks, weights):
                    for c in range(chunks):
                        m = pe.matmul(out, rowsT[:, c, :], weights[c], start=c == 0, stop=c == chunks - 1)
                    return m

                pe.wait_ge(last_ready, 1)
                turn(last, last_turned)
                pe.wait_ge(th, 11)
                dense_rows(pD[0:B, :], turned, KC, [agg_w[:, c, :] for c in range(KC)]).then_inc(agg_ready, 1)
                pe.wait_ge(th_in, 96)
                with pe.Fori(0, K_STEPS) as k:
                    hold(pe, thn, STEPS_TH * k + 6)
                    turn(tn, tn_turned)
                    pe.wait_ge(thn, STEPS_TH * k + 7)
                    for n in range(HID // D):
                        dense_rows(pH[n][0:B, :], turned, KC, [d1_w[:, c, n * D:(n + 1) * D] for c in range(KC)])\
                            .then_inc(d1_ready, 1)
                    hold(pe, gelu_done, 4 * k + 4)
                    for m in range(HC):
                        mm = pe.transpose(pL[:, m * B:(m + 1) * B], hid[:, m::HC], ident[0:B, 0:B])
                    mm.then_inc(hid_turned, 1)
                    pe.wait_ge(hidT_done, k + 1)
                    dense_rows(pD[0:B, :], hidT, HC, [d2_w[:, m, :] for m in range(HC)]).then_inc(d2_ready, 1)
                pe.wait_ge(thn, STEPS_TH * K_STEPS)
                turn(thought, final_turned)
                pe.wait_ge(th, 13)
                dense_rows(pD[0:B, :], turned, KC, [bc_w[:, c, :] for c in range(KC)]).then_inc(bc_ready, 1)
                pe.wait_ge(bc_row_done, 2)
                for b in range(B):
                    if b >= 2:
                        pe.wait_ge(bc_done, b - 1)
                    pe.matmul(pB[b % 2][:], chosen[:, b, :], bc_row[:], start=True, stop=True).then_inc(spread_ready, 1)

            @block.scalar
            def _(act):
                with act.Fori(0, K_STEPS) as k:
                    for n in range(HID // D):
                        act.wait_ge(gelu_in, 4 * k + n + 1)
                        act.activation(hid[:, n * D:(n + 1) * D], hid[:, n * D:(n + 1) * D], ACT.Gelu)\
                            .then_inc(gelu_done, 1)

            @block.vector
            def _(dve):
                steps = [0]

                def done(*instructions):
                    for ins in instructions:
                        ins.then_inc(th, 1)
                        steps[0] += 1
                    dve.wait_ge(th, steps[0])

                dve.wait_ge(last_in, 16 * 12)
                for i, eps in enumerate((1e-5, 1e-6)):
                    done(dve.bn_stats(stats[:], last[:]))
                    done(dve.bn_aggr(meanvar[:], stats[:]))
                    done(dve.tensor_scalar(vareps[:], meanvar[:, 1:2], eps, None, ALU.add))
                    dve.wait_ge(th_rstd, i + 1)
                    done(dve.tensor_scalar(last[:], last[:], meanvar[:, 0:1], rstd[:, 0:1], ALU.subtract, ALU.mult))
                done(dve.tensor_tensor(last[:], last[:], vecs[:, 0, :], ALU.mult))
                done(dve.tensor_tensor(last[:], last[:], vecs[:, 1, :], ALU.add))
                dve.sem_inc(last_ready, 1)
                dve.wait_ge(last_turned, 1)
                done(dve.tensor_copy(turned[:].rearrange("p c b -> p (c b)"), pL[:, 0:KC * B]))
                dve.wait_ge(agg_ready, 1)
                done(dve.tensor_tensor(thought[:], pD[0:B, :], vecs[:, 2, :], ALU.add))
                dve.wait_ge(th_in, 96)
                with dve.Fori(0, K_STEPS) as k:
                    n = [0]

                    def step(ins):
                        ins.then_inc(thn, 1)
                        n[0] += 1
                        hold(dve, thn, STEPS_TH * k + n[0])

                    step(dve.bn_stats(stats[:], thought[:]))
                    step(dve.bn_aggr(meanvar[:], stats[:]))
                    step(dve.tensor_scalar(vareps[:], meanvar[:, 1:2], 1e-6, None, ALU.add))
                    dve.wait_ge(th_rstd_step, k + 1)
                    step(dve.tensor_scalar(tn[:], thought[:], meanvar[:, 0:1], rstd[:, 0:1], ALU.subtract, ALU.mult))
                    step(dve.tensor_tensor(tn[:], tn[:], vecs[:, 3, :], ALU.mult))
                    step(dve.tensor_tensor(tn[:], tn[:], vecs[:, 4, :], ALU.add))
                    dve.wait_ge(tn_turned, k + 1)
                    step(dve.tensor_copy(turned[:].rearrange("p c b -> p (c b)"), pL[:, 0:KC * B]))
                    for i in range(HID // D):
                        dve.wait_ge(d1_ready, 4 * k + i + 1)
                        dve.tensor_tensor(hid[:, i * D:(i + 1) * D], pH[i][0:B, :], d1_b[:, i * D:(i + 1) * D],
                                          ALU.add).then_inc(gelu_in, 1)
                    dve.wait_ge(hid_turned, k + 1)
                    dve.tensor_copy(hidT[:].rearrange("p m b -> p (m b)"), pL[:, 0:HC * B]).then_inc(hidT_done, 1)
                    dve.wait_ge(d2_ready, k + 1)
                    step(dve.tensor_tensor(thought[:], thought[:], pD[0:B, :], ALU.add))
                    step(dve.tensor_tensor(thought[:], thought[:], vecs[:, 5, :], ALU.add))
                dve.wait_ge(final_turned, 1)
                done(dve.tensor_copy(turned[:].rearrange("p c b -> p (c b)"), pL[:, 0:KC * B]))
                dve.tensor_copy(chosen[:], ident[0:B, 0:B].unsqueeze(2).to_broadcast([B, B, P])).then_inc(bc_row_done, 1)
                dve.wait_ge(bc_ready, 1)
                dve.tensor_tensor(bc_row[:], pD[0:B, :], vecs[:, 6, :], ALU.add).then_inc(bc_row_done, 1)
                for b in range(B):
                    dve.wait_ge(spread_ready, b + 1)
                    dve.tensor_copy(bc_rows[:, b, :], pB[b % 2][:]).then_inc(bc_done, 1)

        PAIR = QH // 2
        SLOT = 64
        ROWS = 3 * DH
        x5_copied = sem("x5_copied")
        beta_added = sem("beta_added")
        n5_done = sem("n5_done")
        n5T_ready = sem("n5T_ready")
        n5T_hi_done = sem("n5T_hi_done")
        n5T_lo_done = sem("n5T_lo_done")
        gate_ready = sem("gate_ready")
        gate_done = sem("gate_done")
        gated = sem("gated")
        x6_step = sem("x6_step")
        n6_done = sem("n6_done")
        q_hi_done = sem("q_hi_done")
        q_lo_done = sem("q_lo_done")
        q_pad_done = sem("q_pad_done")
        k_hi_done = sem("k_hi_done")
        k_lo_done = sem("k_lo_done")
        kT_ready = sem("kT_ready")
        kT_done = sem("kT_done")
        qT_ready = sem("qT_ready")
        qT_done = sem("qT_done")
        qT_odd_done = sem("qT_odd_done")
        s_ready = sem("s_ready")
        s16_done = sem("s16_done")
        halved = sem("halved")
        quartered = sem("quartered")
        max_done = sem("max_done")
        negmax_done = sem("negmax_done")
        negmaxT_ready = sem("negmaxT_ready")
        negmaxT_done = sem("negmaxT_done")
        negmax_moved = sem("negmax_moved")
        sT_ready = sem("sT_ready")
        exp_done = sem("exp_done")
        probs_hi0_done = sem("probs_hi0_done")
        probs_hi1_done = sem("probs_hi1_done")
        probs_lo_done = sem("probs_lo_done")
        probs_lo3_done = sem("probs_lo3_done")
        pv_ready = sem("pv_ready")
        recip_done = sem("recip_done")
        weighed_done = sem("weighed_done")
        x7_done = sem("x7_done")
        n7_done = sem("n7_done")
        amax_done = sem("amax_done")
        scale_step = sem("scale_step")
        quant_step = sem("quant_step")
        q7_done = sem("q7_done")
        q7T_ready = sem("q7T_ready")
        q7T_done = sem("q7T_done")
        hid_ready = sem("hid_ready")
        relu_done = sem("relu_done")
        hmax_done = sem("hmax_done")
        hscale_step = sem("hscale_step")
        hsq_done = sem("hsq_done")
        hquant_step = sem("hquant_step")
        hq_done = sem("hq_done")
        hqT_ready = sem("hqT_ready")
        hqT_done = sem("hqT_done")
        y_ready = sem("y_ready")
        x8_done = sem("x8_done")
        stored = sem("stored")
        k_ones_done = sem("k_ones_done")

        with ExitStack() as scope:
            def sbl(name, shape, dt=F32, scope=scope):
                return scope.enter_context(nc.sbuf_tensor(name, shape, dt))
            l2_ffn = Norm("l2_ffn", sbl, sem, 1e-5)
            l2_out = Norm("l2_out", sbl, sem, 1e-6)
            l3_in = Norm("l3_in", sbl, sem, 1e-5)
            l3_mid = Norm("l3_mid", sbl, sem, 1e-5)
            xw = sbl("xw2", [P, TPB, D])
            nrm = sbl("nrm2", [P, TPB, D])
            with nc.Fori(0, B) as b:
                attn = ExitStack()
                def sba(name, shape, dt=F32):
                    return attn.enter_context(nc.sbuf_tensor(name, shape, dt))
                q_rows = sba("q_rows", [P, TPB, QH, SLOT], F16)
                k_rows = sba("k_rows", [P, TPB, KVH, 2, SLOT], F16)
                qT = sba("qT", [P, PAIR, S], F16)
                kT = sba("kT", [P, KVH, S], F16)
                maxes = sba("maxes", [P, TPB, QH])
                negmax = sba("negmax", [P, TPB, QH], F16)
                negmaxT = sba("negmaxT", [QH, S], F16)

                with ExitStack() as inner, nc.Block() as block:
                    gate = inner.enter_context(nc.sbuf_tensor("gate", [P, TPB, D], F32))
                    n5T_hi = inner.enter_context(nc.sbuf_tensor("n5T_hi", [P, KC, S], F16))
                    n5T_lo = inner.enter_context(nc.sbuf_tensor("n5T_lo", [P, KC, S], F16))
                    pT = psum_banks(inner, "gateT", 4)
                    pG = psum_banks(inner, "gateG", 4)

                    @block.gpsimd
                    def _(pool):
                        l2_ffn.on_gpsimd(pool, minus_half, b)
                        pool.memset(q_rows[:, :, :, ROWS:SLOT], 0.0).then_inc(q_pad_done, 1)
                        pool.memset(k_rows[:, :, :, :, ROWS:SLOT], 0.0).then_inc(q_pad_done, 1)
                        for t in range(TPB):
                            src = ctxs[:, bass.ds(b * TPB + t, 1), :].rearrange("p a (g d) -> p (a g) d", d=DH)
                            for dup in range(2):
                                for i in range(2):
                                    pool.tensor_copy(k_rows[:, t, :, dup, i * DH:(i + 1) * DH], src).then_inc(k_hi_done, 1)
                        hold(pool, q_pad_done, 2 * b + 2)
                        pool.memset(k_rows[:, :, :, :, ROWS:ROWS + 1], 1.0).then_inc(k_ones_done, 1)
                        hold(pool, k_hi_done, 16 * b + 16)
                        for t in range(TPB):
                            src = ctxs[:, bass.ds(b * TPB + t, 1), :].rearrange("p a (g d) -> p (a g) d", d=DH)
                            for dup in range(2):
                                pool.tensor_tensor(k_rows[:, t, :, dup, 2 * DH:ROWS], src, k_rows[:, t, :, dup, 0:DH],
                                                   ALU.subtract).then_inc(k_lo_done, 1)
                        hold(pool, x5_copied, TPB * b + TPB)
                        for t in range(TPB):
                            pool.tensor_tensor(xw[:, t, :], xw[:, t, :], out_beta[:], ALU.add).then_inc(beta_added, 1)
                        l2_out.on_gpsimd(pool, minus_half, b)
                        l3_in.on_gpsimd(pool, minus_half, b)

                    @block.tensor
                    def _(pe):
                        pe.wait_ge(n5_done, TPB * b + TPB)
                        transposed_split(pe, nrm, pT, n5T_ready)
                        pe.wait_ge(n5T_lo_done, KC * b + KC)
                        for t in range(TPB):
                            dense(pe, pG[t][:], t, n5T_hi, n5T_lo, gate2_hi, gate2_lo, gate2_bias)\
                                .then_inc(gate_ready, 1)
                        pe.wait_ge(k_lo_done, 8 * b + 8)
                        pe.wait_ge(k_ones_done, b + 1)
                        for g in range(KVH):
                            bank = pT[g // 2][:].bitcast(F16)
                            for t in range(TPB):
                                at = (g % 2) * S + t * P
                                m = pe.transpose(bank[:, at:at + P], k_rows[:, t, g, :, :].rearrange("p e r -> p (e r)"),
                                                 ident_h[:])
                            if g % 2:
                                m.then_inc(kT_ready, 1)

                    @block.scalar
                    def _(act):
                        for t in range(TPB):
                            act.activation(xw[:, t, :], tile_of(xres, b * TPB + t), ACT.Copy).then_inc(x5_copied, 1)
                        for c in range(KC):
                            act.wait_ge(n5T_ready, KC * b + c + 1)
                            act.activation(n5T_hi[:, c, :], pT[c][:], ACT.Copy).then_inc(n5T_hi_done, 1)
                        for t in range(TPB):
                            act.wait_ge(gate_ready, TPB * b + t + 1)
                            act.activation(gate[:, t, :], pG[t][:], ACT.Sigmoid, scale=1.0 / G_SCALE).then_inc(gate_done, 1)
                        for i in range(KVH // 2):
                            act.wait_ge(kT_ready, KVH // 2 * b + i + 1)
                            act.activation(kT[:, 2 * i:2 * i + 2, :].rearrange("p g s -> p (g s)"),
                                           pT[i][:].bitcast(F16), ACT.Copy).then_inc(kT_done, 1)
                        for t in range(TPB):
                            act.wait_ge(n6_done, TPB * b + t + 1)
                            src = nrm[:, t, :].rearrange("p (h d) -> p h d", d=DH)
                            act.activation(q_rows[:, t, :, 0:DH], src, ACT.Copy).then_inc(q_hi_done, 1)
                            act.activation(q_rows[:, t, :, 2 * DH:ROWS], src, ACT.Copy).then_inc(q_hi_done, 1)

                    @block.vector
                    def _(dve):
                        l2_ffn.on_vector(dve, lambda t: tile_of(xres, b * TPB + t), b, None)
                        for t in range(TPB):
                            dve.tensor_scalar(nrm[:, t, :], tile_of(xres, b * TPB + t), l2_ffn.rstd[:, t:t + 1],
                                              l2_ffn.shift[:, t:t + 1], ALU.mult, ALU.add).then_inc(n5_done, 1)
                        for c in range(KC):
                            dve.wait_ge(n5T_hi_done, KC * b + c + 1)
                            dve.tensor_tensor(n5T_lo[:, c, :], pT[c][:], n5T_hi[:, c, :], ALU.subtract)\
                                .then_inc(n5T_lo_done, 1)
                        for t in range(TPB):
                            dve.wait_ge(gate_done, TPB * b + t + 1)
                            dve.tensor_tensor(gate[:, t, :], gate[:, t, :], tile_of(bc_rows, b), ALU.mult).then_inc(gated, 1)
                        dve.wait_ge(gated, 2 * TPB * b + TPB)
                        dve.tensor_tensor(gate[:], gate[:], nrm[:], ALU.add).then_inc(x6_step, 1)
                        l2_out.on_vector(dve, lambda t: gate[:, t, :], b, (x6_step, 3 * b + 1))
                        for t in range(TPB):
                            dve.tensor_scalar(gate[:, t, :], gate[:, t, :], l2_out.rstd[:, t:t + 1],
                                              l2_out.shift[:, t:t + 1], ALU.mult, ALU.add).then_inc(gated, 1)
                        hold(dve, gated, 2 * TPB * b + 2 * TPB)
                        gamma = out_gamma[:].unsqueeze(1).to_broadcast([P, TPB, D])
                        dve.tensor_tensor(gate[:], gate[:], gamma, ALU.mult).then_inc(x6_step, 1)
                        dve.wait_ge(beta_added, TPB * b + TPB)
                        dve.wait_ge(x6_step, 3 * b + 2)
                        dve.tensor_tensor(xw[:], xw[:], gate[:], ALU.add).then_inc(x6_step, 1)
                        l3_in.on_vector(dve, lambda t: xw[:, t, :], b, (x6_step, 3 * b + 3))
                        for t in range(TPB):
                            dve.tensor_scalar(nrm[:, t, :], xw[:, t, :], l3_in.rstd[:, t:t + 1],
                                              l3_in.shift[:, t:t + 1], ALU.mult, ALU.add).then_inc(n6_done, 1)
                        for t in range(TPB):
                            dve.wait_ge(q_hi_done, 2 * TPB * b + 2 * t + 1)
                            dve.tensor_tensor(q_rows[:, t, :, DH:2 * DH], nrm[:, t, :].rearrange("p (h d) -> p h d", d=DH),
                                              q_rows[:, t, :, 0:DH], ALU.subtract).then_inc(q_lo_done, 1)

                with ExitStack() as inner:
                    with nc.Block() as block:
                        pQ = psum_banks(inner, "qT", 8, F16)

                        @block.tensor
                        def _(pe):
                            for j in range(PAIR):
                                for t in range(TPB):
                                    at = (j % 2) * S + t * P
                                    m = pe.transpose(pQ[j // 2][:, at:at + P],
                                                     q_rows[:, t, 2 * j:2 * j + 2, :].rearrange("p e r -> p (e r)"),
                                                     ident_h[:])
                                if j % 2:
                                    m.then_inc(qT_ready, 1)

                        def copy_out(eng, i):
                            return (qT[:, 2 * i:2 * i + 2, :].rearrange("p j s -> p (j s)"), pQ[i][:])

                        @block.scalar
                        def _(act):
                            for i in range(0, 8, 2):
                                act.wait_ge(qT_ready, 8 * b + i + 1)
                                act.activation(*copy_out(act, i), ACT.Copy).then_inc(qT_done, 1)

                        @block.vector
                        def _(dve):
                            for i in range(1, 8, 2):
                                dve.wait_ge(qT_ready, 8 * b + i + 1)
                                dve.tensor_copy(*copy_out(dve, i)).then_inc(qT_odd_done, 1)

                def rows_of(head, n):
                    return slice(SLOT * (head % 2), SLOT * (head % 2) + n)

                direct = [h for h in range(QH) if h % 8 == 7]
                by_act = [h for h in range(QH) if h % 8 != 7]
                with ExitStack() as inner, nc.Block() as block:
                    s16 = [inner.enter_context(nc.sbuf_tensor(f"s16_{i}", [P, TPB, S], F16)) for i in range(2)]
                    half16 = inner.enter_context(nc.sbuf_tensor("half16", [P, TPB, S // 2], F16))
                    quarter16 = inner.enter_context(nc.sbuf_tensor("quarter16", [P, TPB, S // 4], F16))
                    pS = [inner.enter_context(nc.psum_tensor(f"pS{i}", [P, 2, S], F32)) for i in range(4)]

                    @block.tensor
                    def _(pe):
                        for h in range(QH):
                            r = rows_of(h, ROWS)
                            for half in range(2):
                                n = 2 * h + half
                                if h - 2 in by_act:
                                    pe.wait_ge(s16_done, 2 * (len(by_act) * b + by_act.index(h - 2)) + half + 1)
                                elif h >= 2:
                                    pe.wait_ge(max_done, QH * b + h - 1)
                                for i in range(2):
                                    t = 2 * half + i
                                    m = pe.matmul(pS[n % 4][:, i, :], qT[r, h // 2, t * P:(t + 1) * P],
                                                  kT[r, h // 4, :], start=True, stop=True)
                                m.then_inc(s_ready, 1)
                        pe.wait_ge(negmax_done, b + 1)
                        for t in range(TPB):
                            m = pe.transpose(pS[0][:, 0, :].bitcast(F16)[0:QH, t * P:(t + 1) * P], negmax[:, t, :],
                                             ident_h[:])
                        m.then_inc(negmaxT_ready, 1)

                    @block.scalar
                    def _(act):
                        for n, h in enumerate(by_act):
                            if n >= 2:
                                act.wait_ge(halved, len(by_act) * b + n - 1)
                            for half in range(2):
                                act.wait_ge(s_ready, 2 * QH * b + 2 * h + half + 1)
                                act.activation(s16[n % 2][:, 2 * half:2 * half + 2, :], pS[(2 * h + half) % 4][:],
                                               ACT.Copy).then_inc(s16_done, 1)

                    @block.vector
                    def _(dve):
                        for h in range(QH):
                            at = (h % 2) * PAIR + h // 2
                            if h in direct:
                                for half in range(2):
                                    dve.wait_ge(s_ready, 2 * QH * b + 2 * h + half + 1)
                                    m = dve.tensor_reduce(maxes[:, 2 * half:2 * half + 2, at:at + 1],
                                                          pS[(2 * h + half) % 4][:], AX.X, ALU.max)
                                m.then_inc(max_done, 1)
                                continue
                            n = by_act.index(h)
                            dve.wait_ge(s16_done, 2 * (len(by_act) * b + n) + 2)
                            s = s16[n % 2]
                            dve.tensor_tensor(half16[:], s[:, :, 0:S // 2], s[:, :, S // 2:S], ALU.max).then_inc(halved, 1)
                            dve.wait_ge(halved, len(by_act) * b + n + 1)
                            dve.tensor_tensor(quarter16[:], half16[:, :, 0:S // 4], half16[:, :, S // 4:S // 2], ALU.max)\
                                .then_inc(quartered, 1)
                            dve.wait_ge(quartered, len(by_act) * b + n + 1)
                            dve.tensor_reduce(maxes[:, :, at:at + 1], quarter16[:], AX.X, ALU.max).then_inc(max_done, 1)
                        dve.wait_ge(max_done, QH * b + QH)
                        dve.tensor_scalar(negmax[:], maxes[:], -1.0, None, ALU.mult).then_inc(negmax_done, 1)
                        dve.wait_ge(negmaxT_ready, b + 1)
                        dve.tensor_copy(negmaxT[:], pS[0][:, 0, :].bitcast(F16)[0:QH, 0:S]).then_inc(negmaxT_done, 1)

                    @block.sync
                    def _(sp):
                        for parity in range(2):
                            sp.wait_ge(negmaxT_done, b + 1)
                            row = SLOT * parity + ROWS
                            sp.dma_start(qT[row:row + 1, :, :], negmaxT[parity * PAIR:(parity + 1) * PAIR, :])\
                                .then_inc(negmax_moved, 16)

                with ExitStack() as inner, nc.Block() as block:
                    probs, probs_hi, probs_lo = [
                        [inner.enter_context(nc.sbuf_tensor(f"{name}{i}", [P, TPB, S], dt)) for i in range(2)]
                        for name, dt in (("probs", F32), ("probs_hi", F16), ("probs_lo", F16))]
                    recip = inner.enter_context(nc.sbuf_tensor("recip", [P, 16], F32))
                    weighed = inner.enter_context(nc.sbuf_tensor("weighed", [P, 16, DH], F32))
                    pX = [inner.enter_context(nc.psum_tensor(f"pX{i}", [P, 2, S], F32)) for i in range(3)]
                    pO = psum_banks(inner, "pO", 2)
                    W = DH + 1

                    @block.tensor
                    def _(pe):
                        pe.wait_ge(negmax_moved, 32 * b + 32)

                        def scores(h):
                            for half in range(2):
                                n = 2 * h + half
                                if n >= 3:
                                    pe.wait_ge(exp_done, 2 * QH * b + n - 2)
                                r = rows_of(h, ROWS + 1)
                                for i in range(2):
                                    kt = 2 * half + i
                                    m = pe.matmul(pX[n % 3][:, i, :], kT[r, h // 4, kt * P:(kt + 1) * P],
                                                  qT[r, h // 2, :], start=True, stop=True)
                                m.then_inc(sT_ready, 1)

                        def weigh(h):
                            pe.wait_ge(probs_lo_done, 2 * QH * b + 2 * h + 2)
                            pe.wait_ge(probs_lo3_done, QH * b + h + 1)
                            if h % 4 == 0 and h >= 8:
                                pe.wait_ge(weighed_done, KVH * b + h // 4 - 1)
                            for qt in range(TPB):
                                at = ((h % 4) * TPB + qt) * W
                                for kt in range(TPB):
                                    v_hi, v_lo = [v[:, bass.ds(b * TPB + kt, 1), h // 4, :].rearrange("p a w -> p (a w)")
                                                  for v in (values_hi, values_lo)]
                                    q = slice(qt * P, (qt + 1) * P)
                                    m = split_matmul(pe, pO[h // 4 % 2][:, at:at + W], probs_hi[h % 2][:, kt, q],
                                                     probs_lo[h % 2][:, kt, q], v_hi, v_lo, kt == 0, kt == TPB - 1)
                            m.then_inc(pv_ready, 1)

                        scores(0)
                        scores(1)
                        for h in range(QH):
                            if h + 2 < QH:
                                scores(h + 2)
                            weigh(h)

                    @block.scalar
                    def _(act):
                        def high(h):
                            if h >= 2:
                                act.wait_ge(pv_ready, QH * b + h - 1)
                            act.wait_ge(exp_done, 2 * QH * b + 2 * h + 1)
                            act.activation(probs_hi[h % 2][:, 0:2, :], probs[h % 2][:, 0:2, :], ACT.Copy)\
                                .then_inc(probs_hi0_done, 1)

                        for h in range(QH):
                            for half in range(2):
                                n = 2 * h + half
                                if h >= 2:
                                    act.wait_ge(probs_lo_done, 2 * QH * b + n - 3)
                                    if half:
                                        act.wait_ge(probs_lo3_done, QH * b + h - 1)
                                act.wait_ge(sT_ready, 2 * QH * b + n + 1)
                                act.activation(probs[h % 2][:, 2 * half:2 * half + 2, :], pX[n % 3][:], ACT.Exp,
                                               scale=DH ** -0.5).then_inc(exp_done, 1)
                            high(h)

                    @block.gpsimd
                    def _(pool):
                        for h in range(QH):
                            hold(pool, probs_hi1_done, QH * b + h + 1)
                            pool.tensor_tensor(probs_lo[h % 2][:, 3, :], probs[h % 2][:, 3, :], probs_hi[h % 2][:, 3, :],
                                               ALU.subtract).then_inc(probs_lo3_done, 1)

                    @block.vector
                    def _(dve):
                        def normalise(g):
                            dve.wait_ge(pv_ready, QH * b + 4 * g + 4)
                            o = pO[g % 2][:, 0:16 * W].rearrange("p (q w) -> p q w", w=W)
                            dve.reciprocal(recip[:].unsqueeze(2), o[:, :, DH:W]).then_inc(recip_done, 1)
                            if g >= 1:
                                dve.wait_ge(x7_done, KVH * b + g)
                            dve.wait_ge(recip_done, KVH * b + g + 1)
                            dve.tensor_tensor(weighed[:], o[:, :, 0:DH], recip[:].unsqueeze(2).to_broadcast([P, 16, DH]),
                                              ALU.mult).then_inc(weighed_done, 1)
                            dve.wait_ge(weighed_done, KVH * b + g + 1)
                            x = xw[:, :, g * 4 * DH:(g + 1) * 4 * DH].rearrange("p t (h d) -> p t h d", d=DH)
                            dve.tensor_tensor(x, x, weighed[:].rearrange("p (h t) d -> p t h d", t=TPB), ALU.add)\
                                .then_inc(x7_done, 1)

                        for h in range(QH):
                            if h >= 2:
                                dve.wait_ge(pv_ready, QH * b + h - 1)
                            dve.wait_ge(exp_done, 2 * QH * b + 2 * h + 2)
                            full, hi, lo = probs[h % 2], probs_hi[h % 2], probs_lo[h % 2]
                            dve.tensor_copy(hi[:, 2:4, :], full[:, 2:4, :]).then_inc(probs_hi1_done, 1)
                            dve.wait_ge(probs_hi0_done, QH * b + h + 1)
                            dve.tensor_tensor(lo[:, 0:2, :], full[:, 0:2, :], hi[:, 0:2, :], ALU.subtract)\
                                .then_inc(probs_lo_done, 1)
                            dve.wait_ge(probs_hi1_done, QH * b + h + 1)
                            dve.tensor_tensor(lo[:, 2, :], full[:, 2, :], hi[:, 2, :], ALU.subtract)\
                                .then_inc(probs_lo_done, 1)
                            if h % 4 == 1 and h >= 5:
                                normalise(h // 4 - 1)
                        normalise(KVH - 1)
                attn.close()

                with ExitStack() as inner, nc.Block() as block:
                    def sbf(name, shape, dt=F32):
                        return inner.enter_context(nc.sbuf_tensor(name, shape, dt))
                    q7 = sbf("q7", [P, TPB, D], BF16)
                    q7T = sbf("q7T", [P, KC, S], BF16)
                    hid = sbf("hidden", [P, TPB, IUP])
                    hq = sbf("hq", [P, TPB, IUP], BF16)
                    hqT = sbf("hqT", [P, IUP // P, S], BF16)
                    amax, scale7, deq7, hmax, hscale, hdeq = [sbf(n, [P, TPB]) for n in
                                                              ("amax", "scale7", "deq7", "hmax", "hscale", "hdeq")]
                    pT = psum_banks(inner, "ffnT", 4)
                    pU = psum_banks(inner, "ffnU", 4)

                    @block.gpsimd
                    def _(pool):
                        l3_mid.on_gpsimd(pool, minus_half, b)

                    @block.tensor
                    def _(pe):
                        pe.wait_ge(q7_done, b + 1)
                        for c in range(KC):
                            for t in range(TPB):
                                m = pe.transpose(pT[c][:].bitcast(BF16)[:, t * P:(t + 1) * P], q7[:, t, c::KC], ident_b[:])
                            m.then_inc(q7T_ready, 1)
                        pe.wait_ge(q7T_done, KC * b + KC)
                        for t in range(TPB):
                            for half in range(2):
                                n = 2 * t + half
                                if n >= 4:
                                    pe.wait_ge(relu_done, 8 * b + n - 3)
                                for c in range(KC):
                                    m = pe.matmul(pU[n % 4][:], q7T[:, c, t * P:(t + 1) * P],
                                                  up_t[:, c, half * D:(half + 1) * D], start=c == 0, stop=c == KC - 1)
                                m.then_inc(hid_ready, 1)
                        for t in range(TPB):
                            pe.wait_ge(hq_done, TPB * b + t + 1)
                            for k in range(8):
                                m = pe.transpose(pT[t][:].bitcast(BF16)[:, k * P:(k + 1) * P], hq[:, t, k::8], ident_b[:])
                            m.then_inc(hqT_ready, 1)
                        for t in range(TPB):
                            pe.wait_ge(hqT_done, TPB * b + t + 1)
                            for k in range(8):
                                m = pe.matmul(pU[t][:], hqT[:, k, t * P:(t + 1) * P], dn_t[:, k, :], start=k == 0, stop=k == 7)
                            m.then_inc(y_ready, 1)

                    @block.scalar
                    def _(act):
                        for c in range(KC):
                            act.wait_ge(q7T_ready, KC * b + c + 1)
                            act.activation(q7T[:, c, :], pT[c][:].bitcast(BF16)[:, 0:S], ACT.Copy).then_inc(q7T_done, 1)
                        for t in range(TPB):
                            for half in range(2):
                                n = 2 * t + half
                                act.wait_ge(hid_ready, 8 * b + n + 1)
                                act.activation(hid[:, t, half * D:(half + 1) * D], pU[n % 4][:], ACT.Relu,
                                               scale=deq7[:, t:t + 1]).then_inc(relu_done, 1)
                        for t in range(TPB):
                            act.wait_ge(hmax_done, TPB * b + t + 1)
                            act.activation(hid[:, t, :], hid[:, t, :], ACT.Square).then_inc(hsq_done, 1)
                        for t in range(TPB):
                            act.wait_ge(hqT_ready, TPB * b + t + 1)
                            act.activation(hqT[:, :, t * P:(t + 1) * P],
                                           pT[t][:].bitcast(BF16).rearrange("p (k s) -> p k s", k=8), ACT.Copy)\
                                .then_inc(hqT_done, 1)

                    @block.vector
                    def _(dve):
                        l3_mid.on_vector(dve, lambda t: xw[:, t, :], b, None)
                        for t in range(TPB):
                            dve.tensor_scalar(nrm[:, t, :], xw[:, t, :], l3_mid.rstd[:, t:t + 1],
                                              l3_mid.shift[:, t:t + 1], ALU.mult, ALU.add).then_inc(n7_done, 1)
                        dve.wait_ge(n7_done, TPB * b + TPB)
                        dve.tensor_reduce(amax[:], nrm[:], AX.X, ALU.max, apply_absolute_value=True).then_inc(amax_done, 1)
                        dve.wait_ge(amax_done, b + 1)

                        def scales(top, scale, deq, mean, counter):
                            dve.tensor_scalar(top[:], top[:], 1e-5, None, ALU.max).then_inc(counter, 1)
                            dve.wait_ge(counter, 4 * b + 1)
                            dve.reciprocal(scale[:], top[:]).then_inc(counter, 1)
                            dve.wait_ge(counter, 4 * b + 2)
                            dve.tensor_scalar(scale[:], scale[:], 127.0, None, ALU.mult).then_inc(counter, 1)
                            dve.tensor_scalar(deq[:], top[:], 1.0 / 127.0, mean, ALU.mult, ALU.mult).then_inc(counter, 1)
                            dve.wait_ge(counter, 4 * b + 4)

                        scales(amax, scale7, deq7, tern[:, 1:2], scale_step)
                        for t in range(TPB):
                            dve.tensor_scalar(nrm[:, t, :], nrm[:, t, :], scale7[:, t:t + 1], 127.0, ALU.mult, ALU.min)\
                                .then_inc(quant_step, 1)
                        dve.wait_ge(quant_step, 5 * b + 4)
                        dve.tensor_scalar(nrm[:], nrm[:], -127.0, MAGIC, ALU.max, ALU.add).then_inc(quant_step, 1)
                        dve.wait_ge(quant_step, 5 * b + 5)
                        dve.tensor_scalar(q7[:], nrm[:], MAGIC, None, ALU.subtract).then_inc(q7_done, 1)
                        for t in range(TPB):
                            dve.wait_ge(relu_done, 8 * b + 2 * t + 2)
                            dve.tensor_reduce(hmax[:, t:t + 1], hid[:, t, :], AX.X, ALU.max).then_inc(hmax_done, 1)
                        dve.wait_ge(hmax_done, TPB * b + TPB)
                        dve.tensor_tensor(hmax[:], hmax[:], hmax[:], ALU.mult).then_inc(hquant_step, 1)
                        dve.wait_ge(hquant_step, 9 * b + 1)
                        scales(hmax, hscale, hdeq, tern[:, 3:4], hscale_step)
                        for t in range(TPB):
                            dve.wait_ge(hsq_done, TPB * b + t + 1)
                            dve.tensor_scalar(hid[:, t, :], hid[:, t, :], hscale[:, t:t + 1], 127.0, ALU.mult, ALU.min)\
                                .then_inc(hquant_step, 1)
                            dve.wait_ge(hquant_step, 9 * b + 2 * t + 2)
                            dve.tensor_scalar(hid[:, t, :], hid[:, t, :], -127.0, MAGIC, ALU.max, ALU.add)\
                                .then_inc(hquant_step, 1)
                            dve.wait_ge(hquant_step, 9 * b + 2 * t + 3)
                            dve.tensor_scalar(hq[:, t, :], hid[:, t, :], MAGIC, None, ALU.subtract).then_inc(hq_done, 1)
                        for t in range(TPB):
                            dve.wait_ge(y_ready, TPB * b + t + 1)
                            dve.scalar_tensor_tensor(out=nrm[:, t, :], in0=pU[t][:], scalar=hdeq[:, t:t + 1],
                                                     in1=xw[:, t, :], op0=ALU.mult, op1=ALU.add).then_inc(x8_done, 1)

                    @block.sync
                    def _(sp):
                        for t in range(TPB):
                            sp.wait_ge(x8_done, TPB * b + t + 1)
                            sp.dma_start(out_d[:, bass.ds(b * TPB + t, 1), :], nrm[:, t:t + 1, :]).then_inc(stored, 16)
                        sp.wait_ge(stored, 16 * TPB * b + 16 * TPB)
                        sp.sem_inc(Norm.held, 1)




_INS = ['x', 'ctx_512', 'mask_SxS2_bk1', 'mask_BxS2_bf0', 'L0_xattn_W', 'L0_xattn_b', 'L0_ffn_gate_w', 'L0_ffn_wg',
        'L0_ffn_wu', 'L0_ffn_wd', 'L0_ffn_sg', 'L0_ffn_su', 'L0_ffn_sd', 'L1_xattn_Wq', 'L1_xattn_Wk',
        'L1_xattn_gamma_raw', 'L1_ffn_factors', 'L1_ffn_bias', 'L2_xattn_Wq', 'L2_xattn_bq', 'L2_xattn_Wk',
        'L2_xattn_bk', 'L2_ffn_in_gamma', 'L2_ffn_in_beta', 'L2_ffn_agg_w', 'L2_ffn_agg_b', 'L2_ffn_pn_gamma',
        'L2_ffn_pn_beta', 'L2_ffn_d1_w', 'L2_ffn_d1_b', 'L2_ffn_d2_w', 'L2_ffn_d2_b', 'L2_ffn_bc_w', 'L2_ffn_bc_b',
        'L2_ffn_gate_w', 'L2_ffn_gate_b', 'L2_ffn_out_gamma', 'L2_ffn_out_beta', 'L3_ffn_w_up', 'L3_ffn_w_down']


def kernel(**inputs):
    import numpy as _np
    import concourse.bacc as _bacc
    from concourse import mybir as _mybir
    from concourse.bass_utils import run_bass_kernel_spmd as _run

    nc = _bacc.Bacc("TRN2", target_bir_lowering=False, num_devices=1)
    arrays, args = {}, []
    for name in _INS:
        a = _np.ascontiguousarray(inputs[name]).reshape(_np.shape(inputs[name]) or (1,))
        if a.dtype == _np.bool_:
            a = a.view(_np.int32)
        arrays[f"in_{name}_dram"] = a
        args.append(nc.dram_tensor(f"in_{name}_dram", a.shape, _mybir.dt.from_np(a.dtype), kind="ExternalInput").ap())
    args.append(nc.dram_tensor("out_0_dram", (B, S, D), F32, kind="ExternalOutput").ap())
    program(nc, *args)
    r = _run(nc, [arrays], core_ids=[0])
    return r.results[0]["out_0_dram"]
```
